# Optimizing a Trainium2 kernel written in Bass

```python
import numpy as np
import jax
import jax.numpy as jnp

def _softmax(x, axis=-1):
    return jax.nn.softmax(x, axis=axis)

def _gelu(x):
    return jax.nn.gelu(x, approximate=True)

def _silu(x):
    return jax.nn.silu(x)

def _sigmoid(x):
    return jax.nn.sigmoid(x)

def _layernorm(x, axis=-1, eps=1e-05):
    m = jnp.mean(x, axis=axis, keepdims=True)
    v = jnp.var(x, axis=axis, keepdims=True)
    return (x - m) / jnp.sqrt(v + eps)

def _scatter_add(tgt, idx, src, axis=0):
    return tgt.at[idx].add(src)

def _segment_sum(src, seg, n):
    return jax.ops.segment_sum(src, seg, n)
kernel_name = 'mk_macaron_d2_jaxref_r8_dedac5'

def setup_inputs(seed: int=0):
    np.random.seed(seed)
    _w = jnp.asarray

    def _L0_attn_setup():
        import jax, jax.numpy as jnp
        import numpy as np
        B, S, D = (2, 256, 128)
        NH, KVH = (16, 4)
        HD = D // NH
        ROPE_BASE = 10000.0

        def rotate_half(x):
            half = x.shape[-1] // 2
            x1, x2 = (x[..., :half], x[..., half:])
            return jnp.concatenate((-x2, x1), axis=-1)

        def rope_cache(seq_len, head_dim, base, dtype):
            half = head_dim // 2
            inv_freq = 1.0 / base ** (jnp.arange(half, dtype=jnp.float32) / max(1, half))
            t = jnp.arange(seq_len, dtype=jnp.float32)
            freqs = jnp.einsum('i,j->ij', t, inv_freq)
            emb = jnp.concatenate((freqs, freqs), axis=-1)
            cos = jnp.cos(emb)[None, None].astype(dtype)
            sin = jnp.sin(emb)[None, None].astype(dtype)
            return (sin, cos)
        key = jax.random.key(seed)
        ks = jax.random.split(key, 5)
        s = 0.02
        return {'x': jax.random.normal(ks[0], (B, S, D), dtype=jnp.float32), 'Wq': jax.random.normal(ks[1], (D, D), dtype=jnp.float32) * s, 'Wk': jax.random.normal(ks[2], (D, KVH * HD), dtype=jnp.float32) * s, 'Wv': jax.random.normal(ks[3], (D, KVH * HD), dtype=jnp.float32) * s, 'Wo': jax.random.normal(ks[4], (D, D), dtype=jnp.float32) * s}
    _L0_attn_in = _L0_attn_setup()

    def _L0_ffn_setup():
        import jax, jax.numpy as jnp
        import numpy as np
        D_MODEL = 128
        M = 64
        INNER = 16
        key = jax.random.key(seed)
        ks = jax.random.split(key, 9)

        def init(k, shape, fan_in):
            bound = 1.0 / np.sqrt(fan_in)
            return jax.random.uniform(k, shape, jnp.float32, -bound, bound)
        x = jax.random.normal(ks[0], (16, 512, D_MODEL), dtype=jnp.float32)
        Win = init(ks[1], (D_MODEL, M), D_MODEL)
        bin_ = init(ks[2], (M,), D_MODEL)
        W1 = init(ks[3], (M, INNER), 1)
        b1 = init(ks[4], (M, INNER), 1)
        W2 = init(ks[5], (M, INNER), INNER)
        b2 = init(ks[6], (M,), INNER)
        Wout = init(ks[7], (M, D_MODEL), M)
        bout = init(ks[8], (D_MODEL,), M)
        return {'x': x, 'Win': Win, 'bin_': bin_, 'W1': W1, 'b1': b1, 'W2': W2, 'b2': b2, 'Wout': Wout, 'bout': bout}
    _L0_ffn_in = _L0_ffn_setup()

    def _L1_attn_setup():
        import jax, jax.numpy as jnp
        import numpy as np
        B, T, D, P, ALPHA, PR = (4, 512, 128, 64, 4, 64)
        key = jax.random.key(seed)
        ks = jax.random.split(key, 9)
        g = lambda k, shape, scale: jax.random.normal(k, shape, jnp.float32) * scale
        return {'x': jax.random.normal(ks[0], (B, T, D), jnp.float32), 'W_toP': g(ks[1], (D, P), D ** (-0.5)), 'W_U': g(ks[2], (D, P, ALPHA), D ** (-0.5)), 'W_F': g(ks[3], (D, P), D ** (-0.5)), 'W_V': g(ks[4], (P, ALPHA), 1.0), 'W_lam': g(ks[5], (P, PR), P ** (-0.5)), 'B_mat': g(ks[6], (P, PR), P ** (-0.5)), 'C_mat': g(ks[7], (PR, P), PR ** (-0.5)), 'W_fromP': g(ks[8], (P, D), P ** (-0.5))}
    _L1_attn_in = _L1_attn_setup()

    def _L1_ffn_setup():
        import jax, jax.numpy as jnp
        import numpy as np
        NUM_EXPERTS = 8
        EXPERT_CAPACITY = 2.0
        DIM = 128
        HIDDEN_DIM = 512
        key = jax.random.key(seed)
        k_x, k_g, k_w1, k_w2 = jax.random.split(key, 4)
        n, t, d, f, e = (8, 128, DIM, HIDDEN_DIM, NUM_EXPERTS)
        x = jax.random.normal(k_x, (n, t, d), dtype=jnp.float32)
        gate_w = jax.random.normal(k_g, (e, d), dtype=jnp.float32) * 0.02
        w1 = jax.random.normal(k_w1, (e, d, f), dtype=jnp.float32) * 0.02
        w2 = jax.random.normal(k_w2, (e, f, d), dtype=jnp.float32) * 0.02
        return {'x': x, 'gate_w': gate_w, 'w1': w1, 'w2': w2}
    _L1_ffn_in = _L1_ffn_setup()
    _d = {'L0_attn_x': _L0_attn_in['x'], 'L0_attn_Wq': _L0_attn_in['Wq'], 'L0_attn_Wk': _L0_attn_in['Wk'], 'L0_attn_Wv': _L0_attn_in['Wv'], 'L0_attn_Wo': _L0_attn_in['Wo'], 'L0_ffn_Win': _L0_ffn_in['Win'], 'L0_ffn_bin_': _L0_ffn_in['bin_'], 'L0_ffn_W1': _L0_ffn_in['W1'], 'L0_ffn_b1': _L0_ffn_in['b1'], 'L0_ffn_W2': _L0_ffn_in['W2'], 'L0_ffn_b2': _L0_ffn_in['b2'], 'L0_ffn_Wout': _L0_ffn_in['Wout'], 'L0_ffn_bout': _L0_ffn_in['bout'], 'L1_attn_W_toP': _L1_attn_in['W_toP'], 'L1_attn_W_U': _L1_attn_in['W_U'], 'L1_attn_W_F': _L1_attn_in['W_F'], 'L1_attn_W_V': _L1_attn_in['W_V'], 'L1_attn_W_lam': _L1_attn_in['W_lam'], 'L1_attn_B_mat': _L1_attn_in['B_mat'], 'L1_attn_C_mat': _L1_attn_in['C_mat'], 'L1_attn_W_fromP': _L1_attn_in['W_fromP'], 'L1_ffn_gate_w': _L1_ffn_in['gate_w'], 'L1_ffn_w1': _L1_ffn_in['w1'], 'L1_ffn_w2': _L1_ffn_in['w2']}
    _x0 = _d['L0_attn_x']
    _d['L0_attn_x'] = jax.random.normal(jax.random.fold_in(jax.random.key(seed), 1), (16, 512, 128), dtype=_x0.dtype)
    del _x0
    return _d

def reference(L0_attn_x, L0_attn_Wq, L0_attn_Wk, L0_attn_Wv, L0_attn_Wo, L0_ffn_Win, L0_ffn_bin_, L0_ffn_W1, L0_ffn_b1, L0_ffn_W2, L0_ffn_b2, L0_ffn_Wout, L0_ffn_bout, L1_attn_W_toP, L1_attn_W_U, L1_attn_W_F, L1_attn_W_V, L1_attn_W_lam, L1_attn_B_mat, L1_attn_C_mat, L1_attn_W_fromP, L1_ffn_gate_w, L1_ffn_w1, L1_ffn_w2):

    def _L0_attn_ref(x, Wq, Wk, Wv, Wo):
        import jax, jax.numpy as jnp
        import numpy as np
        B, S, D = (2, 256, 128)
        NH, KVH = (16, 4)
        HD = D // NH
        ROPE_BASE = 10000.0

        def rotate_half(x):
            half = x.shape[-1] // 2
            x1, x2 = (x[..., :half], x[..., half:])
            return jnp.concatenate((-x2, x1), axis=-1)

        def rope_cache(seq_len, head_dim, base, dtype):
            half = head_dim // 2
            inv_freq = 1.0 / base ** (jnp.arange(half, dtype=jnp.float32) / max(1, half))
            t = jnp.arange(seq_len, dtype=jnp.float32)
            freqs = jnp.einsum('i,j->ij', t, inv_freq)
            emb = jnp.concatenate((freqs, freqs), axis=-1)
            cos = jnp.cos(emb)[None, None].astype(dtype)
            sin = jnp.sin(emb)[None, None].astype(dtype)
            return (sin, cos)
        bsz, seq_len, _ = x.shape
        scale = HD ** (-0.5)
        q = (x @ Wq).reshape(bsz, seq_len, NH, HD).transpose(0, 2, 1, 3)
        k = (x @ Wk).reshape(bsz, seq_len, KVH, HD).transpose(0, 2, 1, 3)
        v = (x @ Wv).reshape(bsz, seq_len, KVH, HD).transpose(0, 2, 1, 3)
        sin, cos = rope_cache(seq_len, HD, ROPE_BASE, q.dtype)
        q = q * cos + rotate_half(q) * sin
        k = k * cos + rotate_half(k) * sin
        rep = NH // KVH
        k = jnp.repeat(k, rep, axis=1)
        v = jnp.repeat(v, rep, axis=1)
        att = jnp.einsum('bhqd,bhkd->bhqk', q, k) * scale
        causal = jnp.tril(jnp.ones((seq_len, seq_len), dtype=bool))
        att = jnp.where(causal, att, jnp.finfo(att.dtype).min)
        att = jax.nn.softmax(att, axis=-1)
        y = jnp.einsum('bhqk,bhkd->bhqd', att, v)
        y = y.transpose(0, 2, 1, 3).reshape(bsz, seq_len, NH * HD)
        return y @ Wo

    def _L0_ffn_ref(x, Win, bin_, W1, b1, W2, b2, Wout, bout):
        import jax, jax.numpy as jnp
        import numpy as np
        D_MODEL = 128
        M = 64
        INNER = 16
        s = jnp.einsum('btd,dm->btm', x, Win) + bin_
        h = jax.nn.relu(s[..., None] * W1 + b1)
        g = jnp.einsum('btmh,mh->btm', h, W2) + b2
        out = jnp.einsum('btm,md->btd', g, Wout) + bout
        return out

    def _L1_attn_ref(x, W_toP, W_U, W_F, W_V, W_lam, B_mat, C_mat, W_fromP):
        import jax, jax.numpy as jnp
        import numpy as np
        B, T, D, P, ALPHA, PR = (4, 512, 128, 64, 4, 64)
        pre = jnp.einsum('btd,dp->btp', x, W_toP)
        U = jnp.einsum('btd,dpa->btpa', x, W_U)
        Fg = jax.nn.sigmoid(jnp.einsum('btd,dp->btp', x, W_F))
        Y = U * W_V
        t = Y.sum(-1) + pre
        lam = jax.nn.sigmoid(jnp.einsum('btp,pr->btr', Fg, W_lam))
        u_in = jnp.einsum('btp,pr->btr', t, B_mat)

        def step(s, inp):
            l, u = inp
            s = l * s + u
            return (s, s)
        s0 = jnp.zeros((x.shape[0], PR), x.dtype)
        _, s_seq = jax.lax.scan(step, s0, (lam.transpose(1, 0, 2), u_in.transpose(1, 0, 2)))
        s_seq = s_seq.transpose(1, 0, 2)
        t_tilde = t + jnp.einsum('btr,rp->btp', s_seq, C_mat)
        h = jnp.einsum('btp,pd->btd', t_tilde, W_fromP)
        return h

    def _L1_ffn_ref(x, gate_w, w1, w2):
        import jax, jax.numpy as jnp
        import numpy as np
        NUM_EXPERTS = 8
        EXPERT_CAPACITY = 2.0
        DIM = 128
        HIDDEN_DIM = 512
        n, t, d = x.shape
        e = gate_w.shape[0]
        k = int(EXPERT_CAPACITY * t / e)
        scores = jnp.einsum('ntd,ed->nte', x, gate_w)
        probs = jax.nn.softmax(scores, axis=-1)
        g, m = jax.lax.top_k(probs.transpose(0, 2, 1), k)
        batch_idx = jnp.arange(n)[:, None, None]
        xin = x[batch_idx, m]
        h = jnp.einsum('nekd,edf->nekf', xin, w1)
        h = jax.nn.gelu(h, approximate=False)
        h = jnp.einsum('nekf,efd->nekd', h, w2)
        out_tok = g[..., None] * h
        out = jnp.zeros((n, t, d), dtype=x.dtype).at[batch_idx, m].add(out_tok)
        return out
    x = L0_attn_x
    x = x + 0.5 * _L0_ffn_ref(_layernorm(x, axis=-1), L0_ffn_Win, L0_ffn_bin_, L0_ffn_W1, L0_ffn_b1, L0_ffn_W2, L0_ffn_b2, L0_ffn_Wout, L0_ffn_bout)
    x = x + _L0_attn_ref(_layernorm(x, axis=-1), L0_attn_Wq, L0_attn_Wk, L0_attn_Wv, L0_attn_Wo)
    x = x + 0.5 * _L0_ffn_ref(_layernorm(x, axis=-1), L0_ffn_Win, L0_ffn_bin_, L0_ffn_W1, L0_ffn_b1, L0_ffn_W2, L0_ffn_b2, L0_ffn_Wout, L0_ffn_bout)
    x = x + 0.5 * _L1_ffn_ref(_layernorm(x, axis=-1), L1_ffn_gate_w, L1_ffn_w1, L1_ffn_w2)
    x = x + _L1_attn_ref(_layernorm(x, axis=-1), L1_attn_W_toP, L1_attn_W_U, L1_attn_W_F, L1_attn_W_V, L1_attn_W_lam, L1_attn_B_mat, L1_attn_C_mat, L1_attn_W_fromP)
    x = x + 0.5 * _L1_ffn_ref(_layernorm(x, axis=-1), L1_ffn_gate_w, L1_ffn_w1, L1_ffn_w2)
    return x

_drawn_inputs = setup_inputs


def setup_inputs(seed=0):
    import zlib

    import numpy as np

    out = dict(_drawn_inputs(seed))
    spreads = {}
    factors = {'L0_attn_Wq': 8.0,
     'L0_attn_Wk': 8.0,
     'L0_attn_Wv': 5.475,
     'L0_attn_Wo': 5.554,
     'L0_ffn_bin_': 6.747,
     'L1_ffn_gate_w': 8.0,
     'L1_ffn_w1': 8.0,
     'L1_ffn_w2': 8.0}
    for name, (base, spread) in spreads.items():
        noise = np.random.default_rng([zlib.crc32(name.encode()), seed]).standard_normal(out[name].shape)
        drawn = base * np.exp(spread * noise) if base else spread * noise
        out[name] = jnp.asarray(drawn.astype(out[name].dtype))
    for name, factor in factors.items():
        out[name] = (out[name] * factor).astype(out[name].dtype)
    return out
```

```python
from contextlib import ExitStack

import concourse.bass as bass
from concourse import mybir

F32 = mybir.dt.float32
BF16 = mybir.dt.bfloat16
U32 = mybir.dt.uint32
ALU = mybir.AluOpType
ACT = mybir.ActivationFunctionType
AX = mybir.AxisListType

P = 128
NB = 16
T = 512
D = 128
C = T // P
EPS = 1e-5
NH, NKV = 16, 4
HD = D // NH
GH = NH // NKV
SCALE = HD ** -0.5
PARTS = 3
KQ = PARTS * PARTS * HD
KM = KQ + 2
MASKED = -1.0e38
M = 64
INNER = 16
HT = M * INNER // P
E = 8
F = 512
FC = F // P
K = 2 * T // E
PR = 64
RING = 4
W4 = 4


def load_constants(nc, w, sb, sem):
    h = {}
    for n, s, d in [
        ("win2", [P, P], F32), ("bin2", [P, 1], F32), ("w1p", [P, HT], F32), ("nb1p", [P, HT], F32),
        ("w2out", [P, HT, D], F32), ("cvec", [P, 1], F32),
        ("wq", [P, D], F32), ("wqs", [P, D], F32), ("wk", [P, PARTS * NKV * HD], F32),
        ("wks", [P, PARTS * NKV * HD], F32), ("wv", [P, NKV * HD], F32), ("wo", [P, D], F32),
        ("cosq", [P, T], F32), ("sinq", [P, T], F32), ("cosk", [96, T], F32), ("sink", [96, T], F32),
        ("ident", [P, P], F32), ("identb", [P, P], BF16), ("maskb", [P, P], BF16), ("iota", [P, T], F32),
        ("gw", [P, E], F32), ("wtf", [P, P], F32), ("wlam", [P, PR], F32), ("bmat", [PR, PR], F32),
        ("wcw", [P, D], F32), ("w1e", [P, E, F], F32), ("w2e", [P, E, FC, D], F32),
        ("rowbase", [P, 1], F32), ("mhalf", [P, 16], F32),
    ]:
        h[n] = sb(n, s, d)
    with ExitStack() as tmp:
        t = lambda n, s, d: tmp.enter_context(nc.sbuf_tensor(n, s, d))
        wout2 = t("wout2", [P, D], F32)
        w2p = t("w2p", [P, HT], F32)
        b1p = t("b1p", [P, HT], F32)
        b2p = t("b2p", [P, 1], F32)
        boutc = t("boutc", [P, 1], F32)
        b1w2 = t("b1w2", [P, HT], F32)
        csum = t("csum", [P, 1], F32)
        wu = t("wu", [P, M * 4], F32)
        wv4 = t("wv4", [P, M * 4], F32)
        wtop = t("wtop", [P, M], F32)
        ct = t("ct", [PR, PR], F32)
        maskf = t("maskf", [P, P], F32)
        cps = tmp.enter_context(nc.psum_tensor("cps", [P, 512], F32))
        small_in, experts_in = sem("small_in"), sem("experts_in")
        fold, fold_mm, cast = sem("fold"), sem("fold_mm"), sem("cast")
        h["experts_in"] = experts_in
        loads = [
            (h["win2"][:], w["win2"]), (h["bin2"][:], w["bin2"]), (h["w1p"][:], w["w1p"]),
            (wout2[:], w["wout2"]), (w2p[:], w["w2p"]), (b1p[:], w["b1p"]), (b2p[:], w["b2p"]),
            (boutc[:], w["bout"]), (h["wq"][:], w["wq"]), (h["wqs"][:], w["wqs"]), (h["wk"][:], w["wk"]),
            (h["wks"][:], w["wks"]), (h["wv"][:], w["wv"]), (h["wo"][:], w["wo"]), (h["cosq"][:], w["cosq"]),
            (h["sinq"][:], w["sinq"]), (h["cosk"][:], w["cosk"]), (h["sink"][:], w["sink"]),
            (h["ident"][:], w["ident"]), (maskf[:], w["mask"]), (h["iota"][:], w["iota"]), (h["gw"][:], w["gw"]),
            (wu[:], w["wu"]), (wv4[:], w["wv4"].to_broadcast([P, M * 4])), (wtop[:], w["wtop"]),
            (h["wtf"][:, M:P], w["wf"]), (h["wlam"][PR:P, :], w["wlam"]), (h["bmat"][:], w["bmat"]),
            (ct[:], w["ct"]), (h["wcw"][0:PR, :], w["wfromp"]), (h["rowbase"][:], w["rowbase"]),
            (h["mhalf"][:], w["mhalf"]),
        ]
        with nc.Block() as block:

            @block.sync
            def _(sp):
                for dst, src in loads:
                    sp.dma_start(dst, src).then_inc(small_in, 16)
                sp.wait_ge(small_in, 16 * len(loads))
                sp.dma_start(h["w1e"][:], w["w1e"]).then_inc(experts_in, 16)
                sp.dma_start(h["w2e"][:], w["w2e"]).then_inc(experts_in, 16)

            @block.vector
            def _(dve):
                v = nc.vector
                dve.wait_ge(small_in, 16 * len(loads))
                v.tensor_copy(h["identb"][:], h["ident"][:])
                v.tensor_copy(h["maskb"][:], maskf[:])
                v.tensor_scalar(h["nb1p"][:], b1p[:], -1.0, None, ALU.mult)
                for j in range(HT):
                    v.tensor_scalar(h["w2out"][:, j, :], wout2[:], w2p[:, j:j + 1], 0.5, ALU.mult, ALU.mult)
                v.tensor_tensor(b1w2[:], w2p[:], b1p[:], ALU.mult).then_inc(fold, 1)
                dve.wait_ge(fold, 1)
                v.tensor_reduce(csum[:], b1w2[:], AX.X, ALU.add).then_inc(fold, 1)
                dve.wait_ge(fold, 2)
                v.tensor_tensor(csum[:], csum[:], b2p[:], ALU.add).then_inc(fold, 1)
                v.tensor_tensor(wu[:], wu[:], wv4[:], ALU.mult).then_inc(fold, 1)
                dve.wait_ge(fold, 4)
                v.tensor_reduce(h["wtf"][:, 0:M], wu[:].rearrange("p (m a) -> p m a", a=4), AX.X, ALU.add).then_inc(fold, 1)
                dve.wait_ge(fold, 5)
                v.tensor_tensor(h["wtf"][:, 0:M], h["wtf"][:, 0:M], wtop[:], ALU.add)
                dve.wait_ge(fold_mm, 2)
                v.tensor_scalar(h["cvec"][:], cps[:, 0:1], boutc[:], 0.5, ALU.add, ALU.mult)
                v.tensor_copy(h["wcw"][PR:P, :], cps[PR:P, 128:256]).then_inc(cast, 1)
                dve.wait_ge(cast, 1)

            @block.tensor
            def _(pe):
                pe.wait_ge(small_in, 16 * len(loads))
                pe.wait_ge(fold, 3)
                pe.matmul(cps[:, 0:1], wout2[:], csum[:], start=True, stop=True).then_inc(fold_mm, 1)
                pe.matmul(cps[PR:P, 128:256], ct[:], h["wcw"][0:PR, :], start=True, stop=True).then_inc(fold_mm, 1)
    return h


class Norm:

    def __init__(self, nc, name, sb, sem, h, xres, per_turn):
        self.nc, self.h, self.xres, self.per = nc, h, xres, per_turn
        self.stats = sb(name + "_stats", [P, W4 * C, 6], F32)
        self.mv = sb(name + "_mv", [P, W4 * C, 2], F32)
        self.vare = sb(name + "_vare", [P, W4 * C], F32)
        self.rstd = sb(name + "_rstd", [P, W4 * C], F32)
        self.stats_done, self.mv_done = sem(name + "_stats_done"), sem(name + "_mv_done")
        self.var_done, self.rstd_done = sem(name + "_var_done"), sem(name + "_rstd_done")
        self.pool_turn, self.dve_turn = sem(name + "_pool_turn"), sem(name + "_dve_turn")

    def vector(self, dve, i, k, xhat, xhat_done):
        v, nth = self.nc.vector, i * self.per + k + 1
        dve.sem_inc(self.dve_turn, 1)
        for b in range(W4):
            for c in range(C):
                s = v.bn_stats(self.stats[:, b * C + c, :], self.xres[:, i * W4 + b, c * D:(c + 1) * D])
        s.then_inc(self.stats_done, 1)
        dve.wait_ge(self.stats_done, nth)
        dve.sem_inc(self.dve_turn, 1)
        for j in range(W4 * C):
            s = v.bn_aggr(self.mv[:, j, :], self.stats[:, j, :])
        s.then_inc(self.mv_done, 1)
        dve.wait_ge(self.mv_done, nth)
        v.tensor_scalar(self.vare[:], self.mv[:, :, 1], EPS, None, ALU.add).then_inc(self.var_done, 1)
        dve.wait_ge(self.rstd_done, nth)
        for b in range(W4):
            for c in range(C):
                j = b * C + c
                s = v.tensor_scalar(xhat[b][:, c * D:(c + 1) * D], self.xres[:, i * W4 + b, c * D:(c + 1) * D],
                                    self.mv[:, j, 0:1], self.rstd[:, j:j + 1], ALU.subtract, ALU.mult)
            s.then_inc(xhat_done, 1)

    def gpsimd(self, pool, i, k):
        nth = i * self.per + k + 1
        pool.wait_ge(self.var_done, nth)
        pool.sem_inc(self.pool_turn, 1)
        self.nc.gpsimd.tensor_tensor(self.rstd[:], self.vare[:], self.h["mhalf"][:], ALU.pow).then_inc(self.rstd_done, 1)


class Gate:

    def __init__(self, nc, name, sb, sem, h, probs):
        self.nc, self.h, self.probs = nc, h, probs
        self.mx = sb("mx", [P, W4 * C], F32)
        self.ex = sb("ex", [P, W4, C, E], F32)
        self.den = sb("den", [P, W4 * C], F32)
        self.rden = sb("rden", [P, W4 * C], F32)
        self.soft, self.exp_done = sem("soft"), sem("exp_done")

    def tensor(self, pe, b, bank, xhat_t, full):
        for c in range(C):
            at = (b * C + c) * E
            mm = pe.matmul(bank[:, at:at + E], xhat_t[:, c * P:(c + 1) * P], self.h["gw"][:], start=True, stop=True)
        mm.then_inc(full, 1)

    def scalar(self, act):
        self.nc.scalar.activation(self.ex[:], self.ex[:], ACT.Exp).then_inc(self.exp_done, 1)

    def vector(self, dve, i, bank, read):
        v = self.nc.vector
        sc = bank[:, 0:W4 * C * E].rearrange("p (j e) -> p j e", e=E)
        exj = self.ex[:].rearrange("p b c e -> p (b c) e")
        v.tensor_reduce(self.mx[:], sc, AX.X, ALU.max).then_inc(self.soft, 1)
        dve.wait_ge(self.soft, i * 4 + 1)
        v.tensor_tensor(exj, sc, self.mx[:].unsqueeze(2).to_broadcast([P, W4 * C, E]), ALU.subtract).then_inc(read, W4)
        dve.wait_ge(self.exp_done, i + 1)
        v.tensor_reduce(self.den[:], exj, AX.X, ALU.add).then_inc(self.soft, 1)
        dve.wait_ge(self.soft, i * 4 + 2)
        v.reciprocal(self.rden[:], self.den[:]).then_inc(self.soft, 1)
        dve.wait_ge(self.soft, i * 4 + 3)
        for b in range(W4):
            pr = v.tensor_tensor(self.probs[:, :, bass.ds((i * W4 + b) * E, E)], self.ex[:, b],
                                 self.rden[:, b * C:(b + 1) * C].unsqueeze(2).to_broadcast([P, C, E]), ALU.mult)
        pr.then_inc(self.soft, 1)
        dve.wait_ge(self.soft, i * 4 + 4)


def transpose_chunks(pe, out, src, ident):
    for c in range(C):
        last = pe.transpose(out[:, c * P:(c + 1) * P], src[:, c * P:(c + 1) * P], ident[:])
    return last


def mlp_layer(nc, sem, h, xres, tail, name, x_src=None, q_dram=None, k_dram=None, v_all=None,
              xn_dram=None, probs=None):
    qkv = tail == "qkv"
    turns = NB // W4
    with ExitStack() as tmp:
        t = lambda n, s, d: tmp.enter_context(nc.sbuf_tensor(f"{name}_{n}", s, d))
        norm = Norm(nc, name, t, sem, h, xres, 2)
        xhat = [t(f"xhat{b}", [P, T], F32) for b in range(W4)]
        xhat_t = [t(f"xhat_t{b}", [P, T], F32) for b in range(W4)]
        s_in = [t(f"s{b}", [P, T], F32) for b in range(W4)]
        hid = [t(f"hid{j}", [P, T], F32) for j in range(HT)]
        y_t = [t(f"y_t{b}", [P, T], F32) for b in range(W4)]
        s = lambda n: sem(f"{name}_{n}")
        a_ring = [tmp.enter_context(nc.psum_tensor(f"{name}_a{j}", [P, T], F32)) for j in range(4)]
        v_ring = [tmp.enter_context(nc.psum_tensor(f"{name}_v{j}", [P, T], F32)) for j in range(4)]
        a_full, a_read, v_full, v_read = s("a_full"), s("a_read"), s("v_full"), s("v_read")
        AT = 5 * W4 if qkv else 4 * W4
        VT = 5 * W4 if qkv else 2 * W4
        x_in, xhat_done, hid_done, hid_used = s("x_in"), s("xhat_done"), s("hid_done"), s("hid_used")
        act_turn = s("act_turn")
        if qkv:
            rq, rk = PARTS * P, 96
            rot = {}
            for b in range(W4):
                for n, rows in (("q", P), ("k", 96)):
                    rot[n, b] = dict(a=t(f"{n}a{b}", [rows, T], F32), b=t(f"{n}b{b}", [rows, T], F32),
                                     parts=t(f"{n}parts{b}", [rows, PARTS, T], BF16))
            full_done, p1_done, r1_done, p2_done, p3_done = (
                s("full_done"), s("p1_done"), s("r1_done"), s("p2_done"), s("p3_done"))
            parts_out = [s(f"parts_out{b}") for b in range(W4)]
            pool_turn = s("rope_pool_turn")
        else:
            gate = Gate(nc, name, t, s, h, probs)
            xn_out = [s(f"xn_out{b}") for b in range(W4)]
        XT, S, Y, XT2, V = range(5)
        a_tile = lambda i, stage, b: i * AT + stage * W4 + b
        v_rope = lambda i, b, j: i * VT + W4 + b * 4 + j
        with nc.Block() as block:

            @block.sync
            def _(sp):
                if x_src is not None:
                    for i in range(turns):
                        sp.dma_start(xres[:, i * W4:(i + 1) * W4, :].rearrange("p n (c d) -> p n c d", c=C),
                                     x_src[i * W4:(i + 1) * W4].rearrange("n (c p) d -> p n c d", p=P)).then_inc(x_in, 16)
                        sp.wait_ge(x_in, 16 * (i + 1))
                with sp.Fori(0, turns) as i:
                    if qkv:
                        for b in range(W4):
                            sp.wait_ge(p3_done, i * 2 * W4 + 2 * b + 2)
                            sp.dma_start(q_dram[i * W4 + b].rearrange("(j p) t -> p j t", p=P),
                                         rot["q", b]["parts"][:]).then_inc(parts_out[b], 16)
                            sp.dma_start(k_dram[i * W4 + b].rearrange("(j p) t -> p j t", p=96),
                                         rot["k", b]["parts"][:]).then_inc(parts_out[b], 16)
                    else:
                        for b in range(W4):
                            sp.wait_ge(xhat_done, i * 2 * W4 + W4 + b + 1)
                            sp.dma_start(xn_dram[bass.ds((i * W4 + b) * T, T), :].rearrange("(c p) d -> p c d", p=P),
                                         xhat[b][:].rearrange("p (c d) -> p c d", c=C)).then_inc(xn_out[b], 16)
                for b in range(W4):
                    sp.wait_ge(parts_out[b] if qkv else xn_out[b], (32 if qkv else 16) * turns)

            @block.tensor
            def _(pe):
                with pe.Fori(0, turns) as i:
                    for b in range(W4):
                        pe.wait_ge(xhat_done, i * 2 * W4 + b + 1)
                        pe.wait_ge(a_read, a_tile(i, XT, b) + 1)
                        transpose_chunks(pe, a_ring[b % 4], xhat[b], h["ident"]).then_inc(a_full, 1)
                    for b in range(W4):
                        pe.wait_ge(a_read, RING + a_tile(i, XT, b) + 1)
                        pe.matmul(a_ring[b % 4][:], h["win2"][:], xhat_t[b][:], start=True, stop=True).then_inc(a_full, 1)
                    for b in range(W4):
                        pe.wait_ge(a_read, a_tile(i, Y, b) + 1)
                        for j in range(HT):
                            pe.wait_ge(hid_done, (i * W4 + b) * HT + j + 1)
                            mm = pe.matmul(a_ring[b % 4][:], h["w2out"][:, j, :], hid[j][:], start=(j == 0), stop=(j == HT - 1))
                            mm.then_inc(hid_used, 1)
                    for b in range(W4):
                        pe.wait_ge(a_read, RING + a_tile(i, Y, b) + 1)
                        pe.wait_ge(v_read, i * VT + b + 1)
                        transpose_chunks(pe, v_ring[b % 4], y_t[b], h["ident"]).then_inc(v_full, 1)
                    for b in range(W4):
                        pe.wait_ge(xhat_done, i * 2 * W4 + W4 + b + 1)
                        pe.wait_ge(a_read, a_tile(i, XT2, b) + 1)
                        transpose_chunks(pe, a_ring[b % 4], xhat[b], h["ident"]).then_inc(a_full, 1)
                    for b in range(W4):
                        pe.wait_ge(a_read, RING + a_tile(i, XT2, b) + 1)
                        if qkv:
                            for j, wt in enumerate(("wq", "wqs", "wk", "wks")):
                                rows = P if j < 2 else 96
                                pe.wait_ge(v_read, v_rope(i, b, j) + 1)
                                pe.matmul(v_ring[j][0:rows, :], h[wt][:], xhat_t[b][:], start=True, stop=True).then_inc(v_full, 1)
                            pe.wait_ge(a_read, a_tile(i, V, b) + 1)
                            for c in range(C):
                                mm = pe.matmul(a_ring[b % 4][:, c * 32:(c + 1) * 32], xhat_t[b][:, c * P:(c + 1) * P], h["wv"][:],
                                               start=True, stop=True)
                            mm.then_inc(a_full, 1)
                        else:
                            if b == 0:
                                pe.wait_ge(v_read, i * VT + W4 + 1)
                            gate.tensor(pe, b, v_ring[0], xhat_t[b], v_full)

            @block.scalar
            def _(act):
                a = nc.scalar
                act.sem_inc(a_read, RING)
                with act.Fori(0, turns) as i:
                    for b in range(W4):
                        act.wait_ge(a_full, i * (AT - W4) + b + 1)
                        a.activation(xhat_t[b][:], a_ring[b % 4][:], ACT.Copy).then_inc(a_read, 1)
                    for b in range(W4):
                        act.wait_ge(a_full, i * (AT - W4) + W4 + b + 1)
                        a.activation(s_in[b][:], a_ring[b % 4][:], ACT.Identity, bias=h["bin2"][:]).then_inc(a_read, 1)
                    for b in range(W4):
                        act.wait_ge(hid_used, (i * W4 + b + 1) * HT)
                        a.activation(y_t[b][:], a_ring[b % 4][:], ACT.Identity, bias=h["cvec"][:]).then_inc(a_read, 1)
                    for b in range(W4):
                        act.wait_ge(a_full, i * (AT - W4) + 2 * W4 + b + 1)
                        a.activation(xhat_t[b][:], a_ring[b % 4][:], ACT.Copy).then_inc(a_read, 1)
                    if qkv:
                        for b in range(W4):
                            for k, n in enumerate("qk"):
                                r = rot[n, b]
                                act.wait_ge(full_done, i * 2 * W4 + 2 * b + k + 1)
                                a.activation(r["parts"][:, 0, :], r["a"][:], ACT.Copy).then_inc(p1_done, 1)
                                act.wait_ge(r1_done, i * 2 * W4 + 2 * b + k + 1)
                                a.activation(r["parts"][:, 1, :], r["b"][:], ACT.Copy).then_inc(p2_done, 1)
                            act.wait_ge(a_full, i * (AT - W4) + 3 * W4 + b + 1)
                            act.sem_inc(act_turn, 1)
                            a.activation(v_all[:, i * W4 + b, :], a_ring[b % 4][:, 0:C * 32], ACT.Copy).then_inc(a_read, 1)
                    else:
                        act.wait_ge(v_read, RING + (i + 1) * VT)
                        gate.scalar(act)

            @block.gpsimd
            def _(pool):
                g = nc.gpsimd
                with pool.Fori(0, turns) as i:
                    norm.gpsimd(pool, i, 0)
                    norm.gpsimd(pool, i, 1)
                    if qkv:
                        for b in range(W4):
                            for k, n in enumerate("qk"):
                                r, nth = rot[n, b], i * 2 * W4 + 2 * b + k + 1
                                pool.wait_ge(v_read, RING + v_rope(i, b, 2 * k + 1) + 1)
                                pool.sem_inc(pool_turn, 1)
                                g.tensor_tensor(r["a"][:], r["a"][:], r["b"][:], ALU.add).then_inc(full_done, 1)
                                pool.wait_ge(full_done, nth)
                                pool.wait_ge(p1_done, nth)
                                pool.sem_inc(pool_turn, 1)
                                g.tensor_tensor(r["b"][:], r["a"][:], r["parts"][:, 0, :], ALU.subtract).then_inc(r1_done, 1)
                                pool.wait_ge(r1_done, nth)
                                pool.wait_ge(p2_done, nth)
                                pool.sem_inc(pool_turn, 1)
                                g.tensor_tensor(r["parts"][:, 2, :], r["b"][:], r["parts"][:, 1, :], ALU.subtract).then_inc(p3_done, 1)

            @block.vector
            def _(dve):
                v = nc.vector
                dve.sem_inc(v_read, RING)
                if x_src is not None:
                    dve.wait_ge(x_in, 16 * turns)
                with dve.Fori(0, turns) as i:
                    norm.vector(dve, i, 0, xhat, xhat_done)
                    for b in range(W4):
                        dve.wait_ge(a_read, RING + a_tile(i, S, b) + 1)
                        for j in range(HT):
                            if b > 0:
                                dve.wait_ge(hid_used, (i * W4 + b - 1) * HT + j + 1)
                            v.tensor_scalar(hid[j][:], s_in[b][:], h["w1p"][:, j:j + 1], h["nb1p"][:, j:j + 1],
                                            ALU.mult, ALU.max).then_inc(hid_done, 1)
                    for b in range(W4):
                        dve.wait_ge(v_full, i * VT + b + 1)
                        v.tensor_tensor(xres[:, i * W4 + b, :], v_ring[b % 4][:], xres[:, i * W4 + b, :], ALU.add).then_inc(v_read, 1)
                    dve.wait_ge(v_read, RING + i * VT + W4)
                    norm.vector(dve, i, 1, xhat, xhat_done)
                    if qkv:
                        for b in range(W4):
                            for k, n in enumerate("qk"):
                                r, rows = rot[n, b], P if n == "q" else 96
                                for j, (dst, tab) in enumerate((("a", "cos"), ("b", "sin"))):
                                    dve.wait_ge(v_full, v_rope(i, b, 2 * k + j) + 1)
                                    v.tensor_tensor(r[dst][:], v_ring[2 * k + j][0:rows, :], h[tab + n][:], ALU.mult).then_inc(v_read, 1)
                        for b in range(W4):
                            dve.wait_ge(parts_out[b], i * 32 + 32)
                    else:
                        dve.wait_ge(v_full, i * VT + 2 * W4)
                        gate.vector(dve, i, v_ring[0], v_read)
                        for b in range(W4):
                            dve.wait_ge(xn_out[b], i * 16 + 16)


SW = 512
XW = 1024
S_TILES = [(0, range(0, 4)), (1, range(0, 2)), (1, range(2, 4))] + [(c, [j]) for c in (2, 3) for j in range(GH)]
S_SLOTS = [range(0, 2), range(2, 4), range(4, 6), range(6, 8), range(8, 11)]
NS = len(S_TILES)
NX = GH + 1
X_HEAD = [(0, 0), (1, 512), (3, 896)]
NP = 4
LAG = 2


def attention(nc, sem, h, xres, q_dram, k_dram, v_all):
    m_dram = nc.dram_tensor("row_max", [2, 2, NH * C, P], BF16, kind="Internal").ap()
    with ExitStack() as tmp:
        t = lambda n, s, d: tmp.enter_context(nc.sbuf_tensor(f"at_{n}", s, d))
        ps = lambda n, s, d: tmp.enter_context(nc.psum_tensor(f"at_{n}_ps", s, d))
        s = lambda n: sem(f"at_{n}")
        qr = [t(f"qr{u}", [P, NH * T], BF16) for u in range(2)]
        kr = [t(f"kr{u}", [P, NKV * T], BF16) for u in range(2)]
        va = [t(f"va{u}", [P, C, NKV, 32], F32) for u in range(2)]
        p_sb = [t(f"p{j}", [P, XW], F32) for j in range(NP)]
        rowmax = [t(f"rowmax{u}", [P, NH, C], F32) for u in range(2)]
        m_parts = [t(f"m_parts{j}", [GH * C, 2, P], BF16) for j in range(2)]
        o_t = [t(f"o_t{j}", [P, T], F32) for j in range(2)]
        rden = t("rden", [P, C, GH], F32)
        o_n = t("o_n", [P, C, D], F32)
        o_nt = t("o_nt", [P, T], F32)
        s_ps = [ps(f"s{j}", [P, SW], F32) for j in range(2)]
        x_ps = [ps(f"x{j}", [P, XW], F32) for j in range(2)]
        o_ps = ps("o", [P, T], F32)
        misc = ps("misc", [P, T], F32)
        qk_in = [[s(f"qk_in{u}{g}") for g in range(NKV)] for u in range(2)]
        m_in = [[s(f"m_in{u}{g}") for g in range(NKV)] for u in range(2)]
        ones_done, va_done = s("ones_done"), s("va_done")
        s_read, x_read, p_used, x_added = s("s_read"), s("x_read"), s("p_used"), s("x_added")
        s_full, x_full, p_masked = s("s_full"), s("x_full"), s("p_masked")
        max_t, m1_done, m2_done, m_stored = s("max_t"), s("m1_done"), s("m2_done"), s("m_stored")
        o_copied, o_trans, o_rden, o_norm = s("o_copied"), s("o_trans"), s("o_rden"), s("o_norm")
        on_trans, on_copied, proj = s("on_trans"), s("on_copied"), s("proj")
        pool_turn, dve_turn = s("pool_turn"), s("dve_turn")

        def schedule(eng, pair, first, last):
            first()
            with eng.Fori(0, NB // 2 - 1) as i:
                pair((i * 2 + 1, 1, i), (i * 2, 0, i))
                pair((i * 2 + 2, 0, i + 1), (i * 2 + 1, 1, i))
            pair((NB - 1, 1, NB // 2 - 1), (NB - 2, 0, NB // 2 - 1))
            last()

        FIRST, LAST = (0, 0, 0), (NB - 1, 1, NB // 2 - 1)

        with nc.Block() as block:

            @block.sync
            def _(sp):
                def load(n, u, r, g):
                    q = q_dram[n].rearrange("(r h) t -> r h t", h=NH)
                    k = k_dram[n].rearrange("(r h) t -> r h t", h=NKV)
                    rows = PARTS * HD
                    for j in range(PARTS):
                        sp.dma_start(qr[u][j * rows:(j + 1) * rows, g * GH * T:(g + 1) * GH * T].rearrange("r (h t) -> r h t", h=GH),
                                     q[:, g * GH:(g + 1) * GH, :]).then_inc(qk_in[u][g], 16)
                    sp.dma_start(kr[u][0:KQ, g * T:(g + 1) * T], k[:, g, :]).then_inc(qk_in[u][g], 16)

                def maxima(n, u, r, g):
                    sp.wait_ge(m2_done, n * NKV + g + 1)
                    sp.dma_start(m_dram[u].rearrange("a r q -> r a q")[g * GH * C:(g + 1) * GH * C], m_parts[g % 2][:]).then_inc(m_stored, 16)
                    sp.wait_ge(m_stored, (n * NKV + g + 1) * 16)
                    sp.dma_start(qr[u][KQ:KM, g * GH * T:(g + 1) * GH * T],
                                 m_dram[u].rearrange("a r q -> a (r q)")[:, g * GH * T:(g + 1) * GH * T]).then_inc(m_in[u][g], 16)

                def first():
                    sp.wait_ge(ones_done, 1)
                    for u in range(2):
                        for g in range(NKV):
                            load(u, u, 0, g)
                    for g in range(NKV):
                        maxima(*FIRST, g)

                def pair(front, back, more=True):
                    n, u, r = back
                    for g in range(NKV):
                        if more:
                            sp.wait_ge(x_full, (n * NKV + g + 1) * NX)
                            load(n + 2, u, r + 1, g)
                        maxima(*front, g)

                def tail(front, back):
                    pair(front, back, more=not isinstance(back[0], int))

                schedule(sp, tail, first, lambda: None)

            @block.tensor
            def _(pe):
                def scores(n, u, r, g, slot):
                    if slot == 0:
                        pe.wait_ge(qk_in[u][g], r * 64 + 64)
                    for k in S_SLOTS[slot]:
                        c, heads = S_TILES[k]
                        w = (c + 1) * P
                        tile = s_ps[(g * NS + k) % 2]
                        pe.wait_ge(s_read, (n * NKV + g) * NS + k + 1)
                        for x, j in enumerate(heads):
                            q0 = (g * GH + j) * T + c * P
                            pe.matmul(tile[:, x * w:(x + 1) * w], qr[u][0:KQ, q0:q0 + P], kr[u][0:KQ, g * T:g * T + w],
                                      start=True, stop=False)
                            mm = pe.matmul(tile[:, (x + 1) * w - P:(x + 1) * w], h["identb"][:], h["maskb"][:],
                                           start=False, stop=True)
                        mm.then_inc(s_full, 1)

                def less_max(n, u, r, g, k):
                    if k == 0:
                        pe.wait_ge(m_in[u][g], r * 16 + 16)
                    pe.wait_ge(x_read, (n * NKV + g) * NX + k + 1)
                    blocks = [(c, k, at) for c, at in X_HEAD] if k < GH else [(2, j, j * 2 * P) for j in range(GH)]
                    for c, j, at in blocks:
                        q0 = (g * GH + j) * T
                        mm = pe.matmul(x_ps[(g * NX + k) % 2][:, at:at + T - c * P], kr[u][0:KM, g * T + c * P:g * T + (c + 1) * P],
                                       qr[u][0:KM, q0 + c * P:q0 + T], start=True, stop=True)
                    mm.then_inc(x_full, 1)

                def weigh(n, u, r, g, k):
                    q = g * NX + k
                    if g == 0 and k == 0:
                        pe.wait_ge(va_done, n + 1)
                    if k == 0:
                        if not (isinstance(n, int) and n == 0 and g == 0):
                            pe.wait_ge(o_copied, n * NKV + g + 1)
                    pe.wait_ge(p_masked, n * NKV * NX + q + 1)
                    blocks = [(c, k, at) for c, at in X_HEAD] if k < GH else [(2, j, j * 2 * P) for j in range(GH)]
                    for c, j, at in blocks:
                        mm = pe.matmul(o_ps[32 * j:32 * j + 32, c * P:T], va[u][:, c, g, :], p_sb[q % NP][:, at:at + T - c * P],
                                       start=(c == 0), stop=(c == 2))
                    mm.then_inc(p_used, 1)

                def max_rows(front, back, g):
                    n, u, r = front
                    pe.wait_ge(s_read, 2 + (n * NKV + g + 1) * NS)
                    if back is not None:
                        pe.wait_ge(m2_done, n * NKV + g)
                        if g == 0:
                            pe.wait_ge(x_added, n)
                        else:
                            pe.wait_ge(o_norm, back[0] * NKV + g)
                    elif g > 0:
                        pe.wait_ge(m2_done, g)
                    pe.transpose(misc[0:GH * C, 0:P], rowmax[u][:, g * GH:(g + 1) * GH, :].rearrange("p j c -> p (j c)"),
                                 h["ident"][:]).then_inc(max_t, 1)

                def turn_output(front, back, g):
                    n, u, r = back
                    pe.wait_ge(o_copied, 1 + n * NKV + g + 1)
                    if front is not None:
                        pe.wait_ge(m2_done, front[0] * NKV + g + 1)
                    elif g == 0:
                        pe.wait_ge(x_added, n + 1)
                    else:
                        pe.wait_ge(o_norm, n * NKV + g)
                    transpose_chunks(pe, misc, o_t[g % 2], h["ident"]).then_inc(o_trans, 1)

                def project(n, u, r):
                    pe.wait_ge(o_norm, (n + 1) * NKV)
                    for c in range(C):
                        mm = pe.transpose(misc[:, c * P:(c + 1) * P], o_n[:, c, :], h["ident"][:])
                    mm.then_inc(on_trans, 1)
                    pe.wait_ge(on_copied, n + 1)
                    for c in range(C):
                        mm = pe.matmul(misc[:, c * P:(c + 1) * P], o_nt[:, c * P:(c + 1) * P], h["wo"][:], start=True, stop=True)
                    mm.then_inc(proj, 1)

                def pair(front, back):
                    for g in range(NKV):
                        for k in range(NX):
                            if front is not None:
                                scores(*front, g, k)
                            less_max(*back, g, k)
                            q = g * NX + k - LAG
                            if q >= 0:
                                weigh(*back, q // NX, q % NX)
                            if front is not None and k == 0 and g > 0:
                                max_rows(front, back, g - 1)
                            if k == 3 and g > 0:
                                turn_output(front, back, g - 1)
                    for q in range(NKV * NX - LAG, NKV * NX):
                        weigh(*back, q // NX, q % NX)
                    if front is not None:
                        max_rows(front, back, NKV - 1)
                    turn_output(front, back, NKV - 1)
                    project(*back)

                def first():
                    pe.sem_inc(p_used, NP)
                    for g in range(NKV):
                        for k in range(NX):
                            scores(*FIRST, g, k)
                        max_rows(FIRST, None, g)

                schedule(pe, pair, first, lambda: pair(None, LAST))

            @block.scalar
            def _(act):
                a = nc.scalar

                def copy_output(n, u, r, g):
                    act.wait_ge(p_used, NP + (n * NKV + g + 1) * NX)
                    a.activation(o_t[g % 2][:], o_ps[:], ACT.Copy).then_inc(o_copied, 1)

                def pair(front, back):
                    n, u, r = back
                    for g in range(NKV):
                        for k in range(NX):
                            q = g * NX + k
                            act.wait_ge(x_full, n * NKV * NX + q + 1)
                            act.wait_ge(p_used, n * NKV * NX + q + 1)
                            a.activation(p_sb[q % NP][:], x_ps[q % 2][:], ACT.Exp, scale=SCALE).then_inc(x_read, 1)
                            if k == 1 and g > 0:
                                copy_output(*back, g - 1)
                    copy_output(*back, NKV - 1)
                    act.wait_ge(on_trans, n + 1)
                    a.activation(o_nt[:], misc[:], ACT.Copy).then_inc(on_copied, 1)

                def first():
                    act.sem_inc(x_read, 2)
                    act.sem_inc(o_copied, 1)

                schedule(act, pair, first, lambda: pair(None, LAST))

            @block.gpsimd
            def _(pool):
                gp = nc.gpsimd

                def values(n, u, before):
                    if before is not None:
                        pool.wait_ge(p_used, NP + before * NKV * NX)
                    pool.sem_inc(pool_turn, 1)
                    gp.tensor_copy(va[u][:, :, :, 0:HD], v_all[:, n, :].rearrange("p (c g d) -> p c g d", c=C, g=NKV)).then_inc(va_done, 1)

                def pair(front, back):
                    n, u, r = back
                    if front is not None:
                        values(front[0], front[1], n)
                    for g in range(NKV):
                        for k in range(NX):
                            q = g * NX + k
                            pool.wait_ge(x_read, 2 + n * NKV * NX + q + 1)
                            pool.sem_inc(pool_turn, 1)
                            blocks = p_sb[q % NP][:].rearrange("p (b q) -> p b q", q=P)
                            for part in ([blocks[:, 0], blocks[:, 4:8:3]] if k < GH else [blocks[:, 0:8:2]]):
                                sel = gp.affine_select(out=part, in_=part, compare_op=ALU.is_ge, fill=0.0, base=0,
                                                       pattern=[[0, n] for n in part.shape[1:-1]] + [[1, P]], channel_multiplier=-1)
                            sel.then_inc(p_masked, 1)

                def first():
                    for u in range(2):
                        gp.memset(kr[u][:], 1.0)
                        last = gp.memset(va[u][:], 1.0)
                    last.then_inc(ones_done, 1)
                    pool.wait_ge(ones_done, 1)
                    values(0, 0, None)

                schedule(pool, pair, first, lambda: pair(None, LAST))

            @block.vector
            def _(dve):
                v = nc.vector

                def maxima(n, u, r, g, slot):
                    for k in S_SLOTS[slot]:
                        c, heads = S_TILES[k]
                        w, h0 = (c + 1) * P, g * GH + heads[0]
                        dve.wait_ge(s_full, (n * NKV + g) * NS + k + 1)
                        v.tensor_reduce(rowmax[u][:, h0:h0 + len(heads), c],
                                        s_ps[(g * NS + k) % 2][:, 0:len(heads) * w].rearrange("p (j w) -> p j w", w=w),
                                        AX.X, ALU.max).then_inc(s_read, 1)

                def max_parts(n, u, r, g):
                    dve.wait_ge(max_t, n * NKV + g + 1)
                    if not (isinstance(n, int) and n == 0 and g < 2):
                        dve.wait_ge(m_stored, (n * NKV + g - 1) * 16)
                    v.tensor_scalar(m_parts[g % 2][:, 0, :], misc[0:GH * C, 0:P], -1.0, None, ALU.mult).then_inc(m1_done, 1)
                    dve.wait_ge(m1_done, n * NKV + g + 1)
                    v.scalar_tensor_tensor(out=m_parts[g % 2][:, 1, :], in0=misc[0:GH * C, 0:P], scalar=-1.0,
                                           in1=m_parts[g % 2][:, 0, :], op0=ALU.mult, op1=ALU.subtract).then_inc(m2_done, 1)

                def normalise(n, u, r, g):
                    dve.wait_ge(o_trans, n * NKV + g + 1)
                    o = misc[:].rearrange("p (c j e) -> p c j e", c=C, e=32)
                    v.reciprocal(rden[:], o[:, :, :, HD]).then_inc(o_rden, 1)
                    dve.wait_ge(o_rden, n * NKV + g + 1)
                    v.tensor_tensor(o_n[:, :, g * 32:(g + 1) * 32].rearrange("p c (j d) -> p c j d", d=HD), o[:, :, :, 0:HD],
                                    rden[:].unsqueeze(3).to_broadcast([P, C, GH, HD]), ALU.mult).then_inc(o_norm, 1)

                def pair(front, back):
                    n, u, r = back
                    for g in range(NKV):
                        for k in range(NX):
                            if front is not None:
                                maxima(*front, g, k)
                                if k == 1 and g > 0:
                                    max_parts(*front, g - 1)
                            if k == 4 and g > 0:
                                normalise(*back, g - 1)
                    if front is not None:
                        max_parts(*front, NKV - 1)
                    normalise(*back, NKV - 1)
                    dve.wait_ge(proj, n + 1)
                    v.tensor_tensor(xres[:, n, :], misc[:], xres[:, n, :], ALU.add).then_inc(x_added, 1)

                def first():
                    dve.sem_inc(s_read, 2)
                    dve.sem_inc(x_added, 1)
                    for g in range(NKV):
                        for k in range(NX):
                            maxima(*FIRST, g, k)
                        max_parts(*FIRST, g)

                schedule(dve, pair, first, lambda: pair(None, LAST))


def choose_tokens(nc, sb, sem, h, probs, name):
    local = sb(f"{name}_local", [K, NB * E], F32)
    rows = sb(f"{name}_rows", [K, NB * E], U32)
    weight = sb(f"{name}_weight", [K, NB * E], F32)
    with ExitStack() as tmp:
        t = lambda n, s, d: tmp.enter_context(nc.sbuf_tensor(f"{name}_{n}", s, d))
        left = t("left", [P, T], F32)
        vals = t("vals", [P, K], F32)
        found = t("found", [P, K], U32)
        foundf = t("foundf", [P, K], F32)
        foundg = t("foundg", [P, K], F32)
        pps = tmp.enter_context(nc.psum_tensor(f"{name}_pps", [P, T], F32))
        tps = [tmp.enter_context(nc.psum_tensor(f"{name}_tps{j}", [P, P], F32)) for j in range(3)]
        turned, copied, top, indexed, removed, numbers, tables = (
            sem(f"{name}_{n}") for n in ("turned", "copied", "top", "indexed", "removed", "numbers", "tables"))
        with nc.Block() as block:

            @block.tensor
            def _(pe):
                for c in range(C):
                    tr = pe.transpose(pps[:, c * P:(c + 1) * P], probs[:, c, :], h["ident"][:])
                tr.then_inc(turned, 1)
                pe.wait_ge(numbers, 2)
                for j, src in enumerate((foundf, foundg, vals)):
                    tr = pe.transpose(tps[j][:], src[:], h["ident"][:])
                tr.then_inc(turned, 1)

            @block.vector
            def _(dve):
                v = nc.vector
                dve.wait_ge(turned, 1)
                v.tensor_copy(left[:], pps[:]).then_inc(copied, 1)
                dve.wait_ge(copied, 1)
                for r in range(K // 8):
                    eight = slice(r * 8, r * 8 + 8)
                    if r:
                        dve.wait_ge(removed, r)
                    v.max(vals[:, eight], left[:]).then_inc(top, 1)
                    dve.wait_ge(top, r + 1)
                    v.max_index(found[:, eight], vals[:, eight], left[:]).then_inc(indexed, 1)
                    v.match_replace(left[:], vals[:, eight], left[:], -1.0).then_inc(removed, 1)
                dve.wait_ge(indexed, K // 8)
                v.tensor_copy(foundf[:], found[:]).then_inc(numbers, 1)
                dve.wait_ge(numbers, 1)
                v.tensor_scalar(foundg[:], foundf[:], h["rowbase"][:], None, ALU.add).then_inc(numbers, 1)
                dve.wait_ge(turned, 2)
                v.tensor_copy(local[:], tps[0][:]).then_inc(tables, 1)
                v.tensor_copy(rows[:], tps[1][:]).then_inc(tables, 1)
                v.tensor_scalar(weight[:], tps[2][:], 0.5, None, ALU.mult).then_inc(tables, 1)
                dve.wait_ge(tables, 3)
    return local, rows, weight


def experts_layer(nc, sem, h, xres, xn_dram, probs, name, out):
    U = 2
    S = U * E
    RD, RO = 2, 4
    with ExitStack() as tmp:
        t = lambda n, s, d: tmp.enter_context(nc.sbuf_tensor(f"{name}_{n}", s, d))
        ps = lambda n, s, d: tmp.enter_context(nc.psum_tensor(f"{name}_{n}_ps", s, d))
        s = lambda n: sem(f"{name}_{n}")
        local, rows, weight = choose_tokens(nc, lambda n, sh, d: tmp.enter_context(nc.sbuf_tensor(n, sh, d)), sem, h, probs, name)
        row_c = [t(f"row_c{u}", [K, E], U32) for u in range(U)]
        loc_c = [t(f"loc_c{u}", [K, E], F32) for u in range(U)]
        wgt_c = [t(f"wgt_c{u}", [K, E], F32) for u in range(U)]
        x_in = [t(f"x_in{k}", [K, D], F32) for k in range(S)]
        x_t = [t(f"x_t{j}", [D, K], F32) for j in range(RD)]
        hid_t = [t(f"hid_t{j}", [P, FC, K], F32) for j in range(RD)]
        y = [t(f"y{j}", [K, D], F32) for j in range(RD)]
        hot = [t(f"hot{j}", [K, T], F32) for j in range(RO)]
        t_ps = [ps(f"t{j}", [D, K], F32) for j in range(RD)]
        h_ps = [ps(f"h{j}", [P, FC, K], F32) for j in range(RD)]
        y_ps = [ps(f"y{j}", [K, D], F32) for j in range(RD)]
        acc = [ps(f"acc{u}", [P, T], F32) for u in range(U)]
        gathered = [s(f"gathered{k}") for k in range(S)]
        rows_done, cols_done = s("rows_done"), s("cols_done")
        t_full, t_read, h_read, y_read, returned, x_added = (
            s("t_full"), s("t_read"), s("h_read"), s("y_read"), s("returned"), s("x_added"))
        h_full, y_full, hot_done = s("h_full"), s("y_full"), s("hot_done")
        stored, pool_turn, pe_turn = s("stored"), s("pool_turn"), s("pe_turn")
        turns = NB // U
        with nc.Block() as block:

            @block.gpsimd
            def _(pool):
                with pool.Fori(0, turns) as i:
                    for u in range(U):
                        pool.wait_ge(t_full, i * S + (u + 1) * E)
                        pool.sem_inc(pool_turn, 1)
                        nc.gpsimd.tensor_copy(row_c[u][:], rows[:, bass.ds((i * U + u) * E, E)]).then_inc(rows_done, 1)
                        pool.wait_ge(rows_done, i * U + u + 1)
                        pool.sem_inc(pool_turn, 1)
                        for e in range(E):
                            nc.gpsimd.indirect_dma_start(
                                out=x_in[u * E + e][:], out_offset=None, in_=xn_dram,
                                in_offset=bass.IndirectOffsetOnAxis(ap=row_c[u][:, e:e + 1], axis=0)).then_inc(gathered[u * E + e], 16)

            @block.tensor
            def _(pe):
                def transpose(i, k):
                    pe.wait_ge(gathered[k], i * 16 + 16)
                    pe.wait_ge(t_read, i * S + k + 1)
                    pe.transpose(t_ps[k % RD][:], x_in[k][:], h["ident"][:]).then_inc(t_full, 1)

                def up(i, k):
                    pe.wait_ge(t_read, RD + i * S + k + 1)
                    pe.wait_ge(h_read, i * S + k + 1)
                    for f in range(FC):
                        mm = pe.matmul(h_ps[k % RD][:, f, :], h["w1e"][:, k % E, f * P:(f + 1) * P], x_t[k % RD][:], start=True, stop=True)
                    mm.then_inc(h_full, 1)

                def down(i, k):
                    pe.wait_ge(h_read, RD + i * S + k + 1)
                    pe.wait_ge(y_read, i * S + k + 1)
                    for f in range(FC):
                        mm = pe.matmul(y_ps[k % RD][:], hid_t[k % RD][:, f, :], h["w2e"][:, k % E, f, :], start=(f == 0), stop=(f == FC - 1))
                    mm.then_inc(y_full, 1)

                def give_back(i, k):
                    u, e = k // E, k % E
                    pe.wait_ge(y_read, RD + i * S + k + 1)
                    pe.wait_ge(hot_done, i * S + k + 1)
                    if e == 0:
                        pe.wait_ge(x_added, i * U + u + 1)
                    for c in range(C):
                        mm = pe.matmul(acc[u][:, c * P:(c + 1) * P], hot[k % RO][:, c * P:(c + 1) * P], y[k % RD][:],
                                       start=(e == 0 and c == 0), stop=(e == E - 1), skip_group_check=True)
                    mm.then_inc(returned, 1)

                pe.sem_inc(t_full, S)
                pe.sem_inc(returned, RO)
                pe.wait_ge(h["experts_in"], 32)
                with pe.Fori(0, turns) as i:
                    for k in range(S + 3):
                        for stage, work in enumerate((transpose, up, down, give_back)):
                            if 0 <= k - stage < S:
                                work(i, k - stage)

            @block.scalar
            def _(act):
                a = nc.scalar
                act.sem_inc(h_read, RD)
                act.sem_inc(y_read, RD)
                with act.Fori(0, turns) as i:
                    for k in range(S + 1):
                        if k < S:
                            act.wait_ge(h_full, i * S + k + 1)
                            a.activation(hid_t[k % RD][:], h_ps[k % RD][:], ACT.Gelu).then_inc(h_read, 1)
                        if k:
                            j = k - 1
                            act.wait_ge(y_full, i * S + j + 1)
                            if j % E == 0:
                                act.wait_ge(cols_done, (i * U + j // E) * 2 + 2)
                            a.activation(y[j % RD][:], y_ps[j % RD][:], ACT.Copy, scale=wgt_c[j // E][:, j % E:j % E + 1]).then_inc(y_read, 1)

            @block.vector
            def _(dve):
                v = nc.vector

                def add(i, u):
                    dve.wait_ge(returned, RO + i * S + (u + 1) * E)
                    v.tensor_tensor(xres[:, i * U + u, :], acc[u][:], xres[:, i * U + u, :], ALU.add).then_inc(x_added, 1)

                dve.sem_inc(t_read, RD)
                dve.sem_inc(x_added, U)
                with dve.Fori(0, turns) as i:
                    for k in range(S):
                        u, e = k // E, k % E
                        if e == 0:
                            for src, dst in ((local, loc_c), (weight, wgt_c)):
                                v.tensor_copy(dst[u][:], src[:, bass.ds((i * U + u) * E, E)]).then_inc(cols_done, 1)
                        dve.wait_ge(t_full, S + i * S + k + 1)
                        v.tensor_copy(x_t[k % RD][:], t_ps[k % RD][:]).then_inc(t_read, 1)
                        if e == 0:
                            dve.wait_ge(cols_done, (i * U + u) * 2 + 1)
                        dve.wait_ge(returned, i * S + k + 1)
                        v.tensor_scalar(hot[k % RO][:], h["iota"][:], loc_c[u][:, e:e + 1], None, ALU.is_equal).then_inc(hot_done, 1)
                        if k == E + 3:
                            add(i, 0)
                    add(i, U - 1)

            @block.sync
            def _(sp):
                if out is not None:
                    with sp.Fori(0, NB) as n:
                        sp.wait_ge(x_added, U + n + 1)
                        sp.dma_start(out[n].rearrange("(c p) d -> p c d", p=P), xres[:, n, :].rearrange("p (c d) -> p c d", c=C)).then_inc(stored, 16)
                    sp.wait_ge(stored, 16 * NB)


def scan_layer(nc, sem, h, xres, xn_dram, probs):
    turns = NB // W4
    with ExitStack() as tmp:
        t = lambda n, s, d: tmp.enter_context(nc.sbuf_tensor(f"sc_{n}", s, d))
        s = lambda n: sem(f"sc_{n}")
        norm = Norm(nc, "sc", t, sem, h, xres, 2)
        gate = Gate(nc, "sc", t, s, h, probs)
        xhat = [t(f"xhat{b}", [P, T], F32) for b in range(W4)]
        xhat_t = [t(f"xhat_t{b}", [P, T], F32) for b in range(W4)]
        ts = [t(f"ts{b}", [P, T], F32) for b in range(W4)]
        fg = [t(f"fg{b}", [P, T], F32) for b in range(W4)]
        lam = [t(f"lam{b}", [P, T], F32) for b in range(W4)]
        a_ring = [tmp.enter_context(nc.psum_tensor(f"sc_a{j}", [P, T], F32)) for j in range(RING)]
        v_ring = [tmp.enter_context(nc.psum_tensor(f"sc_v{j}", [P, T], F32)) for j in range(RING)]
        a_full, a_read, v_full, v_read = s("a_full"), s("a_read"), s("v_full"), s("v_read")
        xhat_done, one_more, sig_done, scanned, pe_turn = s("xhat_done"), s("one_more"), s("sig_done"), s("scanned"), s("pe_turn")
        xn_out = [s(f"xn_out{b}") for b in range(W4)]
        XT, TF, LAM, XT2 = range(4)
        UIN, HOUT, SC = range(3)
        a_tile = lambda i, stage, b: (i * 4 + stage) * W4 + b
        v_tile = lambda i, stage, b: (i * 3 + stage) * W4 + b
        sig = lambda i, which, b: (i * 2 + which) * W4 + b + 1
        lo = slice(PR, P)
        with nc.Block() as block:

            @block.sync
            def _(sp):
                with sp.Fori(0, turns) as i:
                    for b in range(W4):
                        sp.wait_ge(xhat_done, i * 2 * W4 + W4 + b + 1)
                        sp.dma_start(xn_dram[bass.ds((i * W4 + b) * T, T), :].rearrange("(c p) d -> p c d", p=P),
                                     xhat[b][:].rearrange("p (c d) -> p c d", c=C)).then_inc(xn_out[b], 16)
                for b in range(W4):
                    sp.wait_ge(xn_out[b], 16 * turns)

            @block.tensor
            def _(pe):
                with pe.Fori(0, turns) as i:
                    for b in range(W4):
                        pe.wait_ge(xhat_done, i * 2 * W4 + b + 1)
                        pe.wait_ge(a_read, a_tile(i, XT, b) + 1)
                        transpose_chunks(pe, a_ring[b], xhat[b], h["ident"]).then_inc(a_full, 1)
                    for b in range(W4):
                        pe.wait_ge(a_read, RING + a_tile(i, XT, b) + 1)
                        pe.matmul(a_ring[b][:], h["wtf"][:], xhat_t[b][:], start=True, stop=True).then_inc(a_full, 1)
                    for b in range(W4):
                        pe.wait_ge(a_read, RING + a_tile(i, TF, b) + 1)
                        pe.wait_ge(v_read, v_tile(i, UIN, b) + 1)
                        pe.sem_inc(pe_turn, 1)
                        pe.matmul(v_ring[b][lo, :], h["bmat"][:], ts[b][0:PR, :], start=True, stop=True).then_inc(v_full, 1)
                        pe.wait_ge(sig_done, sig(i, 0, b))
                        pe.sem_inc(pe_turn, 1)
                        pe.matmul(a_ring[b][lo, :], h["wlam"][lo, :], fg[b][lo, :], start=True, stop=True).then_inc(a_full, 1)
                    for b in range(W4):
                        pe.wait_ge(scanned, i * W4 + b + 1)
                        pe.wait_ge(v_read, v_tile(i, HOUT, b) + 1)
                        for c in range(C):
                            mm = pe.matmul(v_ring[b][:, c * P:(c + 1) * P], ts[b][:, c * P:(c + 1) * P], h["wcw"][:], start=True, stop=True)
                        mm.then_inc(v_full, 1)
                    for b in range(W4):
                        pe.wait_ge(xhat_done, i * 2 * W4 + W4 + b + 1)
                        pe.wait_ge(a_read, a_tile(i, XT2, b) + 1)
                        transpose_chunks(pe, a_ring[b], xhat[b], h["ident"]).then_inc(a_full, 1)
                    for b in range(W4):
                        pe.wait_ge(a_read, RING + a_tile(i, XT2, b) + 1)
                        if b == 0:
                            pe.wait_ge(v_read, v_tile(i, SC, 0) + 1)
                        gate.tensor(pe, b, v_ring[0], xhat_t[b], v_full)

            @block.scalar
            def _(act):
                a = nc.scalar
                act.sem_inc(a_read, RING)
                with act.Fori(0, turns) as i:
                    for b in range(W4):
                        act.wait_ge(a_full, a_tile(i, XT, b) + 1)
                        a.activation(xhat_t[b][:], a_ring[b][:], ACT.Copy).then_inc(a_read, 1)
                    for b in range(W4):
                        act.wait_ge(a_full, a_tile(i, TF, b) + 1)
                        a.activation(ts[b][0:PR, :], a_ring[b][0:PR, :], ACT.Copy)
                        a.activation(fg[b][lo, :], a_ring[b][lo, :], ACT.Exp, scale=-1.0).then_inc(a_read, 1)
                    for b in range(W4):
                        act.wait_ge(a_full, a_tile(i, LAM, b) + 1)
                        a.activation(lam[b][lo, :], a_ring[b][lo, :], ACT.Exp, scale=-1.0).then_inc(a_read, 1)
                    for b in range(W4):
                        act.wait_ge(a_full, a_tile(i, XT2, b) + 1)
                        a.activation(xhat_t[b][:], a_ring[b][:], ACT.Copy).then_inc(a_read, 1)
                    act.wait_ge(v_read, RING + v_tile(i + 1, 0, 0))
                    gate.scalar(act)

            @block.gpsimd
            def _(pool):
                with pool.Fori(0, turns) as i:
                    norm.gpsimd(pool, i, 0)
                    norm.gpsimd(pool, i, 1)

            @block.vector
            def _(dve):
                v = nc.vector

                def sigmoid(i, which, stage, b, buf):
                    dve.wait_ge(a_read, RING + a_tile(i, stage, b) + 1)
                    v.tensor_scalar(buf[lo, :], buf[lo, :], 1.0, None, ALU.add).then_inc(one_more, 1)
                    dve.wait_ge(one_more, sig(i, which, b))
                    v.reciprocal(buf[lo, :], buf[lo, :]).then_inc(sig_done, 1)

                dve.sem_inc(v_read, RING)
                with dve.Fori(0, turns) as i:
                    norm.vector(dve, i, 0, xhat, xhat_done)
                    for b in range(W4):
                        sigmoid(i, 0, TF, b, fg[b])
                    for b in range(W4):
                        sigmoid(i, 1, LAM, b, lam[b])
                        dve.wait_ge(v_full, v_tile(i, UIN, b) + 1)
                        dve.wait_ge(sig_done, sig(i, 1, b))
                        v.tensor_tensor_scan(ts[b][lo, :], lam[b][lo, :], v_ring[b][lo, :], 0.0, ALU.mult, ALU.add).then_inc(scanned, 1)
                        dve.wait_ge(scanned, i * W4 + b + 1)
                        dve.sem_inc(v_read, 1)
                    for b in range(W4):
                        dve.wait_ge(v_full, v_tile(i, HOUT, b) + 1)
                        v.tensor_tensor(xres[:, i * W4 + b, :], v_ring[b][:], xres[:, i * W4 + b, :], ALU.add).then_inc(v_read, 1)
                    dve.wait_ge(v_read, RING + v_tile(i, SC, 0))
                    norm.vector(dve, i, 1, xhat, xhat_done)
                    dve.wait_ge(v_full, v_tile(i + 1, 0, 0))
                    gate.vector(dve, i, v_ring[0], v_read)
                    for b in range(W4):
                        dve.wait_ge(xn_out[b], i * 16 + 16)


def program(nc, w, out):
    with ExitStack() as ctx:
        sb = lambda n, s, d: ctx.enter_context(nc.sbuf_tensor(n, s, d))
        sem = lambda n: ctx.enter_context(nc.semaphore(n))
        dram = lambda n, s, d: nc.dram_tensor(n, s, d, kind="Internal").ap()
        q_dram = dram("q_parts", [NB, PARTS * P, T], BF16)
        k_dram = dram("k_parts", [NB, PARTS * 96, T], BF16)
        xn_dram = dram("xn", [NB * T, D], F32)
        xres = sb("xres", [P, NB, T], F32)
        v_all = sb("v_all", [P, NB, C * 32], F32)
        probs = sb("probs", [P, C, NB * E], F32)
        h = load_constants(nc, w, sb, sem)

        def layer(build, *args, **kw):
            sems = []

            def sem(n):
                sems.append(nc.alloc_semaphore(name=n))
                return sems[-1]

            build(nc, sem, h, xres, *args, **kw)
            nc.clear_and_free_semaphores(sems)
            nc.all_engine_barrier()

        layer(mlp_layer, "qkv", "m1", x_src=w["x"], q_dram=q_dram, k_dram=k_dram, v_all=v_all)
        layer(attention, q_dram, k_dram, v_all)
        layer(mlp_layer, "gate", "m2", xn_dram=xn_dram, probs=probs)
        layer(experts_layer, xn_dram, probs, "e1", None)
        layer(scan_layer, xn_dram, probs)
        layer(experts_layer, xn_dram, probs, "e2", out)


_OUTS = [((16, 512, 128), 'float32')]


def layouts(i):
    import numpy as np

    a = {k: np.ascontiguousarray(v) for k, v in i.items()}
    half = HD // 2
    wq = a["L0_attn_Wq"].reshape(D, NH, HD).transpose(0, 2, 1)
    wk = a["L0_attn_Wk"].reshape(D, NKV, HD).transpose(0, 2, 1)
    swap = np.r_[half:HD, 0:half]
    three = lambda x: np.tile(x.reshape(D, NKV * HD), (1, PARTS))
    twice = lambda x: np.concatenate([x, x], 0)
    hm = lambda x: x.reshape(M, HT, 2).transpose(2, 0, 1).reshape(P, HT)
    w = {
        "x": a["L0_attn_x"],
        "win2": np.concatenate([a["L0_ffn_Win"]] * 2, 1), "bin2": twice(a["L0_ffn_bin_"])[:, None],
        "w1p": hm(a["L0_ffn_W1"]), "b1p": hm(a["L0_ffn_b1"]), "w2p": hm(a["L0_ffn_W2"]),
        "b2p": np.concatenate([a["L0_ffn_b2"], np.zeros(M, np.float32)])[:, None],
        "wout2": twice(a["L0_ffn_Wout"]), "bout": a["L0_ffn_bout"][:, None],
        "wq": wq.reshape(D, D), "wqs": wq[:, swap].reshape(D, D), "wk": three(wk), "wks": three(wk[:, swap]),
        "wv": a["L0_attn_Wv"], "wo": a["L0_attn_Wo"],
        "gw": a["L1_ffn_gate_w"].T, "w1e": a["L1_ffn_w1"].transpose(1, 0, 2),
        "w2e": a["L1_ffn_w2"].reshape(E, FC, P, D).transpose(2, 0, 1, 3),
        "wu": a["L1_attn_W_U"].reshape(D, M * 4), "wv4": a["L1_attn_W_V"].reshape(1, M * 4),
        "wtop": a["L1_attn_W_toP"], "wf": a["L1_attn_W_F"], "wlam": a["L1_attn_W_lam"], "bmat": a["L1_attn_B_mat"],
        "ct": a["L1_attn_C_mat"].T, "wfromp": a["L1_attn_W_fromP"],
    }
    f32 = np.float32
    freq = (f32(1.0) / np.power(f32(10000.0), np.arange(half, dtype=f32) / f32(half))).astype(f32)
    angle = np.arange(T, dtype=f32)[None, :] * freq[:, None]
    cos = np.cos(np.concatenate([angle, angle])).astype(f32)
    sin = np.sin(np.concatenate([angle, angle])).astype(f32)
    sin[:half] *= f32(-1)
    w["cosq"], w["sinq"] = np.repeat(cos, NH, 0), np.repeat(sin, NH, 0)
    w["cosk"], w["sink"] = (np.tile(np.repeat(x, NKV, 0), (PARTS, 1)) for x in (cos, sin))
    at = np.arange(P)
    w["ident"] = np.eye(P, dtype=f32)
    w["mask"] = np.where(at[None, :] > at[:, None], f32(MASKED), f32(0))
    w["iota"] = np.broadcast_to(np.arange(T, dtype=f32), (P, T))
    w["rowbase"] = (at // E * T).astype(f32)[:, None]
    w["mhalf"] = np.full((P, W4 * C), -0.5, f32)
    return {k: np.ascontiguousarray(v) for k, v in w.items()}


def kernel(**inputs):
    import numpy as _np
    import concourse.bacc as _bacc
    from concourse import mybir as _mybir
    from concourse.bass_utils import run_bass_kernel_spmd as _run

    nc = _bacc.Bacc("TRN2", target_bir_lowering=False, num_devices=1)
    arrays, w = {}, {}
    for name, a in layouts(inputs).items():
        arrays[f"in_{name}_dram"] = a
        w[name] = nc.dram_tensor(f"in_{name}_dram", a.shape, _mybir.dt.from_np(a.dtype), kind="ExternalInput").ap()
    outs = [nc.dram_tensor(f"out_{i}_dram", s, _mybir.dt.from_np(_np.dtype(d)), kind="ExternalOutput").ap()
            for i, (s, d) in enumerate(_OUTS)]
    program(nc, w, outs[0])
    r = _run(nc, [arrays], core_ids=[0])
    return r.results[0]["out_0_dram"]
```

```python
from contextlib import ExitStack

import concourse.bass as bass
from concourse import mybir

F32 = mybir.dt.float32
BF16 = mybir.dt.bfloat16
U32 = mybir.dt.uint32
ALU = mybir.AluOpType
ACT = mybir.ActivationFunctionType
AX = mybir.AxisListType

P = 128
NB = 16
T = 512
D = 128
C = T // P
EPS = 1e-5
NH, NKV = 16, 4
HD = D // NH
GH = NH // NKV
SCALE = HD ** -0.5
PARTS = 3
KQ = PARTS * PARTS * HD
KM = KQ + 2
MASKED = -1.0e38
M = 64
INNER = 16
HT = M * INNER // P
HV = 5
E = 8
F = 512
FC = F // P
K = 2 * T // E
PR = 64
W = 2
TURNS = NB // W


def load_constants(nc, w, sb, sem):
    h = {}
    for n, s, d in [
        ("win2", [P, P], F32), ("bin2", [P, 1], F32), ("w1p", [P, HT], F32), ("nb1p", [P, HT], F32), ("b1p", [P, HT], F32),
        ("w2d", [P, HT, M], F32), ("woutz", [P, W, D], F32), ("gbias", [P, 1], F32), ("yrow", [P, D], F32),
        ("wq", [P, D], F32), ("wqs", [P, D], F32), ("wk", [P, NKV * HD], F32),
        ("wks", [P, NKV * HD], F32), ("wv", [P, NKV * HD], F32), ("wo", [P, D], F32),
        ("cosq", [P, T], F32), ("sinq", [P, T], F32), ("cosk", [W * NKV * HD, T], F32), ("sink", [W * NKV * HD, T], F32),
        ("ident", [P, P], F32), ("identb", [P, P], BF16), ("maskb", [P, P], BF16), ("iota", [P, T], F32),
        ("gw", [P, E], F32), ("wtf", [P, P], F32), ("wlam", [P, PR], F32), ("bmat", [PR, PR], F32),
        ("wcw", [P, D], F32), ("w1e", [P, E, F], F32), ("w2e", [P, E, FC, D], F32),
        ("rowbase", [P, 1], F32), ("mhalf", [P, W * C], F32),
    ]:
        h[n] = sb(n, s, d)
    with ExitStack() as tmp:
        t = lambda n, s, d: tmp.enter_context(nc.sbuf_tensor(n, s, d))
        wout2 = t("wout2", [P, D], F32)
        w2p = t("w2p", [P, HT], F32)
        b2p = t("b2p", [P, 1], F32)
        pairsum = t("pairsum", [P, P], F32)
        b1w2 = t("b1w2", [P, HV], F32)
        csum = t("csum", [P, 1], F32)
        wu = t("wu", [P, M * 4], F32)
        wv4 = t("wv4", [P, M * 4], F32)
        wtop = t("wtop", [P, M], F32)
        ct = t("ct", [PR, PR], F32)
        maskf = t("maskf", [P, P], F32)
        cps = tmp.enter_context(nc.psum_tensor("cps", [P, 512], F32))
        small_in, experts_in = sem("small_in"), sem("experts_in")
        fold, fold_mm, cast = sem("fold"), sem("fold_mm"), sem("cast")
        h["experts_in"] = experts_in
        loads = [
            (h["win2"][:], w["win2"]), (h["bin2"][:], w["bin2"]), (h["w1p"][:], w["w1p"]),
            (wout2[:], w["wout2"]), (w2p[:], w["w2p"]), (h["b1p"][:], w["b1p"]), (b2p[:], w["b2p"]),
            (h["yrow"][:], w["bout"].to_broadcast([P, D])), (pairsum[:], w["pairsum"]), (h["wq"][:], w["wq"]), (h["wqs"][:], w["wqs"]), (h["wk"][:], w["wk"]),
            (h["wks"][:], w["wks"]), (h["wv"][:], w["wv"]), (h["wo"][:], w["wo"]), (h["cosq"][:], w["cosq"]),
            (h["sinq"][:], w["sinq"]), (h["cosk"][:], w["cosk"]), (h["sink"][:], w["sink"]),
            (h["ident"][:], w["ident"]), (maskf[:], w["mask"]), (h["iota"][:], w["iota"]), (h["gw"][:], w["gw"]),
            (wu[:], w["wu"]), (wv4[:], w["wv4"].to_broadcast([P, M * 4])), (wtop[:], w["wtop"]),
            (h["wtf"][:, M:P], w["wf"]), (h["wlam"][PR:P, :], w["wlam"]), (h["bmat"][:], w["bmat"]),
            (ct[:], w["ct"]), (h["wcw"][0:PR, :], w["wfromp"]), (h["rowbase"][:], w["rowbase"]),
            (h["mhalf"][:], w["mhalf"]),
        ]
        with nc.Block() as block:

            @block.sync
            def _(sp):
                for dst, src in loads:
                    sp.dma_start(dst, src).then_inc(small_in, 16)
                sp.wait_ge(small_in, 16 * len(loads))
                sp.dma_start(h["w1e"][:], w["w1e"]).then_inc(experts_in, 16)
                sp.dma_start(h["w2e"][:], w["w2e"]).then_inc(experts_in, 16)

            @block.vector
            def _(dve):
                v = nc.vector
                dve.wait_ge(small_in, 16 * len(loads))
                v.tensor_copy(h["identb"][:], h["ident"][:])
                v.tensor_copy(h["maskb"][:], maskf[:])
                v.tensor_scalar(h["nb1p"][:], h["b1p"][:], -1.0, None, ALU.mult)
                for j in range(HT):
                    v.tensor_scalar(h["w2d"][:, j, :], pairsum[:, 0:M], w2p[:, j:j + 1], 0.5, ALU.mult, ALU.mult)
                v.memset(h["woutz"][:], 0.0).then_inc(cast, 1)
                dve.wait_ge(cast, 1)
                for b in range(W):
                    half = slice(b * M, (b + 1) * M)
                    v.tensor_copy(h["woutz"][half, b, :], wout2[half, :])
                v.tensor_scalar(h["yrow"][:], h["yrow"][:], 0.5, None, ALU.mult)
                v.tensor_tensor(b1w2[:], w2p[:, 0:HV], h["b1p"][:, 0:HV], ALU.mult).then_inc(fold, 1)
                dve.wait_ge(fold, 1)
                v.tensor_reduce(csum[:], b1w2[:], AX.X, ALU.add).then_inc(fold, 1)
                dve.wait_ge(fold, 2)
                v.tensor_tensor(csum[:], csum[:], b2p[:], ALU.add).then_inc(fold, 1)
                v.tensor_tensor(wu[:], wu[:], wv4[:], ALU.mult).then_inc(fold, 1)
                dve.wait_ge(fold, 4)
                v.tensor_reduce(h["wtf"][:, 0:M], wu[:].rearrange("p (m a) -> p m a", a=4), AX.X, ALU.add).then_inc(fold, 1)
                dve.wait_ge(fold, 5)
                v.tensor_tensor(h["wtf"][:, 0:M], h["wtf"][:, 0:M], wtop[:], ALU.add)
                dve.wait_ge(fold_mm, 2)
                v.tensor_scalar(h["gbias"][:], cps[:, 0:1], 0.5, None, ALU.mult)
                v.tensor_copy(h["wcw"][PR:P, :], cps[PR:P, 128:256]).then_inc(cast, 1)
                dve.wait_ge(cast, 2)

            @block.tensor
            def _(pe):
                pe.wait_ge(small_in, 16 * len(loads))
                pe.wait_ge(fold, 3)
                pe.matmul(cps[:, 0:1], pairsum[:], csum[:], start=True, stop=True).then_inc(fold_mm, 1)
                pe.matmul(cps[PR:P, 128:256], ct[:], h["wcw"][0:PR, :], start=True, stop=True).then_inc(fold_mm, 1)
    return h


class Norm:

    def __init__(self, nc, name, sb, sem, h, xres):
        self.nc, self.h, self.xres = nc, h, xres
        self.stats = sb(name + "_stats", [P, W * C, 6], F32)
        self.mv = sb(name + "_mv", [P, W * C, 2], F32)
        self.vare = sb(name + "_vare", [P, W * C], F32)
        self.rstd = sb(name + "_rstd", [P, W * C], F32)
        self.xhat = [sb(f"{name}_xhat{b}", [P, T], F32) for b in range(W)]
        self.stats_done, self.mv_done = sem(name + "_stats_done"), sem(name + "_mv_done")
        self.var_done, self.rstd_done = sem(name + "_var_done"), sem(name + "_rstd_done")
        self.xhat_done = sem(name + "_xhat_done")
        self.pool_turn, self.dve_turn = sem(name + "_pool_turn"), sem(name + "_dve_turn")

    def moments(self, dve, i):
        v = self.nc.vector
        dve.sem_inc(self.dve_turn, 1)
        for b in range(W):
            for c in range(C):
                s = v.bn_stats(self.stats[:, b * C + c, :], self.xres[:, i * W + b, c * D:(c + 1) * D])
        s.then_inc(self.stats_done, 1)
        dve.wait_ge(self.stats_done, i + 1)
        dve.sem_inc(self.dve_turn, 1)
        for j in range(W * C):
            s = v.bn_aggr(self.mv[:, j, :], self.stats[:, j, :])
        s.then_inc(self.mv_done, 1)
        dve.wait_ge(self.mv_done, i + 1)
        v.tensor_scalar(self.vare[:], self.mv[:, :, 1], EPS, None, ALU.add).then_inc(self.var_done, 1)

    def gpsimd(self, pool, i):
        pool.wait_ge(self.var_done, i + 1)
        pool.sem_inc(self.pool_turn, 1)
        self.nc.gpsimd.tensor_tensor(self.rstd[:], self.vare[:], self.h["mhalf"][:], ALU.pow).then_inc(self.rstd_done, 1)

    def apply(self, dve, i):
        dve.wait_ge(self.rstd_done, i + 1)
        for b in range(W):
            for c in range(C):
                j = b * C + c
                s = self.nc.vector.tensor_scalar(
                    self.xhat[b][:, c * D:(c + 1) * D], self.xres[:, i * W + b, c * D:(c + 1) * D],
                    self.mv[:, j, 0:1], self.rstd[:, j:j + 1], ALU.subtract, ALU.mult)
            s.then_inc(self.xhat_done, 1)


class Gate:

    def __init__(self, nc, sb, sem, h, probs, bank):
        self.nc, self.h, self.probs, self.bank = nc, h, probs, bank
        self.mx = sb("mx", [P, W * C], F32)
        self.ex = sb("ex", [P, W, C, E], F32)
        self.den = sb("den", [P, W * C], F32)
        self.rden = sb("rden", [P, W * C], F32)
        self.scored, self.maxed, self.read = sem("scored"), sem("maxed"), sem("scores_read")
        self.exp_done, self.summed, self.inverted = sem("exp_done"), sem("summed"), sem("inverted")
        self.probs_done = sem("probs_done")

    def tensor(self, pe, i, b, xhat_t):
        if b == 0:
            after(pe, self.read, i)
        for c in range(C):
            at = (b * C + c) * E
            mm = pe.matmul(self.bank[:, at:at + E], xhat_t[:, c * P:(c + 1) * P], self.h["gw"][:], start=True, stop=True)
        mm.then_inc(self.scored, 1)

    def scalar(self, act, i):
        act.wait_ge(self.read, i + 1)
        self.nc.scalar.activation(self.ex[:], self.ex[:], ACT.Exp).then_inc(self.exp_done, 1)

    def less_max(self, dve, i):
        v = self.nc.vector
        sc = self.bank[:, 0:W * C * E].rearrange("p (j e) -> p j e", e=E)
        dve.wait_ge(self.scored, (i + 1) * W)
        v.tensor_reduce(self.mx[:], sc, AX.X, ALU.max).then_inc(self.maxed, 1)
        dve.wait_ge(self.maxed, i + 1)
        v.tensor_tensor(self.ex[:].rearrange("p b c e -> p (b c) e"), sc,
                        self.mx[:].unsqueeze(2).to_broadcast([P, W * C, E]), ALU.subtract).then_inc(self.read, 1)

    def normalise(self, dve, i):
        v = self.nc.vector
        dve.wait_ge(self.exp_done, i + 1)
        v.tensor_reduce(self.den[:], self.ex[:].rearrange("p b c e -> p (b c) e"), AX.X, ALU.add).then_inc(self.summed, 1)
        dve.wait_ge(self.summed, i + 1)
        v.reciprocal(self.rden[:], self.den[:]).then_inc(self.inverted, 1)
        dve.wait_ge(self.inverted, i + 1)
        for b in range(W):
            pr = v.tensor_tensor(self.probs[:, :, bass.ds((i * W + b) * E, E)], self.ex[:, b],
                                 self.rden[:, b * C:(b + 1) * C].unsqueeze(2).to_broadcast([P, C, E]), ALU.mult)
        pr.then_inc(self.probs_done, 1)
        dve.wait_ge(self.probs_done, i + 1)


def transpose_chunks(pe, out, src, ident):
    for c in range(C):
        last = pe.transpose(out[:, c * P:(c + 1) * P], src[:, c * P:(c + 1) * P], ident[:])
    return last


def after(eng, sem, value):
    if not (isinstance(value, int) and value <= 0):
        eng.wait_ge(sem, value)


def pipeline(eng, turn):
    turn(0, None, None)
    turn(1, 0, None)
    turn(2, 1, 0)
    with eng.Fori(0, TURNS - 3) as r:
        turn(r + 3, r + 2, r + 1)
    turn(None, TURNS - 1, TURNS - 2)
    turn(None, None, TURNS - 1)


def mlp_layer(nc, sem, h, xres, tail_kind, name, x_src=None, q_dram=None, k_dram=None, v_all=None,
              xn_dram=None, probs=None):
    qkv = tail_kind == "qkv"
    with ExitStack() as tmp:
        t = lambda n, s, d: tmp.enter_context(nc.sbuf_tensor(f"{name}_{n}", s, d))
        s = lambda n: sem(f"{name}_{n}")
        bank = lambda n: tmp.enter_context(nc.psum_tensor(f"{name}_{n}_ps", [P, T], F32))
        norm1, norm2 = Norm(nc, "n1", t, s, h, xres), Norm(nc, "n2", t, s, h, xres)
        xhat_t = [t(f"xhat_t{b}", [P, T], F32) for b in range(W)]
        xhat2_t = [t(f"xhat2_t{b}", [P, T], F32) for b in range(W)]
        s_in = [t(f"s{b}", [P, T], F32) for b in range(W)]
        hid = [[t(f"hid{b}{j}", [P, T], F32) for j in range(HT)] for b in range(W)]
        g_t = t("g_t", [P, T], F32)
        xt_ps, s_ps = [bank(f"xt{b}") for b in range(W)], [bank(f"s{b}") for b in range(W)]
        g_ps = xt_ps[0]
        r_ps = [bank(f"r{j}") for j in range(4)]
        y_ps = [r_ps[3], r_ps[0]]
        x_in = s("x_in")
        xt_full, xt_read, s_full, s_read, hid_done, hid_a_done, hid_used = (
            s("xt_full"), s("xt_read"), s("s_full"), s("s_read"), s("hid_done"), s("hid_a_done"), s("hid_used"))
        g_read, bias_added, y_full, x_added, xt2_full, xt2_read = (
            s("g_read"), s("bias_added"), s("y_full"), s("x_added"), s("xt2_full"), s("xt2_read"))
        bias_turn = s("bias_turn")
        if qkv:
            KR = NKV * HD
            TILES = [(f"q{b}", P) for b in range(W)] + [("k", W * KR)]
            NT = len(TILES)
            OUT = [16] * W + [16 * W * PARTS]
            rot = {}
            for n, rows in TILES:
                rot[n] = dict(a=t(f"{n}a", [rows, T], F32), b=t(f"{n}b", [rows, T], F32),
                              parts=t(f"{n}parts", [rows, PARTS, T], BF16))
            rope_full, rope_read, v_full, v_read = s("rope_full"), s("rope_read"), s("v_full"), s("v_read")
            full_done, p1_done, r1_done, p2_done, p3_done = (
                s("full_done"), s("p1_done"), s("r1_done"), s("p2_done"), s("p3_done"))
            parts_out = [s(f"parts_out_{n}") for n, _ in TILES]
            pool_turn = s("rope_pool_turn")
        else:
            gate = Gate(nc, t, s, h, probs, r_ps[2])
            xn_out = [s(f"xn_out{b}") for b in range(W)]
        with nc.Block() as block:

            @block.sync
            def _(sp):
                if x_src is not None:
                    for i in range(TURNS):
                        sp.dma_start(xres[:, i * W:(i + 1) * W, :].rearrange("p n (c d) -> p n c d", c=C),
                                     x_src[i * W:(i + 1) * W].rearrange("n (c p) d -> p n c d", p=P)).then_inc(x_in, 16)
                        sp.wait_ge(x_in, 16 * (i + 1))
                with sp.Fori(0, TURNS) as i:
                    if qkv:
                        for b in range(W):
                            sp.wait_ge(p3_done, i * NT + b + 1)
                            sp.dma_start(q_dram[i * W + b].rearrange("(j p) t -> p j t", p=P),
                                         rot[f"q{b}"]["parts"][:]).then_inc(parts_out[b], 16)
                        sp.wait_ge(p3_done, i * NT + NT)
                        for b in range(W):
                            for copy in range(PARTS):
                                sp.dma_start(k_dram[i * W + b].rearrange("(j c p) t -> c p j t", c=PARTS, p=KR)[copy],
                                             rot["k"]["parts"][b * KR:(b + 1) * KR]).then_inc(parts_out[W], 16)
                    else:
                        for b in range(W):
                            sp.wait_ge(norm2.xhat_done, i * W + b + 1)
                            sp.dma_start(xn_dram[bass.ds((i * W + b) * T, T), :].rearrange("(c p) d -> p c d", p=P),
                                         norm2.xhat[b][:].rearrange("p (c d) -> p c d", c=C)).then_inc(xn_out[b], 16)
                if qkv:
                    for x in range(NT):
                        sp.wait_ge(parts_out[x], OUT[x] * TURNS)
                else:
                    for b in range(W):
                        sp.wait_ge(xn_out[b], 16 * TURNS)

            @block.tensor
            def _(pe):
                def channels(i):
                    for j in range(HT):
                        for b in range(W):
                            if j < HV:
                                pe.wait_ge(hid_done, (i * W + b) * HV + j + 1)
                            else:
                                pe.wait_ge(hid_a_done, (i * W + b) * (HT - HV) + j - HV + 1)
                            mm = pe.matmul(g_ps[b * M:(b + 1) * M, :], h["w2d"][:, j, :], hid[b][j][:],
                                           start=(j == 0), stop=(j == HT - 1))
                            if b == W - 1:
                                mm.then_inc(hid_used, 1)

                def output(i, tail):
                    pe.wait_ge(g_read, i + 1)
                    for b in range(W):
                        if qkv and tail is not None:
                            after(pe, rope_read, tail * 2 * NT)
                        for c in range(C):
                            mm = pe.matmul(y_ps[b][:, c * P:(c + 1) * P], g_t[:, c * P:(c + 1) * P], h["woutz"][:, b, :],
                                           start=True, stop=True)
                        mm.then_inc(y_full, 1)

                def queries(i, b):
                    for j, wt in enumerate(("wq", "wqs")):
                        if b == 1 and j == 0:
                            after(pe, v_read, i)
                        if b == 0 and j == 0:
                            pe.wait_ge(x_added, min((i + 2) * W, NB) if isinstance(i, int) else (i + 2) * W)
                        pe.matmul(r_ps[2 * b + j][:], h[wt][:], xhat2_t[b][:], start=True, stop=True).then_inc(rope_full, 1)

                def keys(i):
                    for j, wt in enumerate(("wk", "wks")):
                        pe.wait_ge(rope_read, i * 2 * NT + j + 1)
                        for b in range(W):
                            mm = pe.matmul(r_ps[j][b * KR:(b + 1) * KR, :], h[wt][:], xhat2_t[b][:], start=True, stop=True)
                        mm.then_inc(rope_full, 1)

                def values(i):
                    pe.wait_ge(rope_read, i * 2 * NT + 3)
                    for b in range(W):
                        for c in range(C):
                            mm = pe.matmul(r_ps[2][:, (b * C + c) * KR:(b * C + c + 1) * KR], xhat2_t[b][:, c * P:(c + 1) * P], h["wv"][:],
                                           start=True, stop=True)
                    mm.then_inc(v_full, 1)

                def turn(head, middle, tail):
                    if middle is not None:
                        channels(middle)
                    if tail is not None:
                        for b in range(W):
                            pe.wait_ge(norm2.xhat_done, tail * W + b + 1)
                            transpose_chunks(pe, s_ps[b], norm2.xhat[b], h["ident"]).then_inc(xt2_full, 1)
                    if middle is not None:
                        output(middle, tail)
                    if head is not None:
                        for b in range(W):
                            pe.wait_ge(norm1.xhat_done, head * W + b + 1)
                            if middle is not None:
                                pe.wait_ge(g_read, middle + 1)
                            transpose_chunks(pe, xt_ps[b], norm1.xhat[b], h["ident"]).then_inc(xt_full, 1)
                    if tail is not None:
                        pe.wait_ge(xt2_read, tail * W + W)
                        if qkv:
                            queries(tail, 0)
                        else:
                            for b in range(W):
                                gate.tensor(pe, tail, b, xhat2_t[b])
                    if head is not None:
                        for b in range(W):
                            pe.wait_ge(xt_read, head * W + b + 1)
                            pe.matmul(s_ps[b][:], h["win2"][:], xhat_t[b][:], start=True, stop=True).then_inc(s_full, 1)
                    if qkv and tail is not None:
                        queries(tail, 1)
                        keys(tail)
                    if qkv and tail is not None:
                        values(tail)

                pipeline(pe, turn)

            @block.scalar
            def _(act):
                a = nc.scalar

                def split(tail):
                    for x in range(NT + 1):
                        if x < NT:
                            r = rot[TILES[x][0]]
                            act.wait_ge(full_done, tail * NT + x + 1)
                            a.activation(r["parts"][:, 0, :], r["a"][:], ACT.Copy).then_inc(p1_done, 1)
                        if x > 0:
                            r = rot[TILES[x - 1][0]]
                            act.wait_ge(r1_done, tail * NT + x)
                            a.activation(r["parts"][:, 1, :], r["b"][:], ACT.Copy).then_inc(p2_done, 1)

                def turn(head, middle, tail):
                    if middle is not None:
                        act.wait_ge(hid_used, (middle + 1) * HT)
                        a.activation(g_t[:], g_ps[:], ACT.Identity, bias=h["gbias"][:]).then_inc(g_read, 1)
                    if tail is not None:
                        for b in range(W):
                            act.wait_ge(xt2_full, tail * W + b + 1)
                            a.activation(xhat2_t[b][:], s_ps[b][:], ACT.Copy).then_inc(xt2_read, 1)
                    if head is not None:
                        for b in range(W):
                            act.wait_ge(xt_full, head * W + b + 1)
                            a.activation(xhat_t[b][:], xt_ps[b][:], ACT.Copy).then_inc(xt_read, 1)
                    if not qkv and tail is not None:
                        gate.scalar(act, tail)
                    if head is not None:
                        for b in range(W):
                            act.wait_ge(s_full, head * W + b + 1)
                            a.activation(s_in[b][:], s_ps[b][:], ACT.Identity, bias=h["bin2"][:]).then_inc(s_read, 1)
                        for b in range(W):
                            act.wait_ge(s_read, head * W + b + 1)
                            for j in range(HV, HT):
                                a.activation(hid[b][j][:], s_in[b][:], ACT.Relu, bias=h["b1p"][:, j:j + 1],
                                             scale=h["w1p"][:, j:j + 1]).then_inc(hid_a_done, 1)
                    if qkv and tail is not None:
                        split(tail)

                pipeline(act, turn)

            @block.gpsimd
            def _(pool):
                g = nc.gpsimd

                def split(tail):
                    for x in range(NT + 2):
                        if x < NT:
                            r = rot[TILES[x][0]]
                            pool.wait_ge(rope_read, (tail * NT + x) * 2 + 2)
                            pool.sem_inc(pool_turn, 1)
                            g.tensor_tensor(r["a"][:], r["a"][:], r["b"][:], ALU.add).then_inc(full_done, 1)
                        if 1 <= x <= NT:
                            r = rot[TILES[x - 1][0]]
                            pool.wait_ge(full_done, tail * NT + x)
                            pool.wait_ge(p1_done, tail * NT + x)
                            pool.sem_inc(pool_turn, 1)
                            g.tensor_tensor(r["b"][:], r["a"][:], r["parts"][:, 0, :], ALU.subtract).then_inc(r1_done, 1)
                        if x >= 2:
                            r = rot[TILES[x - 2][0]]
                            pool.wait_ge(r1_done, tail * NT + x - 1)
                            pool.wait_ge(p2_done, tail * NT + x - 1)
                            pool.sem_inc(pool_turn, 1)
                            g.tensor_tensor(r["parts"][:, 2, :], r["b"][:], r["parts"][:, 1, :], ALU.subtract).then_inc(p3_done, 1)

                def turn(head, middle, tail):
                    if tail is not None:
                        norm2.gpsimd(pool, tail)
                    if head is not None:
                        norm1.gpsimd(pool, head)
                        pool.wait_ge(norm1.xhat_done, (head + 1) * W)
                        pool.sem_inc(bias_turn, 1)
                        for b in range(W):
                            x = xres[:, head * W + b, :].rearrange("p (c d) -> p c d", c=C)
                            bias = g.tensor_tensor(x, x, h["yrow"][:].unsqueeze(1).to_broadcast([P, C, D]), ALU.add)
                        bias.then_inc(bias_added, 1)
                    if qkv and tail is not None:
                        split(tail)

                pipeline(pool, turn)

            @block.vector
            def _(dve):
                v = nc.vector

                def hidden(i):
                    for b in range(W):
                        dve.wait_ge(s_read, i * W + b + 1)
                        for j in range(HV):
                            after(dve, hid_used, (i - 1) * HT + j + 1)
                            v.tensor_scalar(hid[b][j][:], s_in[b][:], h["w1p"][:, j:j + 1], h["nb1p"][:, j:j + 1],
                                            ALU.mult, ALU.max).then_inc(hid_done, 1)

                def rope(i):
                    for x, (n, rows) in enumerate(TILES):
                        r = rot[n]
                        after(dve, parts_out[x], i * OUT[x])
                        for j, (dst, tab) in enumerate((("a", "cos"), ("b", "sin"))):
                            dve.wait_ge(rope_full, (i * NT + x) * 2 + j + 1)
                            v.tensor_tensor(r[dst][:], r_ps[(2 * x + j) % 4][0:rows, :], h[tab + n[0]][:], ALU.mult).then_inc(rope_read, 1)

                def turn(head, middle, tail):
                    if middle is not None:
                        hidden(middle)
                    if tail is not None:
                        dve.wait_ge(x_added, tail * W + W)
                        norm2.moments(dve, tail)
                    if head is not None:
                        if x_src is not None:
                            dve.wait_ge(x_in, 16 * (head + 1))
                        norm1.moments(dve, head)
                    if tail is not None:
                        if not qkv:
                            for b in range(W):
                                after(dve, xn_out[b], tail * 16)
                        norm2.apply(dve, tail)
                    if head is not None:
                        norm1.apply(dve, head)
                    if middle is not None:
                        dve.wait_ge(bias_added, middle + 1)
                        for b in range(W):
                            dve.wait_ge(y_full, middle * W + b + 1)
                            v.tensor_tensor(xres[:, middle * W + b, :], y_ps[b][:], xres[:, middle * W + b, :], ALU.add).then_inc(x_added, 1)
                    if tail is not None:
                        if qkv:
                            rope(tail)
                            dve.wait_ge(v_full, tail + 1)
                            v.tensor_copy(v_all[:, bass.ds(tail * W, W), :],
                                          r_ps[2][:, 0:W * C * KR].rearrange("p (b x) -> p b x", b=W)).then_inc(v_read, 1)
                        else:
                            gate.less_max(dve, tail)
                            gate.normalise(dve, tail)

                pipeline(dve, turn)


SW = 512
XW = 1024
S_TILES = [(0, range(0, 4)), (1, range(0, 2)), (1, range(2, 4))] + [(c, [j]) for c in (2, 3) for j in range(GH)]
S_SLOTS = [range(0, 2), range(2, 4), range(4, 6), range(6, 8), range(8, 11)]
NS = len(S_TILES)
NX = GH + 1
X_HEAD = [(0, 0), (1, 512), (3, 896)]
NP = 4
LAG = 2


def attention(nc, sem, h, xres, q_dram, k_dram, v_all):
    m_dram = nc.dram_tensor("row_max", [2, 2, NH * C, P], BF16, kind="Internal").ap()
    with ExitStack() as tmp:
        t = lambda n, s, d: tmp.enter_context(nc.sbuf_tensor(f"at_{n}", s, d))
        ps = lambda n, s, d: tmp.enter_context(nc.psum_tensor(f"at_{n}_ps", s, d))
        s = lambda n: sem(f"at_{n}")
        qr = [t(f"qr{u}", [P, NH * T], BF16) for u in range(2)]
        kr = [t(f"kr{u}", [P, NKV * T], BF16) for u in range(2)]
        va = [t(f"va{u}", [P, C, NKV, 32], F32) for u in range(2)]
        p_sb = [t(f"p{j}", [P, XW], F32) for j in range(NP)]
        rowmax = [t(f"rowmax{u}", [P, NH, C], F32) for u in range(2)]
        m_parts = [t(f"m_parts{j}", [GH * C, 2, P], BF16) for j in range(2)]
        o_t = [t(f"o_t{j}", [P, T], F32) for j in range(2)]
        rden = t("rden", [P, C, GH], F32)
        o_n = t("o_n", [P, C, D], F32)
        o_nt = t("o_nt", [P, T], F32)
        s_ps = [ps(f"s{j}", [P, SW], F32) for j in range(2)]
        x_ps = [ps(f"x{j}", [P, XW], F32) for j in range(2)]
        o_ps = ps("o", [P, T], F32)
        misc = ps("misc", [P, T], F32)
        qk_in = [[s(f"qk_in{u}{g}") for g in range(NKV)] for u in range(2)]
        m_in = [[s(f"m_in{u}{g}") for g in range(NKV)] for u in range(2)]
        ones_done, va_done = s("ones_done"), s("va_done")
        s_read, x_read, p_used, x_added = s("s_read"), s("x_read"), s("p_used"), s("x_added")
        s_full, x_full, p_masked = s("s_full"), s("x_full"), s("p_masked")
        max_t, m1_done, m2_done, m_stored = s("max_t"), s("m1_done"), s("m2_done"), s("m_stored")
        o_copied, o_trans, o_rden, o_norm = s("o_copied"), s("o_trans"), s("o_rden"), s("o_norm")
        on_trans, on_copied, proj = s("on_trans"), s("on_copied"), s("proj")
        pool_turn, dve_turn = s("pool_turn"), s("dve_turn")

        def schedule(eng, pair, first, last):
            first()
            with eng.Fori(0, NB // 2 - 1) as i:
                pair((i * 2 + 1, 1, i), (i * 2, 0, i))
                pair((i * 2 + 2, 0, i + 1), (i * 2 + 1, 1, i))
            pair((NB - 1, 1, NB // 2 - 1), (NB - 2, 0, NB // 2 - 1))
            last()

        FIRST, LAST = (0, 0, 0), (NB - 1, 1, NB // 2 - 1)

        with nc.Block() as block:

            @block.sync
            def _(sp):
                def load(n, u, r, g):
                    q = q_dram[n].rearrange("(r h) t -> r h t", h=NH)
                    k = k_dram[n].rearrange("(r h) t -> r h t", h=NKV)
                    rows = PARTS * HD
                    for j in range(PARTS):
                        sp.dma_start(qr[u][j * rows:(j + 1) * rows, g * GH * T:(g + 1) * GH * T].rearrange("r (h t) -> r h t", h=GH),
                                     q[:, g * GH:(g + 1) * GH, :]).then_inc(qk_in[u][g], 16)
                    sp.dma_start(kr[u][0:KQ, g * T:(g + 1) * T], k[:, g, :]).then_inc(qk_in[u][g], 16)

                def maxima(n, u, r, g):
                    sp.wait_ge(m2_done, n * NKV + g + 1)
                    sp.dma_start(m_dram[u].rearrange("a r q -> r a q")[g * GH * C:(g + 1) * GH * C], m_parts[g % 2][:]).then_inc(m_stored, 16)
                    sp.wait_ge(m_stored, (n * NKV + g + 1) * 16)
                    sp.dma_start(qr[u][KQ:KM, g * GH * T:(g + 1) * GH * T],
                                 m_dram[u].rearrange("a r q -> a (r q)")[:, g * GH * T:(g + 1) * GH * T]).then_inc(m_in[u][g], 16)

                def first():
                    sp.wait_ge(ones_done, 1)
                    for u in range(2):
                        for g in range(NKV):
                            load(u, u, 0, g)
                    for g in range(NKV):
                        maxima(*FIRST, g)

                def pair(front, back, more=True):
                    n, u, r = back
                    for g in range(NKV):
                        if more:
                            sp.wait_ge(x_full, (n * NKV + g + 1) * NX)
                            load(n + 2, u, r + 1, g)
                        maxima(*front, g)

                def tail(front, back):
                    pair(front, back, more=not isinstance(back[0], int))

                schedule(sp, tail, first, lambda: None)

            @block.tensor
            def _(pe):
                def scores(n, u, r, g, slot):
                    if slot == 0:
                        pe.wait_ge(qk_in[u][g], r * 64 + 64)
                    for k in S_SLOTS[slot]:
                        c, heads = S_TILES[k]
                        w = (c + 1) * P
                        tile = s_ps[(g * NS + k) % 2]
                        pe.wait_ge(s_read, (n * NKV + g) * NS + k + 1)
                        for x, j in enumerate(heads):
                            q0 = (g * GH + j) * T + c * P
                            pe.matmul(tile[:, x * w:(x + 1) * w], qr[u][0:KQ, q0:q0 + P], kr[u][0:KQ, g * T:g * T + w],
                                      start=True, stop=False)
                            mm = pe.matmul(tile[:, (x + 1) * w - P:(x + 1) * w], h["identb"][:], h["maskb"][:],
                                           start=False, stop=True)
                        mm.then_inc(s_full, 1)

                def less_max(n, u, r, g, k):
                    if k == 0:
                        pe.wait_ge(m_in[u][g], r * 16 + 16)
                    pe.wait_ge(x_read, (n * NKV + g) * NX + k + 1)
                    blocks = [(c, k, at) for c, at in X_HEAD] if k < GH else [(2, j, j * 2 * P) for j in range(GH)]
                    for c, j, at in blocks:
                        q0 = (g * GH + j) * T
                        mm = pe.matmul(x_ps[(g * NX + k) % 2][:, at:at + T - c * P], kr[u][0:KM, g * T + c * P:g * T + (c + 1) * P],
                                       qr[u][0:KM, q0 + c * P:q0 + T], start=True, stop=True)
                    mm.then_inc(x_full, 1)

                def weigh(n, u, r, g, k):
                    q = g * NX + k
                    if g == 0 and k == 0:
                        pe.wait_ge(va_done, n + 1)
                    if k == 0:
                        if not (isinstance(n, int) and n == 0 and g == 0):
                            pe.wait_ge(o_copied, n * NKV + g + 1)
                    pe.wait_ge(p_masked, n * NKV * NX + q + 1)
                    blocks = [(c, k, at) for c, at in X_HEAD] if k < GH else [(2, j, j * 2 * P) for j in range(GH)]
                    for c, j, at in blocks:
                        mm = pe.matmul(o_ps[32 * j:32 * j + 32, c * P:T], va[u][:, c, g, :], p_sb[q % NP][:, at:at + T - c * P],
                                       start=(c == 0), stop=(c == 2))
                    mm.then_inc(p_used, 1)

                def max_rows(front, back, g):
                    n, u, r = front
                    pe.wait_ge(s_read, 2 + (n * NKV + g + 1) * NS)
                    if back is not None:
                        pe.wait_ge(m2_done, n * NKV + g)
                        if g == 0:
                            pe.wait_ge(x_added, n)
                        else:
                            pe.wait_ge(o_norm, back[0] * NKV + g)
                    elif g > 0:
                        pe.wait_ge(m2_done, g)
                    pe.transpose(misc[0:GH * C, 0:P], rowmax[u][:, g * GH:(g + 1) * GH, :].rearrange("p j c -> p (j c)"),
                                 h["ident"][:]).then_inc(max_t, 1)

                def turn_output(front, back, g):
                    n, u, r = back
                    pe.wait_ge(o_copied, 1 + n * NKV + g + 1)
                    if front is not None:
                        pe.wait_ge(m2_done, front[0] * NKV + g + 1)
                    elif g == 0:
                        pe.wait_ge(x_added, n + 1)
                    else:
                        pe.wait_ge(o_norm, n * NKV + g)
                    transpose_chunks(pe, misc, o_t[g % 2], h["ident"]).then_inc(o_trans, 1)

                def project(n, u, r):
                    pe.wait_ge(o_norm, (n + 1) * NKV)
                    for c in range(C):
                        mm = pe.transpose(misc[:, c * P:(c + 1) * P], o_n[:, c, :], h["ident"][:])
                    mm.then_inc(on_trans, 1)
                    pe.wait_ge(on_copied, n + 1)
                    for c in range(C):
                        mm = pe.matmul(misc[:, c * P:(c + 1) * P], o_nt[:, c * P:(c + 1) * P], h["wo"][:], start=True, stop=True)
                    mm.then_inc(proj, 1)

                def pair(front, back):
                    for g in range(NKV):
                        for k in range(NX):
                            if front is not None:
                                scores(*front, g, k)
                            less_max(*back, g, k)
                            q = g * NX + k - LAG
                            if q >= 0:
                                weigh(*back, q // NX, q % NX)
                            if front is not None and k == 0 and g > 0:
                                max_rows(front, back, g - 1)
                            if k == 3 and g > 0:
                                turn_output(front, back, g - 1)
                    for q in range(NKV * NX - LAG, NKV * NX):
                        weigh(*back, q // NX, q % NX)
                    if front is not None:
                        max_rows(front, back, NKV - 1)
                    turn_output(front, back, NKV - 1)
                    project(*back)

                def first():
                    pe.sem_inc(p_used, NP)
                    for g in range(NKV):
                        for k in range(NX):
                            scores(*FIRST, g, k)
                        max_rows(FIRST, None, g)

                schedule(pe, pair, first, lambda: pair(None, LAST))

            @block.scalar
            def _(act):
                a = nc.scalar

                def copy_output(n, u, r, g):
                    act.wait_ge(p_used, NP + (n * NKV + g + 1) * NX)
                    a.activation(o_t[g % 2][:], o_ps[:], ACT.Copy).then_inc(o_copied, 1)

                def pair(front, back):
                    n, u, r = back
                    for g in range(NKV):
                        for k in range(NX):
                            q = g * NX + k
                            act.wait_ge(x_full, n * NKV * NX + q + 1)
                            act.wait_ge(p_used, n * NKV * NX + q + 1)
                            a.activation(p_sb[q % NP][:], x_ps[q % 2][:], ACT.Exp, scale=SCALE).then_inc(x_read, 1)
                            if k == 1 and g > 0:
                                copy_output(*back, g - 1)
                    copy_output(*back, NKV - 1)
                    act.wait_ge(on_trans, n + 1)
                    a.activation(o_nt[:], misc[:], ACT.Copy).then_inc(on_copied, 1)

                def first():
                    act.sem_inc(x_read, 2)
                    act.sem_inc(o_copied, 1)

                schedule(act, pair, first, lambda: pair(None, LAST))

            @block.gpsimd
            def _(pool):
                gp = nc.gpsimd

                def values(n, u, before):
                    if before is not None:
                        pool.wait_ge(p_used, NP + before * NKV * NX)
                    pool.sem_inc(pool_turn, 1)
                    gp.tensor_copy(va[u][:, :, :, 0:HD], v_all[:, n, :].rearrange("p (c g d) -> p c g d", c=C, g=NKV)).then_inc(va_done, 1)

                def pair(front, back):
                    n, u, r = back
                    if front is not None:
                        values(front[0], front[1], n)
                    for g in range(NKV):
                        for k in range(NX):
                            q = g * NX + k
                            pool.wait_ge(x_read, 2 + n * NKV * NX + q + 1)
                            pool.sem_inc(pool_turn, 1)
                            blocks = p_sb[q % NP][:].rearrange("p (b q) -> p b q", q=P)
                            for part in ([blocks[:, 0], blocks[:, 4:8:3]] if k < GH else [blocks[:, 0:8:2]]):
                                sel = gp.affine_select(out=part, in_=part, compare_op=ALU.is_ge, fill=0.0, base=0,
                                                       pattern=[[0, n] for n in part.shape[1:-1]] + [[1, P]], channel_multiplier=-1)
                            sel.then_inc(p_masked, 1)

                def first():
                    for u in range(2):
                        gp.memset(kr[u][:], 1.0)
                        last = gp.memset(va[u][:], 1.0)
                    last.then_inc(ones_done, 1)
                    pool.wait_ge(ones_done, 1)
                    values(0, 0, None)

                schedule(pool, pair, first, lambda: pair(None, LAST))

            @block.vector
            def _(dve):
                v = nc.vector

                def maxima(n, u, r, g, slot):
                    for k in S_SLOTS[slot]:
                        c, heads = S_TILES[k]
                        w, h0 = (c + 1) * P, g * GH + heads[0]
                        dve.wait_ge(s_full, (n * NKV + g) * NS + k + 1)
                        v.tensor_reduce(rowmax[u][:, h0:h0 + len(heads), c],
                                        s_ps[(g * NS + k) % 2][:, 0:len(heads) * w].rearrange("p (j w) -> p j w", w=w),
                                        AX.X, ALU.max).then_inc(s_read, 1)

                def max_parts(n, u, r, g):
                    dve.wait_ge(max_t, n * NKV + g + 1)
                    if not (isinstance(n, int) and n == 0 and g < 2):
                        dve.wait_ge(m_stored, (n * NKV + g - 1) * 16)
                    v.tensor_scalar(m_parts[g % 2][:, 0, :], misc[0:GH * C, 0:P], -1.0, None, ALU.mult).then_inc(m1_done, 1)
                    dve.wait_ge(m1_done, n * NKV + g + 1)
                    v.scalar_tensor_tensor(out=m_parts[g % 2][:, 1, :], in0=misc[0:GH * C, 0:P], scalar=-1.0,
                                           in1=m_parts[g % 2][:, 0, :], op0=ALU.mult, op1=ALU.subtract).then_inc(m2_done, 1)

                def normalise(n, u, r, g):
                    dve.wait_ge(o_trans, n * NKV + g + 1)
                    o = misc[:].rearrange("p (c j e) -> p c j e", c=C, e=32)
                    v.reciprocal(rden[:], o[:, :, :, HD]).then_inc(o_rden, 1)
                    dve.wait_ge(o_rden, n * NKV + g + 1)
                    v.tensor_tensor(o_n[:, :, g * 32:(g + 1) * 32].rearrange("p c (j d) -> p c j d", d=HD), o[:, :, :, 0:HD],
                                    rden[:].unsqueeze(3).to_broadcast([P, C, GH, HD]), ALU.mult).then_inc(o_norm, 1)

                def pair(front, back):
                    n, u, r = back
                    for g in range(NKV):
                        for k in range(NX):
                            if front is not None:
                                maxima(*front, g, k)
                                if k == 1 and g > 0:
                                    max_parts(*front, g - 1)
                            if k == 4 and g > 0:
                                normalise(*back, g - 1)
                    if front is not None:
                        max_parts(*front, NKV - 1)
                    normalise(*back, NKV - 1)
                    dve.wait_ge(proj, n + 1)
                    v.tensor_tensor(xres[:, n, :], misc[:], xres[:, n, :], ALU.add).then_inc(x_added, 1)

                def first():
                    dve.sem_inc(s_read, 2)
                    dve.sem_inc(x_added, 1)
                    for g in range(NKV):
                        for k in range(NX):
                            maxima(*FIRST, g, k)
                        max_parts(*FIRST, g)

                schedule(dve, pair, first, lambda: pair(None, LAST))


def choose_tokens(nc, sb, sem, h, probs, name):
    local = sb(f"{name}_local", [K, NB * E], F32)
    rows = sb(f"{name}_rows", [K, NB * E], U32)
    weight = sb(f"{name}_weight", [K, NB * E], F32)
    with ExitStack() as tmp:
        t = lambda n, s, d: tmp.enter_context(nc.sbuf_tensor(f"{name}_{n}", s, d))
        left = t("left", [P, T], F32)
        vals = t("vals", [P, K], F32)
        found = t("found", [P, K], U32)
        foundf = t("foundf", [P, K], F32)
        foundg = t("foundg", [P, K], F32)
        pps = tmp.enter_context(nc.psum_tensor(f"{name}_pps", [P, T], F32))
        tps = [tmp.enter_context(nc.psum_tensor(f"{name}_tps{j}", [P, P], F32)) for j in range(3)]
        turned, copied, top, indexed, removed, numbers, tables = (
            sem(f"{name}_{n}") for n in ("turned", "copied", "top", "indexed", "removed", "numbers", "tables"))
        with nc.Block() as block:

            @block.tensor
            def _(pe):
                for c in range(C):
                    tr = pe.transpose(pps[:, c * P:(c + 1) * P], probs[:, c, :], h["ident"][:])
                tr.then_inc(turned, 1)
                pe.wait_ge(numbers, 2)
                for j, src in enumerate((foundf, foundg, vals)):
                    tr = pe.transpose(tps[j][:], src[:], h["ident"][:])
                tr.then_inc(turned, 1)

            @block.vector
            def _(dve):
                v = nc.vector
                dve.wait_ge(turned, 1)
                v.tensor_copy(left[:], pps[:]).then_inc(copied, 1)
                dve.wait_ge(copied, 1)
                for r in range(K // 8):
                    eight = slice(r * 8, r * 8 + 8)
                    if r:
                        dve.wait_ge(removed, r)
                    v.max(vals[:, eight], left[:]).then_inc(top, 1)
                    dve.wait_ge(top, r + 1)
                    v.max_index(found[:, eight], vals[:, eight], left[:]).then_inc(indexed, 1)
                    v.match_replace(left[:], vals[:, eight], left[:], -1.0).then_inc(removed, 1)
                dve.wait_ge(indexed, K // 8)
                v.tensor_copy(foundf[:], found[:]).then_inc(numbers, 1)
                dve.wait_ge(numbers, 1)
                v.tensor_scalar(foundg[:], foundf[:], h["rowbase"][:], None, ALU.add).then_inc(numbers, 1)
                dve.wait_ge(turned, 2)
                v.tensor_copy(local[:], tps[0][:]).then_inc(tables, 1)
                v.tensor_copy(rows[:], tps[1][:]).then_inc(tables, 1)
                v.tensor_scalar(weight[:], tps[2][:], 0.5, None, ALU.mult).then_inc(tables, 1)
                dve.wait_ge(tables, 3)
    return local, rows, weight


def experts_layer(nc, sem, h, xres, xn_dram, probs, name, out):
    U = 2
    S = U * E
    RD, RO = 2, 4
    with ExitStack() as tmp:
        t = lambda n, s, d: tmp.enter_context(nc.sbuf_tensor(f"{name}_{n}", s, d))
        ps = lambda n, s, d: tmp.enter_context(nc.psum_tensor(f"{name}_{n}_ps", s, d))
        s = lambda n: sem(f"{name}_{n}")
        local, rows, weight = choose_tokens(nc, lambda n, sh, d: tmp.enter_context(nc.sbuf_tensor(n, sh, d)), sem, h, probs, name)
        row_c = [t(f"row_c{u}", [K, E], U32) for u in range(U)]
        loc_c = [t(f"loc_c{u}", [K, E], F32) for u in range(U)]
        wgt_c = [t(f"wgt_c{u}", [K, E], F32) for u in range(U)]
        x_in = [t(f"x_in{k}", [K, D], F32) for k in range(S)]
        x_t = [t(f"x_t{j}", [D, K], F32) for j in range(RD)]
        hid_t = [t(f"hid_t{j}", [P, FC, K], F32) for j in range(RD)]
        y = [t(f"y{j}", [K, D], F32) for j in range(RD)]
        hot = [t(f"hot{j}", [K, T], F32) for j in range(RO)]
        t_ps = [ps(f"t{j}", [D, K], F32) for j in range(RD)]
        h_ps = [ps(f"h{j}", [P, FC, K], F32) for j in range(RD)]
        y_ps = [ps(f"y{j}", [K, D], F32) for j in range(RD)]
        acc = [ps(f"acc{u}", [P, T], F32) for u in range(U)]
        gathered = [s(f"gathered{k}") for k in range(S)]
        rows_done, cols_done = s("rows_done"), s("cols_done")
        t_full, t_read, h_read, y_read, returned, x_added = (
            s("t_full"), s("t_read"), s("h_read"), s("y_read"), s("returned"), s("x_added"))
        h_full, y_full, hot_done = s("h_full"), s("y_full"), s("hot_done")
        stored, pool_turn, pe_turn = s("stored"), s("pool_turn"), s("pe_turn")
        turns = NB // U
        with nc.Block() as block:

            @block.gpsimd
            def _(pool):
                with pool.Fori(0, turns) as i:
                    for u in range(U):
                        pool.wait_ge(t_full, i * S + (u + 1) * E)
                        pool.sem_inc(pool_turn, 1)
                        nc.gpsimd.tensor_copy(row_c[u][:], rows[:, bass.ds((i * U + u) * E, E)]).then_inc(rows_done, 1)
                        pool.wait_ge(rows_done, i * U + u + 1)
                        pool.sem_inc(pool_turn, 1)
                        for e in range(E):
                            nc.gpsimd.indirect_dma_start(
                                out=x_in[u * E + e][:], out_offset=None, in_=xn_dram,
                                in_offset=bass.IndirectOffsetOnAxis(ap=row_c[u][:, e:e + 1], axis=0)).then_inc(gathered[u * E + e], 16)

            @block.tensor
            def _(pe):
                def transpose(i, k):
                    pe.wait_ge(gathered[k], i * 16 + 16)
                    pe.wait_ge(t_read, i * S + k + 1)
                    pe.transpose(t_ps[k % RD][:], x_in[k][:], h["ident"][:]).then_inc(t_full, 1)

                def up(i, k):
                    pe.wait_ge(t_read, RD + i * S + k + 1)
                    pe.wait_ge(h_read, i * S + k + 1)
                    for f in range(FC):
                        mm = pe.matmul(h_ps[k % RD][:, f, :], h["w1e"][:, k % E, f * P:(f + 1) * P], x_t[k % RD][:], start=True, stop=True)
                    mm.then_inc(h_full, 1)

                def down(i, k):
                    pe.wait_ge(h_read, RD + i * S + k + 1)
                    pe.wait_ge(y_read, i * S + k + 1)
                    for f in range(FC):
                        mm = pe.matmul(y_ps[k % RD][:], hid_t[k % RD][:, f, :], h["w2e"][:, k % E, f, :], start=(f == 0), stop=(f == FC - 1))
                    mm.then_inc(y_full, 1)

                def give_back(i, k):
                    u, e = k // E, k % E
                    pe.wait_ge(y_read, RD + i * S + k + 1)
                    pe.wait_ge(hot_done, i * S + k + 1)
                    if e == 0:
                        pe.wait_ge(x_added, i * U + u + 1)
                    for c in range(C):
                        mm = pe.matmul(acc[u][:, c * P:(c + 1) * P], hot[k % RO][:, c * P:(c + 1) * P], y[k % RD][:],
                                       start=(e == 0 and c == 0), stop=(e == E - 1), skip_group_check=True)
                    mm.then_inc(returned, 1)

                pe.sem_inc(t_full, S)
                pe.sem_inc(returned, RO)
                pe.wait_ge(h["experts_in"], 32)
                with pe.Fori(0, turns) as i:
                    for k in range(S + 3):
                        for stage, work in enumerate((transpose, up, down, give_back)):
                            if 0 <= k - stage < S:
                                work(i, k - stage)

            @block.scalar
            def _(act):
                a = nc.scalar
                act.sem_inc(h_read, RD)
                act.sem_inc(y_read, RD)
                with act.Fori(0, turns) as i:
                    for k in range(S + 1):
                        if k < S:
                            act.wait_ge(h_full, i * S + k + 1)
                            a.activation(hid_t[k % RD][:], h_ps[k % RD][:], ACT.Gelu).then_inc(h_read, 1)
                        if k:
                            j = k - 1
                            act.wait_ge(y_full, i * S + j + 1)
                            if j % E == 0:
                                act.wait_ge(cols_done, (i * U + j // E) * 2 + 2)
                            a.activation(y[j % RD][:], y_ps[j % RD][:], ACT.Copy, scale=wgt_c[j // E][:, j % E:j % E + 1]).then_inc(y_read, 1)

            @block.vector
            def _(dve):
                v = nc.vector

                def add(i, u):
                    dve.wait_ge(returned, RO + i * S + (u + 1) * E)
                    v.tensor_tensor(xres[:, i * U + u, :], acc[u][:], xres[:, i * U + u, :], ALU.add).then_inc(x_added, 1)

                dve.sem_inc(t_read, RD)
                dve.sem_inc(x_added, U)
                with dve.Fori(0, turns) as i:
                    for k in range(S):
                        u, e = k // E, k % E
                        if e == 0:
                            for src, dst in ((local, loc_c), (weight, wgt_c)):
                                v.tensor_copy(dst[u][:], src[:, bass.ds((i * U + u) * E, E)]).then_inc(cols_done, 1)
                        dve.wait_ge(t_full, S + i * S + k + 1)
                        v.tensor_copy(x_t[k % RD][:], t_ps[k % RD][:]).then_inc(t_read, 1)
                        if e == 0:
                            dve.wait_ge(cols_done, (i * U + u) * 2 + 1)
                        dve.wait_ge(returned, i * S + k + 1)
                        v.tensor_scalar(hot[k % RO][:], h["iota"][:], loc_c[u][:, e:e + 1], None, ALU.is_equal).then_inc(hot_done, 1)
                        if k == E + 3:
                            add(i, 0)
                    add(i, U - 1)

            @block.sync
            def _(sp):
                if out is not None:
                    with sp.Fori(0, NB) as n:
                        sp.wait_ge(x_added, U + n + 1)
                        sp.dma_start(out[n].rearrange("(c p) d -> p c d", p=P), xres[:, n, :].rearrange("p (c d) -> p c d", c=C)).then_inc(stored, 16)
                    sp.wait_ge(stored, 16 * NB)


def scan_layer(nc, sem, h, xres, xn_dram, probs):
    with ExitStack() as tmp:
        t = lambda n, s, d: tmp.enter_context(nc.sbuf_tensor(f"sc_{n}", s, d))
        s = lambda n: sem(f"sc_{n}")
        bank = lambda n: tmp.enter_context(nc.psum_tensor(f"sc_{n}_ps", [P, T], F32))
        norm1, norm2 = Norm(nc, "n1", t, s, h, xres), Norm(nc, "n2", t, s, h, xres)
        xhat_t = [t(f"xhat_t{b}", [P, T], F32) for b in range(W)]
        xhat2_t = [t(f"xhat2_t{b}", [P, T], F32) for b in range(W)]
        ts = [t(f"ts{b}", [P, T], F32) for b in range(W)]
        fg = [t(f"fg{b}", [P, T], F32) for b in range(W)]
        lam = [t(f"lam{b}", [P, T], F32) for b in range(W)]
        xt_ps, tf_ps, y_ps = [[bank(f"{n}{b}") for b in range(W)] for n in ("xt", "tf", "y")]
        gate = Gate(nc, t, s, h, probs, bank("gate"))
        xt_full, xt_read, tf_full, tf_read, u_full, lam_full, lam_done = (
            s("xt_full"), s("xt_read"), s("tf_full"), s("tf_read"), s("u_full"), s("lam_full"), s("lam_done"))
        scanned, y_full, x_added, xt2_full, xt2_read, pe_turn = (
            s("scanned"), s("y_full"), s("x_added"), s("xt2_full"), s("xt2_read"), s("pe_turn"))
        xn_out = [s(f"xn_out{b}") for b in range(W)]
        lo = slice(PR, P)
        with nc.Block() as block:

            @block.sync
            def _(sp):
                with sp.Fori(0, TURNS) as i:
                    for b in range(W):
                        sp.wait_ge(norm2.xhat_done, i * W + b + 1)
                        sp.dma_start(xn_dram[bass.ds((i * W + b) * T, T), :].rearrange("(c p) d -> p c d", p=P),
                                     norm2.xhat[b][:].rearrange("p (c d) -> p c d", c=C)).then_inc(xn_out[b], 16)
                for b in range(W):
                    sp.wait_ge(xn_out[b], 16 * TURNS)

            @block.tensor
            def _(pe):
                def turn(head, middle, tail):
                    if middle is not None:
                        for b in range(W):
                            pe.wait_ge(tf_read, middle * W + b + 1)
                            after(pe, x_added, (middle - 1) * W + b + 1)
                            pe.sem_inc(pe_turn, 1)
                            pe.matmul(tf_ps[b][lo, :], h["wlam"][lo, :], fg[b][lo, :], start=True, stop=True).then_inc(lam_full, 1)
                            pe.matmul(y_ps[b][lo, :], h["bmat"][:], ts[b][0:PR, :], start=True, stop=True).then_inc(u_full, 1)
                    if tail is not None:
                        for b in range(W):
                            pe.wait_ge(norm2.xhat_done, tail * W + b + 1)
                            transpose_chunks(pe, xt_ps[b], norm2.xhat[b], h["ident"]).then_inc(xt2_full, 1)
                    if middle is not None:
                        for b in range(W):
                            pe.wait_ge(scanned, middle * W + b + 1)
                            for c in range(C):
                                mm = pe.matmul(y_ps[b][:, c * P:(c + 1) * P], ts[b][:, c * P:(c + 1) * P], h["wcw"][:], start=True, stop=True)
                            mm.then_inc(y_full, 1)
                    if tail is not None:
                        for b in range(W):
                            pe.wait_ge(xt2_read, tail * W + b + 1)
                            gate.tensor(pe, tail, b, xhat2_t[b])
                    if head is not None:
                        for b in range(W):
                            pe.wait_ge(norm1.xhat_done, head * W + b + 1)
                            transpose_chunks(pe, xt_ps[b], norm1.xhat[b], h["ident"]).then_inc(xt_full, 1)
                        for b in range(W):
                            pe.wait_ge(xt_read, head * W + b + 1)
                            if middle is not None:
                                pe.wait_ge(lam_done, middle * W + b + 1)
                            pe.matmul(tf_ps[b][:], h["wtf"][:], xhat_t[b][:], start=True, stop=True).then_inc(tf_full, 1)

                pipeline(pe, turn)

            @block.scalar
            def _(act):
                a = nc.scalar

                def turn(head, middle, tail):
                    if middle is not None:
                        for b in range(W):
                            act.wait_ge(lam_full, middle * W + b + 1)
                            a.activation(lam[b][lo, :], tf_ps[b][lo, :], ACT.Sigmoid).then_inc(lam_done, 1)
                    if tail is not None:
                        for b in range(W):
                            act.wait_ge(xt2_full, tail * W + b + 1)
                            a.activation(xhat2_t[b][:], xt_ps[b][:], ACT.Copy).then_inc(xt2_read, 1)
                    if head is not None:
                        for b in range(W):
                            act.wait_ge(xt_full, head * W + b + 1)
                            a.activation(xhat_t[b][:], xt_ps[b][:], ACT.Copy).then_inc(xt_read, 1)
                        for b in range(W):
                            act.wait_ge(tf_full, head * W + b + 1)
                            a.activation(ts[b][0:PR, :], tf_ps[b][0:PR, :], ACT.Copy)
                            a.activation(fg[b][lo, :], tf_ps[b][lo, :], ACT.Sigmoid).then_inc(tf_read, 1)
                    if tail is not None:
                        gate.scalar(act, tail)

                pipeline(act, turn)

            @block.gpsimd
            def _(pool):
                def turn(head, middle, tail):
                    if tail is not None:
                        norm2.gpsimd(pool, tail)
                    if head is not None:
                        norm1.gpsimd(pool, head)

                pipeline(pool, turn)

            @block.vector
            def _(dve):
                v = nc.vector

                def turn(head, middle, tail):
                    if tail is not None:
                        dve.wait_ge(x_added, tail * W + W)
                        norm2.moments(dve, tail)
                    if head is not None:
                        norm1.moments(dve, head)
                    if tail is not None:
                        for b in range(W):
                            after(dve, xn_out[b], tail * 16)
                        norm2.apply(dve, tail)
                    if middle is not None:
                        for b in range(W):
                            dve.wait_ge(u_full, middle * W + b + 1)
                            dve.wait_ge(lam_done, middle * W + b + 1)
                            v.tensor_tensor_scan(ts[b][lo, :], lam[b][lo, :], y_ps[b][lo, :], 0.0, ALU.mult, ALU.add).then_inc(scanned, 1)
                    if head is not None:
                        norm1.apply(dve, head)
                    if tail is not None:
                        gate.less_max(dve, tail)
                    if middle is not None:
                        for b in range(W):
                            dve.wait_ge(y_full, middle * W + b + 1)
                            v.tensor_tensor(xres[:, middle * W + b, :], y_ps[b][:], xres[:, middle * W + b, :], ALU.add).then_inc(x_added, 1)
                    if tail is not None:
                        gate.normalise(dve, tail)

                pipeline(dve, turn)


def program(nc, w, out):
    with ExitStack() as ctx:
        sb = lambda n, s, d: ctx.enter_context(nc.sbuf_tensor(n, s, d))
        sem = lambda n: ctx.enter_context(nc.semaphore(n))
        dram = lambda n, s, d: nc.dram_tensor(n, s, d, kind="Internal").ap()
        q_dram = dram("q_parts", [NB, PARTS * P, T], BF16)
        k_dram = dram("k_parts", [NB, PARTS * 96, T], BF16)
        xn_dram = dram("xn", [NB * T, D], F32)
        xres = sb("xres", [P, NB, T], F32)
        v_all = sb("v_all", [P, NB, C * 32], F32)
        probs = sb("probs", [P, C, NB * E], F32)
        h = load_constants(nc, w, sb, sem)

        def layer(build, *args, **kw):
            sems = []

            def sem(n):
                sems.append(nc.alloc_semaphore(name=n))
                return sems[-1]

            build(nc, sem, h, xres, *args, **kw)
            nc.clear_and_free_semaphores(sems)
            nc.all_engine_barrier()

        layer(mlp_layer, "qkv", "m1", x_src=w["x"], q_dram=q_dram, k_dram=k_dram, v_all=v_all)
        layer(attention, q_dram, k_dram, v_all)
        layer(mlp_layer, "gate", "m2", xn_dram=xn_dram, probs=probs)
        layer(experts_layer, xn_dram, probs, "e1", None)
        layer(scan_layer, xn_dram, probs)
        layer(experts_layer, xn_dram, probs, "e2", out)


_OUTS = [((16, 512, 128), 'float32')]


def layouts(i):
    import numpy as np

    a = {k: np.ascontiguousarray(v) for k, v in i.items()}
    half = HD // 2
    wq = a["L0_attn_Wq"].reshape(D, NH, HD).transpose(0, 2, 1)
    wk = a["L0_attn_Wk"].reshape(D, NKV, HD).transpose(0, 2, 1)
    swap = np.r_[half:HD, 0:half]
    twice = lambda x: np.concatenate([x, x], 0)
    hm = lambda x: x.reshape(M, HT, 2).transpose(2, 0, 1).reshape(P, HT)
    w = {
        "x": a["L0_attn_x"],
        "win2": np.concatenate([a["L0_ffn_Win"]] * 2, 1), "bin2": twice(a["L0_ffn_bin_"])[:, None],
        "w1p": hm(a["L0_ffn_W1"]), "b1p": hm(a["L0_ffn_b1"]), "w2p": hm(a["L0_ffn_W2"]),
        "b2p": np.concatenate([a["L0_ffn_b2"], np.zeros(M, np.float32)])[:, None],
        "wout2": twice(a["L0_ffn_Wout"]), "bout": a["L0_ffn_bout"][None, :],
        "wq": wq.reshape(D, D), "wqs": wq[:, swap].reshape(D, D), "wk": wk.reshape(D, -1), "wks": wk[:, swap].reshape(D, -1),
        "wv": a["L0_attn_Wv"], "wo": a["L0_attn_Wo"],
        "gw": a["L1_ffn_gate_w"].T, "w1e": a["L1_ffn_w1"].transpose(1, 0, 2),
        "w2e": a["L1_ffn_w2"].reshape(E, FC, P, D).transpose(2, 0, 1, 3),
        "wu": a["L1_attn_W_U"].reshape(D, M * 4), "wv4": a["L1_attn_W_V"].reshape(1, M * 4),
        "wtop": a["L1_attn_W_toP"], "wf": a["L1_attn_W_F"], "wlam": a["L1_attn_W_lam"], "bmat": a["L1_attn_B_mat"],
        "ct": a["L1_attn_C_mat"].T, "wfromp": a["L1_attn_W_fromP"],
    }
    f32 = np.float32
    freq = (f32(1.0) / np.power(f32(10000.0), np.arange(half, dtype=f32) / f32(half))).astype(f32)
    angle = np.arange(T, dtype=f32)[None, :] * freq[:, None]
    cos = np.cos(np.concatenate([angle, angle])).astype(f32)
    sin = np.sin(np.concatenate([angle, angle])).astype(f32)
    sin[:half] *= f32(-1)
    w["cosq"], w["sinq"] = np.repeat(cos, NH, 0), np.repeat(sin, NH, 0)
    w["cosk"], w["sink"] = (np.tile(np.repeat(x, NKV, 0), (W, 1)) for x in (cos, sin))
    at = np.arange(P)
    w["ident"] = np.eye(P, dtype=f32)
    w["pairsum"] = np.tile(np.eye(M, dtype=f32), (2, 2))
    w["mask"] = np.where(at[None, :] > at[:, None], f32(MASKED), f32(0))
    w["iota"] = np.broadcast_to(np.arange(T, dtype=f32), (P, T))
    w["rowbase"] = (at // E * T).astype(f32)[:, None]
    w["mhalf"] = np.full((P, W * C), -0.5, f32)
    return {k: np.ascontiguousarray(v) for k, v in w.items()}


def kernel(**inputs):
    import numpy as _np
    import concourse.bacc as _bacc
    from concourse import mybir as _mybir
    from concourse.bass_utils import run_bass_kernel_spmd as _run

    nc = _bacc.Bacc("TRN2", target_bir_lowering=False, num_devices=1)
    arrays, w = {}, {}
    for name, a in layouts(inputs).items():
        arrays[f"in_{name}_dram"] = a
        w[name] = nc.dram_tensor(f"in_{name}_dram", a.shape, _mybir.dt.from_np(a.dtype), kind="ExternalInput").ap()
    outs = [nc.dram_tensor(f"out_{i}_dram", s, _mybir.dt.from_np(_np.dtype(d)), kind="ExternalOutput").ap()
            for i, (s, d) in enumerate(_OUTS)]
    program(nc, w, outs[0])
    r = _run(nc, [arrays], core_ids=[0])
    return r.results[0]["out_0_dram"]
```

```python
from contextlib import ExitStack

import concourse.bass as bass
from concourse import mybir

F32 = mybir.dt.float32
BF16 = mybir.dt.bfloat16
U32 = mybir.dt.uint32
F32R = mybir.dt.float32r
ALU = mybir.AluOpType
ACT = mybir.ActivationFunctionType
AX = mybir.AxisListType

P = 128
NB = 16
T = 512
D = 128
C = T // P
EPS = 1e-5
NH, NKV = 16, 4
HD = D // NH
GH = NH // NKV
SCALE = HD ** -0.5
PARTS = 3
KQ = PARTS * PARTS * HD
KM = KQ + 2
MASKED = -1.0e38
M = 64
INNER = 16
HT = M * INNER // P
HV = {"qkv": 5, "gate": 3}
E = 8
F = 512
FC = F // P
K = 2 * T // E
PR = 64
W = 2
TURNS = NB // W


PACK = [("ident", P), ("win2", P), ("bin2", 1), ("w1p", HT), ("b1p", HT), ("w2p", HT), ("b2p", 1), ("wout2", D), ("pairsum", P),
        ("mhalf", W * C), ("wu", M * 4), ("wtop", M), ("maskf", P), ("gw", E), ("rowbase", 1),
        ("wq", D), ("wqs", D), ("wk", NKV * HD), ("wks", NKV * HD), ("wv", NKV * HD), ("wo", D)]
PACK_LATE = [("cosq", T), ("sinq", T), ("iota", T)]


def load_constants(nc, w, sb, sem, xres, x_in):
    h = {}
    for n, s, d in [
        ("nb1p", [P, HT], F32), ("w2d", [P, HT, M], F32), ("woutz", [P, W, D], F32), ("gbias", [P, len(HV)], F32),
        ("yrow", [P, D], F32), ("cosk", [W * NKV * HD, T], F32), ("sink", [W * NKV * HD, T], F32),
        ("identb", [P, P], BF16), ("maskb", [P, P], BF16),
        ("wtf", [P, P], F32), ("wlam", [P, PR], F32), ("bmat", [PR, PR], F32), ("wcw", [P, D], F32),
    ]:
        h[n] = sb(n, s, d)
    packs = []
    for name, columns in (("pack", PACK), ("pack_late", PACK_LATE)):
        pack, first = sb(name, [P, sum(c for _, c in columns)], F32), 0
        for n, c in columns:
            h[n] = pack[:, first:first + c]
            first += c
        packs.append((pack[:], w[name]))
    with ExitStack() as tmp:
        t = lambda n, s, d: tmp.enter_context(nc.sbuf_tensor(n, s, d))
        wout2, w2p, b2p, pairsum, wu, wtop = (h[n] for n in ("wout2", "w2p", "b2p", "pairsum", "wu", "wtop"))
        b1w2 = t("b1w2", [P, HT], F32)
        csum = t("csum", [P, len(HV)], F32)
        wv4 = t("wv4", [P, M * 4], F32)
        ct = t("ct", [PR, PR], F32)
        cps = tmp.enter_context(nc.psum_tensor("cps", [P, 512], F32))
        small_in = sem("small_in")
        fold, fold_mm, cast = sem("fold"), sem("fold_mm"), sem("cast")
        loads = [
            packs[0], (h["yrow"][:], w["bout"].to_broadcast([P, D])), (wv4[:], w["wv4"].to_broadcast([P, M * 4])),
            (h["wtf"][:, M:P], w["wf"]), (h["wlam"][PR:P, :], w["wlam"]), (h["bmat"][:], w["bmat"]),
            (ct[:], w["ct"]), (h["wcw"][0:PR, :], w["wfromp"]), packs[1], (h["cosk"][:], w["cosk"]), (h["sink"][:], w["sink"]),
        ]
        with nc.Block() as block:

            @block.sync
            def _(sp):
                def load_x(i):
                    sp.dma_start(xres[:, i * W:(i + 1) * W, :].rearrange("p n (c d) -> p n c d", c=C),
                                 w["x"][i * W:(i + 1) * W].rearrange("n (c p) d -> p n c d", p=P)).then_inc(x_in[i], 16)

                load_x(0)
                for dst, src in loads:
                    sp.dma_start(dst, src).then_inc(small_in, 16)
                for i in range(1, TURNS):
                    load_x(i)
                sp.wait_ge(small_in, 16 * len(loads))

            @block.vector
            def _(dve):
                v = nc.vector
                dve.wait_ge(small_in, 16 * len(loads))
                v.tensor_copy(h["identb"][:], h["ident"][:])
                v.tensor_copy(h["maskb"][:], h["maskf"][:])
                v.tensor_scalar(h["nb1p"][:], h["b1p"][:], -1.0, None, ALU.mult)
                for j in range(HT):
                    v.tensor_scalar(h["w2d"][:, j, :], pairsum[:, 0:M], w2p[:, j:j + 1], 0.5, ALU.mult, ALU.mult)
                v.memset(h["woutz"][:], 0.0).then_inc(cast, 1)
                dve.wait_ge(cast, 1)
                for b in range(W):
                    half = slice(b * M, (b + 1) * M)
                    v.tensor_copy(h["woutz"][half, b, :], wout2[half, :])
                v.tensor_scalar(h["yrow"][:], h["yrow"][:], 0.5, None, ALU.mult)
                v.tensor_tensor(b1w2[:], w2p[:], h["b1p"][:], ALU.mult).then_inc(fold, 1)
                dve.wait_ge(fold, 1)
                for x, made in enumerate(HV.values()):
                    part = v.tensor_reduce(csum[:, x:x + 1], b1w2[:, 0:made], AX.X, ALU.add)
                part.then_inc(fold, 1)
                dve.wait_ge(fold, 2)
                v.tensor_tensor(csum[:], csum[:], b2p[:].to_broadcast([P, len(HV)]), ALU.add).then_inc(fold, 1)
                v.tensor_tensor(wu[:], wu[:], wv4[:], ALU.mult).then_inc(fold, 1)
                dve.wait_ge(fold, 4)
                v.tensor_reduce(h["wtf"][:, 0:M], wu[:].rearrange("p (m a) -> p m a", a=4), AX.X, ALU.add).then_inc(fold, 1)
                dve.wait_ge(fold, 5)
                v.tensor_tensor(h["wtf"][:, 0:M], h["wtf"][:, 0:M], wtop[:], ALU.add)
                dve.wait_ge(fold_mm, 2)
                v.tensor_scalar(h["gbias"][:], cps[:, 0:len(HV)], 0.5, None, ALU.mult)
                v.tensor_copy(h["wcw"][PR:P, :], cps[PR:P, 128:256]).then_inc(cast, 1)
                dve.wait_ge(cast, 2)

            @block.tensor
            def _(pe):
                pe.wait_ge(small_in, 16 * len(loads))
                pe.wait_ge(fold, 3)
                pe.matmul(cps[:, 0:len(HV)], pairsum[:], csum[:], start=True, stop=True).then_inc(fold_mm, 1)
                pe.matmul(cps[PR:P, 128:256], ct[:], h["wcw"][0:PR, :], start=True, stop=True).then_inc(fold_mm, 1)
    return h


class Norm:

    def __init__(self, nc, name, sb, sem, h, xres):
        self.nc, self.h, self.xres = nc, h, xres
        self.stats = sb(name + "_stats", [P, W * C, 6], F32)
        self.mv = sb(name + "_mv", [P, W * C, 2], F32)
        self.vare = sb(name + "_vare", [P, W * C], F32)
        self.rstd = sb(name + "_rstd", [P, W * C], F32)
        self.xhat = [sb(f"{name}_xhat{b}", [P, T], F32) for b in range(W)]
        self.stats_done, self.mv_done = sem(name + "_stats_done"), sem(name + "_mv_done")
        self.var_done, self.rstd_done = sem(name + "_var_done"), sem(name + "_rstd_done")
        self.xhat_done = sem(name + "_xhat_done")
        self.pool_turn, self.dve_turn = sem(name + "_pool_turn"), sem(name + "_dve_turn")

    def moments(self, dve, i):
        v = self.nc.vector
        dve.sem_inc(self.dve_turn, 1)
        for b in range(W):
            for c in range(C):
                s = v.bn_stats(self.stats[:, b * C + c, :], self.xres[:, i * W + b, c * D:(c + 1) * D])
        s.then_inc(self.stats_done, 1)
        dve.wait_ge(self.stats_done, i + 1)
        dve.sem_inc(self.dve_turn, 1)
        for j in range(W * C):
            s = v.bn_aggr(self.mv[:, j, :], self.stats[:, j, :])
        s.then_inc(self.mv_done, 1)
        dve.wait_ge(self.mv_done, i + 1)
        v.tensor_scalar(self.vare[:], self.mv[:, :, 1], EPS, None, ALU.add).then_inc(self.var_done, 1)

    def gpsimd(self, pool, i):
        pool.wait_ge(self.var_done, i + 1)
        pool.sem_inc(self.pool_turn, 1)
        self.nc.gpsimd.tensor_tensor(self.rstd[:], self.vare[:], self.h["mhalf"][:], ALU.pow).then_inc(self.rstd_done, 1)

    def apply(self, dve, i):
        dve.wait_ge(self.rstd_done, i + 1)
        for b in range(W):
            for c in range(C):
                j = b * C + c
                s = self.nc.vector.tensor_scalar(
                    self.xhat[b][:, c * D:(c + 1) * D], self.xres[:, i * W + b, c * D:(c + 1) * D],
                    self.mv[:, j, 0:1], self.rstd[:, j:j + 1], ALU.subtract, ALU.mult)
            s.then_inc(self.xhat_done, 1)


class Gate:

    def __init__(self, nc, sb, sem, h, probs, bank):
        self.nc, self.h, self.probs, self.bank = nc, h, probs, bank
        self.mx = sb("mx", [P, W * C], F32)
        self.ex = sb("ex", [P, W, C, E], F32)
        self.den = sb("den", [P, W * C], F32)
        self.rden = sb("rden", [P, W * C], F32)
        self.scored, self.maxed, self.read = sem("scored"), sem("maxed"), sem("scores_read")
        self.exp_done, self.summed, self.inverted = sem("exp_done"), sem("summed"), sem("inverted")
        self.probs_done = sem("probs_done")

    def tensor(self, pe, i, b, xhat_t):
        if b == 0:
            after(pe, self.read, i)
        for c in range(C):
            at = (b * C + c) * E
            mm = pe.matmul(self.bank[:, at:at + E], xhat_t[:, c * P:(c + 1) * P], self.h["gw"][:], start=True, stop=True)
        mm.then_inc(self.scored, 1)

    def scalar(self, act, i):
        act.wait_ge(self.read, i + 1)
        self.nc.scalar.activation(self.ex[:], self.ex[:], ACT.Exp).then_inc(self.exp_done, 1)

    def less_max(self, dve, i):
        v = self.nc.vector
        sc = self.bank[:, 0:W * C * E].rearrange("p (j e) -> p j e", e=E)
        dve.wait_ge(self.scored, (i + 1) * W)
        v.tensor_reduce(self.mx[:], sc, AX.X, ALU.max).then_inc(self.maxed, 1)
        dve.wait_ge(self.maxed, i + 1)
        v.tensor_tensor(self.ex[:].rearrange("p b c e -> p (b c) e"), sc,
                        self.mx[:].unsqueeze(2).to_broadcast([P, W * C, E]), ALU.subtract).then_inc(self.read, 1)

    def normalise(self, dve, i):
        v = self.nc.vector
        dve.wait_ge(self.exp_done, i + 1)
        v.tensor_reduce(self.den[:], self.ex[:].rearrange("p b c e -> p (b c) e"), AX.X, ALU.add).then_inc(self.summed, 1)
        dve.wait_ge(self.summed, i + 1)
        v.reciprocal(self.rden[:], self.den[:]).then_inc(self.inverted, 1)
        dve.wait_ge(self.inverted, i + 1)
        for b in range(W):
            pr = v.tensor_tensor(self.probs[:, :, bass.ds((i * W + b) * E, E)], self.ex[:, b],
                                 self.rden[:, b * C:(b + 1) * C].unsqueeze(2).to_broadcast([P, C, E]), ALU.mult)
        pr.then_inc(self.probs_done, 1)
        dve.wait_ge(self.probs_done, i + 1)


def transpose_chunks(pe, out, src, ident):
    for c in range(C):
        last = pe.transpose(out[:, c * P:(c + 1) * P], src[:, c * P:(c + 1) * P], ident[:])
    return last


def after(eng, sem, value):
    if not (isinstance(value, int) and value <= 0):
        eng.wait_ge(sem, value)


def is_first(n):
    return isinstance(n, int) and n == 0


def pipeline(eng, turn):
    turn(0, None, None)
    turn(1, 0, None)
    turn(2, 1, 0)
    with eng.Fori(0, TURNS - 3) as r:
        turn(r + 3, r + 2, r + 1)
    turn(None, TURNS - 1, TURNS - 2)
    turn(None, None, TURNS - 1)


def mlp_layer(nc, sem, h, xres, tail_kind, name, x_in=None, q_dram=None, k_dram=None, v_all=None,
              xn_dram=None, probs=None):
    qkv = tail_kind == "qkv"
    made, at = HV[tail_kind], list(HV).index(tail_kind)
    gbias = h["gbias"][:, at:at + 1]
    with ExitStack() as tmp:
        t = lambda n, s, d: tmp.enter_context(nc.sbuf_tensor(f"{name}_{n}", s, d))
        s = lambda n: sem(f"{name}_{n}")
        bank = lambda n: tmp.enter_context(nc.psum_tensor(f"{name}_{n}_ps", [P, T], F32))
        norm1, norm2 = Norm(nc, "n1", t, s, h, xres), Norm(nc, "n2", t, s, h, xres)
        xhat_t = [t(f"xhat_t{b}", [P, T], F32) for b in range(W)]
        xhat2_t = [t(f"xhat2_t{b}", [P, T], F32) for b in range(W)]
        s_in = [t(f"s{b}", [P, T], F32) for b in range(W)]
        hid = [[t(f"hid{b}{j}", [P, T], F32) for j in range(HT)] for b in range(W)]
        g_t = t("g_t", [P, T], F32)
        xt_ps, s_ps = [bank(f"xt{b}") for b in range(W)], [bank(f"s{b}") for b in range(W)]
        g_ps = xt_ps[0]
        r_ps = [bank(f"r{j}") for j in range(4)]
        y_ps = [r_ps[3], r_ps[0]]
        x_loaded = s("x_loaded")
        xt_full, xt_read, s_full, s_read, hid_done, hid_a_done, hid_used = (
            s("xt_full"), s("xt_read"), s("s_full"), s("s_read"), s("hid_done"), s("hid_a_done"), s("hid_used"))
        g_read, bias_added, y_full, x_added, xt2_full, xt2_read = (
            s("g_read"), s("bias_added"), s("y_full"), s("x_added"), s("xt2_full"), s("xt2_read"))
        bias_turn = s("bias_turn")
        if qkv:
            KR = NKV * HD
            TILES = [(f"q{b}", P) for b in range(W)] + [("k", W * KR)]
            NT = len(TILES)
            OUT = [16] * W + [16 * W * PARTS]
            rot = {}
            for n, rows in TILES:
                rot[n] = dict(a=t(f"{n}a", [rows, T], F32), b=t(f"{n}b", [rows, T], F32),
                              parts=t(f"{n}parts", [rows, PARTS, T], BF16))
            rope_full, rope_read, v_full, v_read = s("rope_full"), s("rope_read"), s("v_full"), s("v_read")
            full_done, p1_done, r1_done, p2_done, p3_done = (
                s("full_done"), s("p1_done"), s("r1_done"), s("p2_done"), s("p3_done"))
            parts_out = [s(f"parts_out_{n}") for n, _ in TILES]
            pool_turn = s("rope_pool_turn")
            EARLY, LATE = range(NT), range(NT, NT + 2)
        else:
            gate = Gate(nc, t, s, h, probs, r_ps[2])
            xn_out = [s(f"xn_out{b}") for b in range(W)]
        with nc.Block() as block:

            @block.sync
            def _(sp):
                if x_in is not None:
                    for i in range(TURNS):
                        sp.wait_ge(x_in[i], 16)
                        sp.sem_inc(x_loaded, 1)
                with sp.Fori(0, TURNS) as i:
                    if qkv:
                        for b in range(W):
                            sp.wait_ge(p3_done, i * NT + b + 1)
                            sp.dma_start(q_dram[i * W + b].rearrange("(j p) t -> p j t", p=P),
                                         rot[f"q{b}"]["parts"][:]).then_inc(parts_out[b], 16)
                        sp.wait_ge(p3_done, i * NT + NT)
                        for b in range(W):
                            for copy in range(PARTS):
                                sp.dma_start(k_dram[i * W + b].rearrange("(j c p) t -> c p j t", c=PARTS, p=KR)[copy],
                                             rot["k"]["parts"][b * KR:(b + 1) * KR]).then_inc(parts_out[W], 16)
                    else:
                        for b in range(W):
                            sp.wait_ge(norm2.xhat_done, i * W + b + 1)
                            sp.dma_start(xn_dram[bass.ds((i * W + b) * T, T), :].rearrange("(c p) d -> p c d", p=P),
                                         norm2.xhat[b][:].rearrange("p (c d) -> p c d", c=C)).then_inc(xn_out[b], 16)
                if qkv:
                    for x in range(NT):
                        sp.wait_ge(parts_out[x], OUT[x] * TURNS)
                else:
                    for b in range(W):
                        sp.wait_ge(xn_out[b], 16 * TURNS)

            @block.tensor
            def _(pe):
                def channels(i):
                    for j in range(HT):
                        for b in range(W):
                            if j < made:
                                pe.wait_ge(hid_done, (i * W + b) * made + j + 1)
                            else:
                                pe.wait_ge(hid_a_done, (i * W + b) * (HT - made) + j - made + 1)
                            mm = pe.matmul(g_ps[b * M:(b + 1) * M, :], h["w2d"][:, j, :], hid[b][j][:],
                                           start=(j == 0), stop=(j == HT - 1))
                            if b == W - 1:
                                mm.then_inc(hid_used, 1)

                def output(i, tail):
                    pe.wait_ge(g_read, i + 1)
                    for b in range(W):
                        if qkv and tail is not None:
                            after(pe, rope_read, tail * 2 * NT)
                        for c in range(C):
                            mm = pe.matmul(y_ps[b][:, c * P:(c + 1) * P], g_t[:, c * P:(c + 1) * P], h["woutz"][:, b, :],
                                           start=True, stop=True)
                        mm.then_inc(y_full, 1)

                def queries(i, b):
                    for j, wt in enumerate(("wq", "wqs")):
                        if b == 1 and j == 0:
                            after(pe, v_read, i)
                        if b == 0 and j == 0:
                            pe.wait_ge(x_added, min((i + 2) * W, NB) if isinstance(i, int) else (i + 2) * W)
                        pe.matmul(r_ps[2 * b + j][:], h[wt][:], xhat2_t[b][:], start=True, stop=True).then_inc(rope_full, 1)

                def keys(i):
                    for j, wt in enumerate(("wk", "wks")):
                        pe.wait_ge(rope_read, i * 2 * NT + j + 1)
                        for b in range(W):
                            mm = pe.matmul(r_ps[j][b * KR:(b + 1) * KR, :], h[wt][:], xhat2_t[b][:], start=True, stop=True)
                        mm.then_inc(rope_full, 1)

                def values(i):
                    pe.wait_ge(rope_read, i * 2 * NT + 3)
                    for b in range(W):
                        for c in range(C):
                            mm = pe.matmul(r_ps[2][:, (b * C + c) * KR:(b * C + c + 1) * KR], xhat2_t[b][:, c * P:(c + 1) * P], h["wv"][:],
                                           start=True, stop=True)
                    mm.then_inc(v_full, 1)

                def turn(head, middle, tail):
                    if middle is not None:
                        channels(middle)
                        if not qkv:
                            output(middle, tail)
                    if tail is not None:
                        for b in range(W):
                            pe.wait_ge(norm2.xhat_done, tail * W + b + 1)
                            transpose_chunks(pe, s_ps[b], norm2.xhat[b], h["ident"]).then_inc(xt2_full, 1)
                    if qkv and middle is not None:
                        output(middle, tail)
                    if head is not None:
                        for b in range(W):
                            pe.wait_ge(norm1.xhat_done, head * W + b + 1)
                            if middle is not None:
                                pe.wait_ge(g_read, middle + 1)
                            transpose_chunks(pe, xt_ps[b], norm1.xhat[b], h["ident"]).then_inc(xt_full, 1)
                    if tail is not None:
                        pe.wait_ge(xt2_read, tail * W + W)
                        if qkv:
                            queries(tail, 0)
                    if head is not None:
                        for b in range(W):
                            pe.wait_ge(xt_read, head * W + b + 1)
                            pe.matmul(s_ps[b][:], h["win2"][:], xhat_t[b][:], start=True, stop=True).then_inc(s_full, 1)
                    if tail is not None:
                        if qkv:
                            queries(tail, 1)
                            keys(tail)
                            values(tail)
                        else:
                            for b in range(W):
                                gate.tensor(pe, tail, b, xhat2_t[b])

                pipeline(pe, turn)

            @block.scalar
            def _(act):
                a = nc.scalar

                def split(tail, steps):
                    for x in steps:
                        if x < NT:
                            r = rot[TILES[x][0]]
                            act.wait_ge(full_done, tail * NT + x + 1)
                            a.activation(r["parts"][:, 0, :], r["a"][:], ACT.Copy).then_inc(p1_done, 1)
                        if 1 <= x <= NT:
                            r = rot[TILES[x - 1][0]]
                            act.wait_ge(r1_done, tail * NT + x)
                            a.activation(r["parts"][:, 1, :], r["b"][:], ACT.Copy).then_inc(p2_done, 1)

                def turn(head, middle, tail):
                    if not qkv and tail is not None and not is_first(tail):
                        gate.scalar(act, tail - 1)
                    if middle is not None:
                        act.wait_ge(hid_used, (middle + 1) * HT)
                        a.activation(g_t[:], g_ps[:], ACT.Identity, bias=gbias).then_inc(g_read, 1)
                    if qkv and tail is not None and not is_first(tail):
                        split(tail - 1, LATE)
                    if tail is not None:
                        for b in range(W):
                            act.wait_ge(xt2_full, tail * W + b + 1)
                            a.activation(xhat2_t[b][:], s_ps[b][:], ACT.Copy).then_inc(xt2_read, 1)
                    if head is not None:
                        for b in range(W):
                            act.wait_ge(xt_full, head * W + b + 1)
                            a.activation(xhat_t[b][:], xt_ps[b][:], ACT.Copy).then_inc(xt_read, 1)
                    if head is not None:
                        for b in range(W):
                            act.wait_ge(s_full, head * W + b + 1)
                            a.activation(s_in[b][:], s_ps[b][:], ACT.Identity, bias=h["bin2"][:]).then_inc(s_read, 1)
                        for b in range(W):
                            act.wait_ge(s_read, head * W + b + 1)
                            for j in range(made, HT):
                                a.activation(hid[b][j][:], s_in[b][:], ACT.Relu, bias=h["b1p"][:, j:j + 1],
                                             scale=h["w1p"][:, j:j + 1]).then_inc(hid_a_done, 1)
                    if qkv and tail is not None:
                        split(tail, EARLY)

                pipeline(act, turn)
                if qkv:
                    split(TURNS - 1, LATE)
                else:
                    gate.scalar(act, TURNS - 1)

            @block.gpsimd
            def _(pool):
                g = nc.gpsimd

                def split(tail, steps):
                    for x in steps:
                        if x < NT:
                            r = rot[TILES[x][0]]
                            pool.wait_ge(rope_read, (tail * NT + x) * 2 + 2)
                            pool.sem_inc(pool_turn, 1)
                            g.tensor_tensor(r["a"][:], r["a"][:], r["b"][:], ALU.add).then_inc(full_done, 1)
                        if 1 <= x <= NT:
                            r = rot[TILES[x - 1][0]]
                            pool.wait_ge(full_done, tail * NT + x)
                            pool.wait_ge(p1_done, tail * NT + x)
                            pool.sem_inc(pool_turn, 1)
                            g.tensor_tensor(r["b"][:], r["a"][:], r["parts"][:, 0, :], ALU.subtract).then_inc(r1_done, 1)
                        if x >= 2:
                            r = rot[TILES[x - 2][0]]
                            pool.wait_ge(r1_done, tail * NT + x - 1)
                            pool.wait_ge(p2_done, tail * NT + x - 1)
                            pool.sem_inc(pool_turn, 1)
                            g.tensor_tensor(r["parts"][:, 2, :], r["b"][:], r["parts"][:, 1, :], ALU.subtract).then_inc(p3_done, 1)

                def turn(head, middle, tail):
                    if tail is not None:
                        norm2.gpsimd(pool, tail)
                    if head is not None:
                        norm1.gpsimd(pool, head)
                    if qkv and tail is not None and not is_first(tail):
                        split(tail - 1, LATE)
                    if head is not None:
                        pool.wait_ge(norm1.xhat_done, (head + 1) * W)
                        pool.sem_inc(bias_turn, 1)
                        for b in range(W):
                            x = xres[:, head * W + b, :].rearrange("p (c d) -> p c d", c=C)
                            bias = g.tensor_tensor(x, x, h["yrow"][:].unsqueeze(1).to_broadcast([P, C, D]), ALU.add)
                        bias.then_inc(bias_added, 1)
                    if qkv and tail is not None:
                        split(tail, EARLY)

                pipeline(pool, turn)
                if qkv:
                    split(TURNS - 1, LATE)

            @block.vector
            def _(dve):
                v = nc.vector

                def hidden(i, b):
                    dve.wait_ge(s_read, i * W + b + 1)
                    for j in range(made):
                        after(dve, hid_used, (i - 1) * HT + j + 1)
                        v.tensor_scalar(hid[b][j][:], s_in[b][:], h["w1p"][:, j:j + 1], h["nb1p"][:, j:j + 1],
                                        ALU.mult, ALU.max).then_inc(hid_done, 1)

                def rope(i, x):
                    n, rows = TILES[x]
                    after(dve, parts_out[x], i * OUT[x])
                    for j, (dst, tab) in enumerate((("a", "cos"), ("b", "sin"))):
                        dve.wait_ge(rope_full, (i * NT + x) * 2 + j + 1)
                        v.tensor_tensor(rot[n][dst][:], r_ps[(2 * x + j) % 4][0:rows, :], h[tab + n[0]][:], ALU.mult).then_inc(rope_read, 1)

                def turn(head, middle, tail):
                    if not qkv and middle is not None:
                        for b in range(W):
                            hidden(middle, b)
                    if not qkv and tail is not None and not is_first(tail):
                        gate.less_max(dve, tail - 1)
                    if tail is not None:
                        dve.wait_ge(x_added, tail * W + W)
                        norm2.moments(dve, tail)
                    if head is not None:
                        if x_in is not None:
                            dve.wait_ge(x_loaded, head + 1)
                        norm1.moments(dve, head)
                    if tail is not None:
                        if not qkv:
                            if not is_first(tail):
                                gate.normalise(dve, tail - 1)
                            for b in range(W):
                                after(dve, xn_out[b], tail * 16)
                        norm2.apply(dve, tail)
                    if head is not None:
                        norm1.apply(dve, head)
                    if middle is not None:
                        dve.wait_ge(bias_added, middle + 1)
                        for b in range(W):
                            dve.wait_ge(y_full, middle * W + b + 1)
                            v.tensor_tensor(xres[:, middle * W + b, :], y_ps[b][:], xres[:, middle * W + b, :], ALU.add).then_inc(x_added, 1)
                    if qkv:
                        for x in range(NT):
                            if tail is not None:
                                rope(tail, x)
                            if head is not None and x < W:
                                hidden(head, x)
                        if tail is not None:
                            dve.wait_ge(v_full, tail + 1)
                            v.tensor_copy(v_all[:, bass.ds(tail * W, W), :],
                                          r_ps[2][:, 0:W * C * KR].rearrange("p (b x) -> p b x", b=W)).then_inc(v_read, 1)

                pipeline(dve, turn)
                if not qkv:
                    gate.less_max(dve, TURNS - 1)
                    gate.normalise(dve, TURNS - 1)


SW = 512
XW = 1024
S_TILES = [(0, range(0, 4)), (1, range(0, 2)), (1, range(2, 4))] + [(c, [j]) for c in (2, 3) for j in range(GH)]
S_SLOTS = [range(0, 2), range(2, 4), range(4, 6), range(6, 8), range(8, 11)]
NS = len(S_TILES)
NX = GH + 1
X_HEAD = [(0, 0), (1, 512), (3, 896)]
NP = 4
NG = NKV // 2
DEN = 2 * HD
LAG = 2


def attention(nc, sem, h, xres, q_dram, k_dram, v_all):
    m_dram = nc.dram_tensor("row_max", [2, 2, NH * C, P], BF16, kind="Internal").ap()
    with ExitStack() as tmp:
        t = lambda n, s, d: tmp.enter_context(nc.sbuf_tensor(f"at_{n}", s, d))
        ps = lambda n, s, d: tmp.enter_context(nc.psum_tensor(f"at_{n}_ps", s, d))
        s = lambda n: sem(f"at_{n}")
        qr = [t(f"qr{u}", [P, NH * T], BF16) for u in range(2)]
        kr = [t(f"kr{u}", [P, NKV * T], BF16) for u in range(2)]
        va = [t(f"va{u}", [P, C, NKV, 32], F32) for u in range(2)]
        p_sb = [t(f"p{j}", [P, XW], F32) for j in range(NP)]
        rowmax = [t(f"rowmax{u}", [P, NH, C], F32) for u in range(2)]
        m_parts = [t(f"m_parts{j}", [GH * C, 2, P], BF16) for j in range(2)]
        o_t = [t(f"o_t{j}", [P, T], F32) for j in range(2)]
        rden = t("rden", [P, C, GH, 2], F32)
        o_n = t("o_n", [P, C, D], F32)
        o_nt = t("o_nt", [P, T], F32)
        s_ps = [ps(f"s{j}", [P, SW], F32) for j in range(2)]
        x_ps = [ps(f"x{j}", [P, XW], F32) for j in range(2)]
        first_ring = s_ps + x_ps
        o_ps = ps("o", [P, T], F32)
        misc = ps("misc", [P, T], F32)
        qk_in = [[s(f"qk_in{u}{g}") for g in range(NKV)] for u in range(2)]
        m_in = [[s(f"m_in{u}{g}") for g in range(NKV)] for u in range(2)]
        keys_set, ones_done, va_done = s("keys_set"), s("ones_done"), s("va_done")
        s_read, x_read, p_used, x_added = s("s_read"), s("x_read"), s("p_used"), s("x_added")
        s_full, x_full, p_masked = s("s_full"), s("x_full"), s("p_masked")
        max_t, m1_done, m2_done, m_stored = s("max_t"), s("m1_done"), s("m2_done"), s("m_stored")
        o_copied, o_trans, o_rden, o_norm = s("o_copied"), s("o_trans"), s("o_rden"), s("o_norm")
        on_trans, on_copied, proj = s("on_trans"), s("on_copied"), s("proj")
        pool_turn, dve_turn = s("pool_turn"), s("dve_turn")

        def schedule(eng, first, step, flush):
            first()
            step((0, 0, 0), (1, 1, 0))
            with eng.Fori(0, NB // 2 - 2) as i:
                step((i * 2 + 1, 1, i), (i * 2 + 2, 0, i + 1))
                step((i * 2 + 2, 0, i + 1), (i * 2 + 3, 1, i + 1))
            for n in range(NB - 3, NB):
                step((n, n % 2, n // 2), (n + 1, (n + 1) % 2, (n + 1) // 2) if n + 1 < NB else None)
            flush()

        FIRST, LAST = (0, 0, 0), (NB - 1, 1, NB // 2 - 1)
        SLOTS = [(g, k) for g in range(NKV) for k in range(NX)]
        ROWS_AT = 1
        LAST_OUT_AT, FIRST_OUT_AT = (0, NX - 1), (2, NX - 1)
        TURN_AT, PROJECT_AT = (1, 2), (2, 2)
        with nc.Block() as block:

            @block.sync
            def _(sp):
                def load(n, u, r, g):
                    q = q_dram[n].rearrange("(r h) t -> r h t", h=NH)
                    k = k_dram[n].rearrange("(r h) t -> r h t", h=NKV)
                    rows = PARTS * HD
                    for j in range(PARTS):
                        sp.dma_start(qr[u][j * rows:(j + 1) * rows, g * GH * T:(g + 1) * GH * T].rearrange("r (h t) -> r h t", h=GH),
                                     q[:, g * GH:(g + 1) * GH, :]).then_inc(qk_in[u][g], 16)
                    sp.dma_start(kr[u][0:KQ, g * T:(g + 1) * T], k[:, g, :]).then_inc(qk_in[u][g], 16)

                def maxima(n, u, r, g):
                    sp.wait_ge(m2_done, n * NKV + g + 1)
                    sp.dma_start(m_dram[u].rearrange("a r q -> r a q")[g * GH * C:(g + 1) * GH * C], m_parts[g % 2][:]).then_inc(m_stored, 16)
                    sp.wait_ge(m_stored, (n * NKV + g + 1) * 16)
                    sp.dma_start(qr[u][KQ:KM, g * GH * T:(g + 1) * GH * T],
                                 m_dram[u].rearrange("a r q -> a (r q)")[:, g * GH * T:(g + 1) * GH * T]).then_inc(m_in[u][g], 16)

                def first():
                    for u in range(2):
                        sp.wait_ge(keys_set, u + 1)
                        for g in range(NKV):
                            load(u, u, 0, g)
                    for g in range(NKV - 1):
                        maxima(*FIRST, g)

                def step(batch, ahead):
                    n, u, r = batch
                    for g in range(NKV):
                        if g == 0:
                            maxima(*batch, NKV - 1)
                        elif ahead is not None:
                            maxima(*ahead, g - 1)
                        if not (isinstance(n, int) and n + 2 >= NB):
                            sp.wait_ge(x_full, (n * NKV + g + 1) * NX)
                            load(n + 2, u, r + 1, g)

                schedule(sp, first, step, lambda: None)

            @block.tensor
            def _(pe):
                def scores(n, u, r, g, tiles, ring=s_ps):
                    for k in tiles:
                        if k == 0:
                            pe.wait_ge(qk_in[u][g], r * 64 + 64)
                        c, heads = S_TILES[k]
                        w = (c + 1) * P
                        tile = ring[(g * NS + k) % len(ring)]
                        after(pe, s_read, 2 + (n * NKV + g) * NS + k + 1 - len(ring))
                        for x, j in enumerate(heads):
                            q0 = (g * GH + j) * T + c * P
                            pe.matmul(tile[:, x * w:(x + 1) * w], qr[u][0:KQ, q0:q0 + P], kr[u][0:KQ, g * T:g * T + w],
                                      start=True, stop=False)
                            mm = pe.matmul(tile[:, (x + 1) * w - P:(x + 1) * w], h["identb"][:], h["maskb"][:],
                                           start=False, stop=True)
                        mm.then_inc(s_full, 1)

                def less_max(n, u, r, g, k):
                    if k == 0:
                        pe.wait_ge(m_in[u][g], r * 16 + 16)
                    pe.wait_ge(x_read, (n * NKV + g) * NX + k + 1)
                    blocks = [(c, k, at) for c, at in X_HEAD] if k < GH else [(2, j, j * 2 * P) for j in range(GH)]
                    for c, j, at in blocks:
                        q0 = (g * GH + j) * T
                        mm = pe.matmul(x_ps[(g * NX + k) % 2][:, at:at + T - c * P], kr[u][0:KM, g * T + c * P:g * T + (c + 1) * P],
                                       qr[u][0:KM, q0 + c * P:q0 + T], start=True, stop=True)
                    mm.then_inc(x_full, 1)

                def weigh(n, u, r, g, k):
                    q = g * NX + k
                    if g == 0 and k == 0:
                        pe.wait_ge(va_done, n + 1)
                    if k == 0:
                        if g % 2 == 0 and not (is_first(n) and g == 0):
                            pe.wait_ge(o_copied, n * NG + g // 2 + 1)
                    pe.wait_ge(p_masked, n * NKV * NX + q + 1)
                    blocks = [(c, k, at) for c, at in X_HEAD] if k < GH else [(2, j, j * 2 * P) for j in range(GH)]
                    for c, j, at in blocks:
                        mm = pe.matmul(o_ps[32 * j:32 * j + 32, c * P:T], va[u][:, c, g, :], p_sb[q % NP][:, at:at + T - c * P],
                                       start=(c == 0 and g % 2 == 0), stop=(c == 2 and g % 2 == 1))
                    mm.then_inc(p_used, 1)

                def max_rows(batch, g, before):
                    n, u, r = batch
                    pe.wait_ge(s_read, 2 + (n * NKV + g + 1) * NS)
                    after(pe, m2_done, n * NKV + g)
                    after(pe, o_norm, before)
                    pe.transpose(misc[0:GH * C, 0:P], rowmax[u][:, g * GH:(g + 1) * GH, :].rearrange("p j c -> p (j c)"),
                                 h["ident"][:]).then_inc(max_t, 1)

                def turn_output(n, p):
                    pe.wait_ge(o_copied, 1 + n * NG + p + 1)
                    transpose_chunks(pe, misc, o_t[p], h["ident"]).then_inc(o_trans, 1)

                def turn_normal(n):
                    pe.wait_ge(o_norm, (n + 1) * NG)
                    for c in range(C):
                        mm = pe.transpose(misc[:, c * P:(c + 1) * P], o_n[:, c, :], h["ident"][:])
                    mm.then_inc(on_trans, 1)

                def project(n):
                    pe.wait_ge(on_copied, n + 1)
                    for c in range(C):
                        mm = pe.matmul(misc[:, c * P:(c + 1) * P], o_nt[:, c * P:(c + 1) * P], h["wo"][:], start=True, stop=True)
                    mm.then_inc(proj, 1)

                def step(batch, ahead):
                    n, u, r = batch
                    for at, (g, k) in enumerate(SLOTS):
                        rows = n * NKV + NKV + g
                        if ahead is None:
                            rows = NB * NKV
                        if ahead is not None:
                            scores(*ahead, g, S_SLOTS[k][:1])
                        less_max(*batch, g, k)
                        if ahead is not None:
                            scores(*ahead, g, S_SLOTS[k][1:2])
                        if at >= LAG:
                            weigh(*batch, *SLOTS[at - LAG])
                        elif not is_first(n):
                            weigh(n - 1, 1 - u, None, *SLOTS[at - LAG])
                        if ahead is not None:
                            scores(*ahead, g, S_SLOTS[k][2:])
                        if k == ROWS_AT:
                            if g == PROJECT_AT[0] and not is_first(n):
                                pe.wait_ge(on_copied, n)
                            if g == 0:
                                max_rows(batch, NKV - 1, n * NG - 1)
                            elif ahead is not None:
                                max_rows(ahead, g - 1, n * NG + (1 if g == NKV - 1 else 0))
                        if not is_first(n) and (g, k) == TURN_AT:
                            pe.wait_ge(m2_done, rows)
                            turn_normal(n - 1)
                        if not is_first(n) and (g, k) == PROJECT_AT:
                            pe.wait_ge(m2_done, rows)
                            project(n - 1)
                        if (g, k) == LAST_OUT_AT and not is_first(n):
                            pe.wait_ge(m2_done, rows)
                            turn_output(n - 1, 1)
                        if (g, k) == FIRST_OUT_AT:
                            if is_first(n):
                                pe.wait_ge(m2_done, rows)
                            else:
                                pe.wait_ge(x_added, 1 + n)
                            turn_output(n, 0)

                def first():
                    pe.sem_inc(p_used, NP)
                    for g in range(NKV):
                        scores(*FIRST, g, range(NS), first_ring)
                        if g < NKV - 1:
                            max_rows(FIRST, g, 0)
                    pe.wait_ge(s_read, 2 + NKV * NS)

                def flush():
                    n, u, r = LAST
                    for at in range(-LAG, 0):
                        weigh(*LAST, *SLOTS[at])
                    pe.wait_ge(o_norm, n * NG + 1)
                    turn_output(n, 1)
                    turn_normal(n)
                    project(n)

                schedule(pe, first, step, flush)

            @block.scalar
            def _(act):
                a = nc.scalar

                def copy_output(n, p):
                    act.wait_ge(p_used, NP + (n * NKV + (p + 1) * 2) * NX)
                    a.activation(o_t[p][:], o_ps[:], ACT.Copy).then_inc(o_copied, 1)

                def copy_normal(n):
                    act.wait_ge(on_trans, n + 1)
                    a.activation(o_nt[:], misc[:], ACT.Copy).then_inc(on_copied, 1)

                def step(batch, ahead):
                    n, u, r = batch
                    for q, (g, k) in enumerate(SLOTS):
                        act.wait_ge(x_full, n * NKV * NX + q + 1)
                        act.wait_ge(p_used, n * NKV * NX + q + 1)
                        a.activation(p_sb[q % NP][:], x_ps[q % 2][:], ACT.Exp, scale=SCALE).then_inc(x_read, 1)
                        if (g, k) == (2, 1):
                            copy_output(n, 0)
                        if (g, k) == (0, 1) and not is_first(n):
                            copy_output(n - 1, 1)
                        if not is_first(n) and (g, k - 1) == TURN_AT:
                            copy_normal(n - 1)

                def first():
                    act.sem_inc(x_read, 2)
                    act.sem_inc(o_copied, 1)

                def flush():
                    copy_output(LAST[0], 1)
                    copy_normal(LAST[0])

                schedule(act, first, step, flush)

            @block.gpsimd
            def _(pool):
                gp = nc.gpsimd

                def values(n, u, before):
                    if not is_first(n):
                        pool.wait_ge(p_used, NP + before * NKV * NX)
                    pool.sem_inc(pool_turn, 1)
                    of_heads = v_all[:, n, :].rearrange("p (c g d) -> p c g d", c=C, g=NKV)
                    for x in range(2):
                        copy = gp.tensor_copy(va[u][:, :, x::2, x * HD:(x + 1) * HD], of_heads[:, :, x::2, :])
                    copy.then_inc(va_done, 1)

                def step(batch, ahead):
                    n, u, r = batch
                    for q, (g, k) in enumerate(SLOTS):
                        pool.wait_ge(x_read, 2 + n * NKV * NX + q + 1)
                        pool.sem_inc(pool_turn, 1)
                        blocks = p_sb[q % NP][:].rearrange("p (b q) -> p b q", q=P)
                        for part in ([blocks[:, 0], blocks[:, 4:8:3]] if k < GH else [blocks[:, 0:8:2]]):
                            sel = gp.affine_select(out=part, in_=part, compare_op=ALU.is_ge, fill=0.0, base=0,
                                                   pattern=[[0, n] for n in part.shape[1:-1]] + [[1, P]], channel_multiplier=-1)
                        sel.then_inc(p_masked, 1)
                        if (g, k) == (1, 0) and ahead is not None:
                            values(ahead[0], ahead[1], n)

                def first():
                    for u in range(2):
                        zeros = gp.memset(va[u][:], 0.0)
                    zeros.then_inc(ones_done, 1)
                    pool.wait_ge(ones_done, 1)
                    for u in range(2):
                        for x in range(2):
                            ones = gp.memset(va[u][:, :, x::2, DEN + x], 1.0)
                    ones.then_inc(ones_done, 1)
                    pool.wait_ge(ones_done, 2)
                    values(0, 0, 0)

                schedule(pool, first, step, lambda: None)

            @block.vector
            def _(dve):
                v = nc.vector

                def maxima(n, u, r, g, slot, ring=s_ps):
                    for k in S_SLOTS[slot]:
                        c, heads = S_TILES[k]
                        w, h0 = (c + 1) * P, g * GH + heads[0]
                        dve.wait_ge(s_full, (n * NKV + g) * NS + k + 1)
                        v.tensor_reduce(rowmax[u][:, h0:h0 + len(heads), c],
                                        ring[(g * NS + k) % len(ring)][:, 0:len(heads) * w].rearrange("p (j w) -> p j w", w=w),
                                        AX.X, ALU.max).then_inc(s_read, 1)

                def max_parts(n, u, r, g):
                    dve.wait_ge(max_t, n * NKV + g + 1)
                    if not (isinstance(n, int) and n == 0 and g < 2):
                        dve.wait_ge(m_stored, (n * NKV + g - 1) * 16)
                    v.tensor_scalar(m_parts[g % 2][:, 0, :], misc[0:GH * C, 0:P], -1.0, None, ALU.mult).then_inc(m1_done, 1)
                    dve.wait_ge(m1_done, n * NKV + g + 1)
                    v.scalar_tensor_tensor(out=m_parts[g % 2][:, 1, :], in0=misc[0:GH * C, 0:P], scalar=-1.0,
                                           in1=m_parts[g % 2][:, 0, :], op0=ALU.mult, op1=ALU.subtract).then_inc(m2_done, 1)

                def normalise(n, p):
                    dve.wait_ge(o_trans, n * NG + p + 1)
                    o = misc[:].rearrange("p (c j e) -> p c j e", c=C, e=32)
                    v.reciprocal(rden[:], o[:, :, :, DEN:DEN + 2]).then_inc(o_rden, 1)
                    dve.wait_ge(o_rden, n * NG + p + 1)
                    for x in range(2):
                        first = (2 * p + x) * GH * HD
                        norm = v.tensor_tensor(o_n[:, :, first:first + GH * HD].rearrange("p c (j d) -> p c j d", d=HD),
                                               o[:, :, :, x * HD:(x + 1) * HD],
                                               rden[:, :, :, x].unsqueeze(3).to_broadcast([P, C, GH, HD]), ALU.mult)
                    norm.then_inc(o_norm, 1)

                def add_output(n):
                    dve.wait_ge(proj, n + 1)
                    v.tensor_tensor(xres[:, n, :], misc[:], xres[:, n, :], ALU.add).then_inc(x_added, 1)

                def step(batch, ahead):
                    n, u, r = batch
                    for g, k in SLOTS:
                        if (g, k) == (LAST_OUT_AT[0] + 1, 0) and not is_first(n):
                            normalise(n - 1, 1)
                        if (g, k) == (FIRST_OUT_AT[0] + 1, 0):
                            normalise(n, 0)
                        if not is_first(n) and (g, k - 1) == PROJECT_AT:
                            add_output(n - 1)
                        if ahead is not None:
                            maxima(*ahead, g, k)
                        if k == ROWS_AT + 1:
                            if g == 0:
                                max_parts(*batch, NKV - 1)
                            elif ahead is not None:
                                max_parts(*ahead, g - 1)

                def first():
                    dve.sem_inc(s_read, 2)
                    dve.sem_inc(x_added, 1)
                    for u in range(2):
                        v.memset(kr[u][:], 1.0).then_inc(keys_set, 1)
                    for g in range(NKV):
                        for k in range(NX):
                            maxima(*FIRST, g, k, first_ring)
                        if g < NKV - 1:
                            max_parts(*FIRST, g)

                def flush():
                    normalise(LAST[0], 1)
                    add_output(LAST[0])

                schedule(dve, first, step, flush)


def split_weights(nc, block, sb, sem, h, weights):
    raw = [sb(f"raw{j}", [P, E, F], F32) for j in range(len(weights))]
    loaded = [[sem(f"raw{j}{e}_in") for e in range(E)] for j in range(len(weights))]
    hi_done, lo_done = sem("w_hi_done"), sem("w_lo_done")
    tiles = [(raw[j][:, e], h[f"w{j + 1}_hi"][:, e], h[f"w{j + 1}_lo"][:, e], w[:, e], loaded[j][e])
             for j, w in enumerate(weights) for e in range(E)]

    @block.sync
    def _(sp):
        for x, hi, lo, w, into in tiles:
            sp.dma_start(x, w).then_inc(into, 16)

    @block.scalar
    def _(act):
        for x, hi, lo, w, into in tiles:
            act.wait_ge(into, 16)
            nc.scalar.activation(hi, x, ACT.Copy).then_inc(hi_done, 1)

    @block.gpsimd
    def _(pool):
        for n, (x, hi, lo, w, into) in enumerate(tiles):
            pool.wait_ge(hi_done, n + 1)
            nc.gpsimd.tensor_tensor(lo, x, hi.bitcast(F32), ALU.subtract).then_inc(lo_done, 1)
        pool.wait_ge(lo_done, len(tiles))


def choose_tokens(nc, sb, sem, h, probs, name, weights=None):
    local = sb(f"{name}_local", [K, NB * E], F32)
    rows = sb(f"{name}_rows", [K, NB * E], U32)
    weight = sb(f"{name}_weight", [K, NB * E], F32)
    with ExitStack() as tmp:
        t = lambda n, s, d: tmp.enter_context(nc.sbuf_tensor(f"{name}_{n}", s, d))
        left = t("left", [P, T], F32)
        vals = t("vals", [P, K], F32)
        found = t("found", [P, K], U32)
        foundf = t("foundf", [P, K], F32)
        foundg = t("foundg", [P, K], F32)
        pps = tmp.enter_context(nc.psum_tensor(f"{name}_pps", [P, T], F32))
        tps = [tmp.enter_context(nc.psum_tensor(f"{name}_tps{j}", [P, P], F32)) for j in range(3)]
        turned, copied, top, indexed, removed, numbers, tables = (
            sem(f"{name}_{n}") for n in ("turned", "copied", "top", "indexed", "removed", "numbers", "tables"))
        with nc.Block() as block:
            if weights is not None:
                split_weights(nc, block, t, sem, h, weights)

            @block.tensor
            def _(pe):
                for c in range(C):
                    tr = pe.transpose(pps[:, c * P:(c + 1) * P], probs[:, c, :], h["ident"][:])
                tr.then_inc(turned, 1)
                pe.wait_ge(numbers, 2)
                for j, src in enumerate((foundf, foundg, vals)):
                    tr = pe.transpose(tps[j][:], src[:], h["ident"][:])
                tr.then_inc(turned, 1)

            @block.vector
            def _(dve):
                v = nc.vector
                dve.wait_ge(turned, 1)
                v.tensor_copy(left[:], pps[:]).then_inc(copied, 1)
                dve.wait_ge(copied, 1)
                for r in range(K // 8):
                    eight = slice(r * 8, r * 8 + 8)
                    if r:
                        dve.wait_ge(removed, r)
                    v.max(vals[:, eight], left[:]).then_inc(top, 1)
                    dve.wait_ge(top, r + 1)
                    v.max_index(found[:, eight], vals[:, eight], left[:]).then_inc(indexed, 1)
                    v.match_replace(left[:], vals[:, eight], left[:], -1.0).then_inc(removed, 1)
                dve.wait_ge(indexed, K // 8)
                v.tensor_copy(foundf[:], found[:]).then_inc(numbers, 1)
                dve.wait_ge(numbers, 1)
                v.tensor_scalar(foundg[:], foundf[:], h["rowbase"][:], None, ALU.add).then_inc(numbers, 1)
                dve.wait_ge(turned, 2)
                v.tensor_copy(local[:], tps[0][:]).then_inc(tables, 1)
                v.tensor_copy(rows[:], tps[1][:]).then_inc(tables, 1)
                v.tensor_scalar(weight[:], tps[2][:], 0.5, None, ALU.mult).then_inc(tables, 1)
                dve.wait_ge(tables, 3)
    return local, rows, weight


def experts_layer(nc, sem, h, xres, xn_dram, probs, name, out, weights=None):
    U = 2
    S = E
    TU = NB // U
    HC = FC // 2
    N = U * K
    with ExitStack() as tmp:
        t = lambda n, s, d: tmp.enter_context(nc.sbuf_tensor(f"{name}_{n}", s, d))
        ps = lambda n, s: tmp.enter_context(nc.psum_tensor(f"{name}_{n}_ps", s, F32))
        s = lambda n: sem(f"{name}_{n}")
        two = lambda n, sh, d=F32R: [t(f"{n}{j}", sh, d) for j in range(2)]
        local, rows, weight = choose_tokens(nc, lambda n, sh, d: tmp.enter_context(nc.sbuf_tensor(n, sh, d)), sem, h, probs, name, weights)
        row_c = [t(f"row_c{k}", [K, U], U32) for k in range(S)]
        loc_c, wgt_c = two("loc_c", [K, U], F32), two("wgt_c", [K, U], F32)
        x_in = [[t(f"x_in{k}{u}", [K, D], F32) for u in range(U)] for k in range(S)]
        x_hi, x_lo = two("x_hi", [D, N]), two("x_lo", [D, N])
        hid = two("hid", [P, HC, N], F32)
        hid_hi, hid_lo = two("hid_hi", [P, FC, N]), two("hid_lo", [P, FC, N])
        y_t = two("y_t", [D, N], F32)
        y_hi, y_lo = two("y_hi", [K, U, D]), two("y_lo", [K, U, D])
        hot = two("hot", [K, U, T])
        acc_sb = [t(f"acc_sb{u}", [D, T], F32) for u in range(U)]
        t_ps, yt_ps, y_ps, o_ps = ps("t", [D, N]), ps("yt", [D, N]), ps("y", [K, U, D]), ps("o", [P, T])
        h_ps = [ps(f"h{j}", [P, HC, N]) for j in range(2)]
        acc = [ps(f"acc{u}", [D, T]) for u in range(U)]
        gathered = [[s(f"gathered{k}{u}") for u in range(U)] for k in range(S)]
        rows_done, cols_done, hot_done = s("rows_done"), s("cols_done"), s("hot_done")
        t_full, xh_done, xl_done, h_full, gelu_done, hl_done = (
            s("t_full"), s("xh_done"), s("xl_done"), s("h_full"), s("gelu_done"), s("hl_done"))
        yt_full, yt_read, y_full, yh_done, yl_done, returned = (
            s("yt_full"), s("yt_read"), s("y_full"), s("yh_done"), s("yl_done"), s("returned"))
        acc_read, o_full, x_added, stored, pool_turn = (
            s("acc_read"), s("o_full"), s("x_added"), s("stored"), s("pool_turn"))
        whole = lambda a: a.bitcast(F32)

        def slots(eng, slot):
            for k in range(S):
                slot(0, k)
            with eng.Fori(0, TU - 1) as r:
                for k in range(S):
                    slot(r + 1, k)
            for k in range(S - 1):
                slot(TU, k)

        def step_at(i, k, stage):
            if k < stage:
                i, k = i - 1, k + S
            k -= stage
            if isinstance(i, int) and not 0 <= i < TU:
                return None
            return i, k, i * S + k

        def run(i, k, *stages):
            for stage, work in stages:
                at = step_at(i, k, stage)
                if at is not None:
                    work(*at)

        SUMS_AT = S + 3
        TURN_AT = [SUMS_AT + 2 + u for u in range(U)]

        def turn_at(i, k, slot):
            if slot - S != k or (isinstance(i, int) and i == 0):
                return None
            return i - 1

        with nc.Block() as block:

            @block.gpsimd
            def _(pool):
                def gather(i):
                    for k in range(S):
                        after(pool, t_full, (i - 1) * S + k + 1)
                        pool.sem_inc(pool_turn, 1)
                        of_turn = rows[:, bass.ds(i * U * E, U * E)].rearrange("p (u e) -> p e u", u=U)
                        nc.gpsimd.tensor_copy(row_c[k][:], of_turn[:, k]).then_inc(rows_done, 1)
                        pool.wait_ge(rows_done, i * S + k + 1)
                        pool.sem_inc(pool_turn, 1)
                        for u in range(U):
                            nc.gpsimd.indirect_dma_start(
                                out=x_in[k][u][:], out_offset=None, in_=xn_dram,
                                in_offset=bass.IndirectOffsetOnAxis(ap=row_c[k][:, u:u + 1], axis=0)).then_inc(gathered[k][u], 16)

                gather(0)
                with pool.Fori(0, TU - 1) as r:
                    gather(r + 1)

            @block.tensor
            def _(pe):
                def transpose(i, k, q):
                    after(pe, xl_done, q)
                    for u in range(U):
                        pe.wait_ge(gathered[k][u], i * 16 + 16)
                        mm = pe.transpose(t_ps[:, u * K:(u + 1) * K], x_in[k][u][:], h["ident"][:])
                    mm.then_inc(t_full, 1)

                def up(i, k, q):
                    pe.wait_ge(xl_done, q + 1)
                    pairs = [(h["w1_hi"], x_hi), (h["w1_hi"], x_lo), (h["w1_lo"], x_hi)]
                    for half in range(2):
                        after(pe, gelu_done, (q - 1) * 2 + half + 1)
                        for f in range(HC):
                            at = (half * HC + f) * P
                            for j, (w1, x) in enumerate(pairs):
                                mm = pe.matmul(h_ps[half][:, f, :], w1[:, k, at:at + P], x[k % 2][:], start=(j == 0), stop=(j == len(pairs) - 1))
                        mm.then_inc(h_full, 1)

                def down(i, k, q):
                    after(pe, yt_read, q)
                    pairs = [(h["w2_hi"], hid_hi), (h["w2_hi"], hid_lo), (h["w2_lo"], hid_hi)]
                    for f in range(FC):
                        if f % HC == 0:
                            pe.wait_ge(hl_done, q * 2 + f // HC + 1)
                        for j, (w2, x) in enumerate(pairs):
                            mm = pe.matmul(yt_ps[:], w2[:, k, f * D:(f + 1) * D], x[k % 2][:, f, :], start=(f == 0 and j == 0),
                                           stop=(f == FC - 1 and j == len(pairs) - 1))
                    mm.then_inc(yt_full, 1)

                def transpose_back(i, k, q):
                    pe.wait_ge(yt_read, q + 1)
                    after(pe, yl_done, q)
                    for u in range(U):
                        mm = pe.transpose(y_ps[:, u, :], y_t[k % 2][:, u * K:(u + 1) * K], h["ident"][:])
                    mm.then_inc(y_full, 1)

                def give_back(i, k, q):
                    pe.wait_ge(yl_done, q + 1)
                    pe.wait_ge(hot_done, q + 1)
                    if k == 0:
                        after(pe, acc_read, i * U)
                    for u in range(U):
                        pe.matmul(acc[u][:], y_hi[k % 2][:, u, :], hot[k % 2][:, u, :], start=(k == 0), stop=False, skip_group_check=True)
                        mm = pe.matmul(acc[u][:], y_lo[k % 2][:, u, :], hot[k % 2][:, u, :], start=False, stop=(k == S - 1),
                                       skip_group_check=True)
                    mm.then_inc(returned, 1)

                def slot(i, k):
                    run(i, k, (0, transpose), (1, up), (2, down), (3, transpose_back), (4, give_back))
                    for u in range(U):
                        turn = turn_at(i, k, TURN_AT[u])
                        if turn is not None:
                            pe.wait_ge(acc_read, turn * U + u + 1)
                            after(pe, x_added, turn * U + u)
                            transpose_chunks(pe, o_ps, acc_sb[u], h["ident"]).then_inc(o_full, 1)

                slots(pe, slot)

            @block.scalar
            def _(act):
                a = nc.scalar

                def split_x(i, k, q):
                    act.wait_ge(t_full, q + 1)
                    a.activation(x_hi[k % 2][:], t_ps[:], ACT.Copy).then_inc(xh_done, 1)

                def gelu(i, k, q):
                    for half in range(2):
                        act.wait_ge(h_full, q * 2 + half + 1)
                        after(act, hl_done, (q - 1) * 2 + half + 1)
                        a.activation(hid[half][:], h_ps[half][:], ACT.Gelu)
                        a.activation(hid_hi[k % 2][:, half * HC:(half + 1) * HC, :], h_ps[half][:], ACT.Gelu).then_inc(gelu_done, 1)

                def copy_y(i, k, q):
                    act.wait_ge(yt_full, q + 1)
                    a.activation(y_t[k % 2][:], yt_ps[:], ACT.Copy).then_inc(yt_read, 1)

                def weigh(i, k, q):
                    act.wait_ge(y_full, q + 1)
                    act.wait_ge(cols_done, q * 2 + 2)
                    for u in range(U):
                        y = a.activation(y_hi[k % 2][:, u, :], y_ps[:, u, :], ACT.Copy, scale=wgt_c[k % 2][:, u:u + 1])
                    y.then_inc(yh_done, 1)

                def slot(i, k):
                    run(i, k, (0, split_x), (1, gelu), (2, copy_y), (3, weigh))
                    turn = turn_at(i, k, SUMS_AT)
                    if turn is not None:
                        act.wait_ge(returned, turn * S + S)
                        for u in range(U):
                            a.activation(acc_sb[u][:], acc[u][:], ACT.Copy).then_inc(acc_read, 1)

                slots(act, slot)

            @block.vector
            def _(dve):
                v = nc.vector

                def split_x(i, k, q):
                    dve.wait_ge(xh_done, q + 1)
                    v.tensor_tensor(x_lo[k % 2][:], t_ps[:], whole(x_hi[k % 2][:]), ALU.subtract).then_inc(xl_done, 1)

                def split_hid(i, k, q):
                    for half in range(2):
                        chunks = slice(half * HC, (half + 1) * HC)
                        dve.wait_ge(gelu_done, q * 2 + half + 1)
                        v.tensor_tensor(hid_lo[k % 2][:, chunks, :], hid[half][:], whole(hid_hi[k % 2][:, chunks, :]),
                                        ALU.subtract).then_inc(hl_done, 1)

                def columns(i, k, q):
                    for src, dst in ((local, loc_c), (weight, wgt_c)):
                        of_turn = src[:, bass.ds(i * U * E, U * E)].rearrange("p (u e) -> p e u", u=U)
                        v.tensor_copy(dst[k % 2][:], of_turn[:, k]).then_inc(cols_done, 1)

                def weigh(i, k, q):
                    dve.wait_ge(yh_done, q + 1)
                    for u in range(U):
                        y = v.scalar_tensor_tensor(out=y_lo[k % 2][:, u, :], in0=y_ps[:, u, :], scalar=wgt_c[k % 2][:, u:u + 1],
                                                   in1=whole(y_hi[k % 2][:, u, :]), op0=ALU.mult, op1=ALU.subtract)
                    y.then_inc(yl_done, 1)

                def one_hot(i, k, q):
                    dve.wait_ge(cols_done, q * 2 + 1)
                    for u in range(U):
                        one = v.tensor_scalar(hot[k % 2][:, u, :], h["iota"][:], loc_c[k % 2][:, u:u + 1], None, ALU.is_equal)
                    one.then_inc(hot_done, 1)

                def slot(i, k):
                    run(i, k, (3, columns), (0, split_x), (1, split_hid), (3, weigh), (3, one_hot))
                    for u in range(U):
                        turn = turn_at(i, k, TURN_AT[u])
                        if turn is not None:
                            dve.wait_ge(o_full, turn * U + u + 1)
                            x = xres[:, turn * U + u, :]
                            v.tensor_tensor(x, o_ps[:], x, ALU.add).then_inc(x_added, 1)

                slots(dve, slot)

            @block.sync
            def _(sp):
                if out is not None:
                    with sp.Fori(0, NB) as n:
                        sp.wait_ge(x_added, n + 1)
                        sp.dma_start(out[n].rearrange("(c p) d -> p c d", p=P), xres[:, n, :].rearrange("p (c d) -> p c d", c=C)).then_inc(stored, 16)
                    sp.wait_ge(stored, 16 * NB)


def scan_layer(nc, sem, h, xres, xn_dram, probs):
    with ExitStack() as tmp:
        t = lambda n, s, d: tmp.enter_context(nc.sbuf_tensor(f"sc_{n}", s, d))
        s = lambda n: sem(f"sc_{n}")
        bank = lambda n: tmp.enter_context(nc.psum_tensor(f"sc_{n}_ps", [P, T], F32))
        norm1, norm2 = Norm(nc, "n1", t, s, h, xres), Norm(nc, "n2", t, s, h, xres)
        xhat_t = [t(f"xhat_t{b}", [P, T], F32) for b in range(W)]
        xhat2_t = [t(f"xhat2_t{b}", [P, T], F32) for b in range(W)]
        ts = [t(f"ts{b}", [P, T], F32) for b in range(W)]
        fg = [t(f"fg{b}", [P, T], F32) for b in range(W)]
        lam = [t(f"lam{b}", [P, T], F32) for b in range(W)]
        xt_ps, tf_ps, y_ps = [[bank(f"{n}{b}") for b in range(W)] for n in ("xt", "tf", "y")]
        gate = Gate(nc, t, s, h, probs, bank("gate"))
        xt_full, xt_read, tf_full, tf_read, u_full, lam_full, lam_done = (
            s("xt_full"), s("xt_read"), s("tf_full"), s("tf_read"), s("u_full"), s("lam_full"), s("lam_done"))
        scanned, y_full, x_added, xt2_full, xt2_read, pe_turn = (
            s("scanned"), s("y_full"), s("x_added"), s("xt2_full"), s("xt2_read"), s("pe_turn"))
        xn_out = [s(f"xn_out{b}") for b in range(W)]
        lo = slice(PR, P)
        with nc.Block() as block:

            @block.sync
            def _(sp):
                with sp.Fori(0, TURNS) as i:
                    for b in range(W):
                        sp.wait_ge(norm2.xhat_done, i * W + b + 1)
                        sp.dma_start(xn_dram[bass.ds((i * W + b) * T, T), :].rearrange("(c p) d -> p c d", p=P),
                                     norm2.xhat[b][:].rearrange("p (c d) -> p c d", c=C)).then_inc(xn_out[b], 16)
                for b in range(W):
                    sp.wait_ge(xn_out[b], 16 * TURNS)

            @block.tensor
            def _(pe):
                def turn(head, middle, tail):
                    if middle is not None:
                        for b in range(W):
                            pe.wait_ge(tf_read, middle * W + b + 1)
                            after(pe, x_added, (middle - 1) * W + b + 1)
                            pe.sem_inc(pe_turn, 1)
                            pe.matmul(tf_ps[b][lo, :], h["wlam"][lo, :], fg[b][lo, :], start=True, stop=True).then_inc(lam_full, 1)
                            pe.matmul(y_ps[b][lo, :], h["bmat"][:], ts[b][0:PR, :], start=True, stop=True).then_inc(u_full, 1)
                    if tail is not None:
                        for b in range(W):
                            pe.wait_ge(norm2.xhat_done, tail * W + b + 1)
                            transpose_chunks(pe, xt_ps[b], norm2.xhat[b], h["ident"]).then_inc(xt2_full, 1)
                    if middle is not None:
                        for b in range(W):
                            pe.wait_ge(scanned, middle * W + b + 1)
                            for c in range(C):
                                mm = pe.matmul(y_ps[b][:, c * P:(c + 1) * P], ts[b][:, c * P:(c + 1) * P], h["wcw"][:], start=True, stop=True)
                            mm.then_inc(y_full, 1)
                    if tail is not None:
                        pe.wait_ge(xt2_read, tail * W + W)
                    if head is not None:
                        for b in range(W):
                            pe.wait_ge(norm1.xhat_done, head * W + b + 1)
                            transpose_chunks(pe, xt_ps[b], norm1.xhat[b], h["ident"]).then_inc(xt_full, 1)
                        for b in range(W):
                            pe.wait_ge(xt_read, head * W + b + 1)
                            if middle is not None:
                                pe.wait_ge(lam_done, middle * W + b + 1)
                            pe.matmul(tf_ps[b][:], h["wtf"][:], xhat_t[b][:], start=True, stop=True).then_inc(tf_full, 1)
                    if tail is not None:
                        for b in range(W):
                            gate.tensor(pe, tail, b, xhat2_t[b])

                pipeline(pe, turn)

            @block.scalar
            def _(act):
                a = nc.scalar

                def turn(head, middle, tail):
                    if tail is not None and not is_first(tail):
                        gate.scalar(act, tail - 1)
                    if middle is not None:
                        for b in range(W):
                            act.wait_ge(lam_full, middle * W + b + 1)
                            a.activation(lam[b][lo, :], tf_ps[b][lo, :], ACT.Sigmoid).then_inc(lam_done, 1)
                    if tail is not None:
                        for b in range(W):
                            act.wait_ge(xt2_full, tail * W + b + 1)
                            a.activation(xhat2_t[b][:], xt_ps[b][:], ACT.Copy).then_inc(xt2_read, 1)
                    if head is not None:
                        for b in range(W):
                            act.wait_ge(xt_full, head * W + b + 1)
                            a.activation(xhat_t[b][:], xt_ps[b][:], ACT.Copy).then_inc(xt_read, 1)
                        for b in range(W):
                            act.wait_ge(tf_full, head * W + b + 1)
                            a.activation(ts[b][0:PR, :], tf_ps[b][0:PR, :], ACT.Copy)
                            a.activation(fg[b][lo, :], tf_ps[b][lo, :], ACT.Sigmoid).then_inc(tf_read, 1)

                pipeline(act, turn)
                gate.scalar(act, TURNS - 1)

            @block.gpsimd
            def _(pool):
                def turn(head, middle, tail):
                    if tail is not None:
                        norm2.gpsimd(pool, tail)
                    if head is not None:
                        norm1.gpsimd(pool, head)

                pipeline(pool, turn)

            @block.vector
            def _(dve):
                v = nc.vector

                def turn(head, middle, tail):
                    if tail is not None:
                        dve.wait_ge(x_added, tail * W + W)
                        norm2.moments(dve, tail)
                        if not is_first(tail):
                            gate.less_max(dve, tail - 1)
                    if head is not None:
                        norm1.moments(dve, head)
                    if tail is not None:
                        for b in range(W):
                            after(dve, xn_out[b], tail * 16)
                        norm2.apply(dve, tail)
                    if middle is not None:
                        for b in range(W):
                            dve.wait_ge(u_full, middle * W + b + 1)
                            dve.wait_ge(lam_done, middle * W + b + 1)
                            v.tensor_tensor_scan(ts[b][lo, :], lam[b][lo, :], y_ps[b][lo, :], 0.0, ALU.mult, ALU.add).then_inc(scanned, 1)
                    if tail is not None and not is_first(tail):
                        gate.normalise(dve, tail - 1)
                    if head is not None:
                        norm1.apply(dve, head)
                    if middle is not None:
                        for b in range(W):
                            dve.wait_ge(y_full, middle * W + b + 1)
                            v.tensor_tensor(xres[:, middle * W + b, :], y_ps[b][:], xres[:, middle * W + b, :], ALU.add).then_inc(x_added, 1)

                pipeline(dve, turn)
                gate.less_max(dve, TURNS - 1)
                gate.normalise(dve, TURNS - 1)


def program(nc, w, out):
    with ExitStack() as ctx:
        sb = lambda n, s, d: ctx.enter_context(nc.sbuf_tensor(n, s, d))
        sem = lambda n: ctx.enter_context(nc.semaphore(n))
        dram = lambda n, s, d: nc.dram_tensor(n, s, d, kind="Internal").ap()
        q_dram = dram("q_parts", [NB, PARTS * P, T], BF16)
        k_dram = dram("k_parts", [NB, PARTS * 96, T], BF16)
        xn_dram = dram("xn", [NB * T, D], F32)
        xres = sb("xres", [P, NB, T], F32)
        v_all = sb("v_all", [P, NB, C * 32], F32)
        probs = sb("probs", [P, C, NB * E], F32)
        x_in = [sem(f"x_in{i}") for i in range(TURNS)]
        h = load_constants(nc, w, sb, sem, xres, x_in)

        def layer(build, *args, **kw):
            sems = []

            def sem(n):
                sems.append(nc.alloc_semaphore(name=n))
                return sems[-1]

            build(nc, sem, h, xres, *args, **kw)
            nc.clear_and_free_semaphores(sems)
            nc.all_engine_barrier()

        layer(mlp_layer, "qkv", "m1", x_in=x_in, q_dram=q_dram, k_dram=k_dram, v_all=v_all)
        layer(attention, q_dram, k_dram, v_all)
        layer(mlp_layer, "gate", "m2", xn_dram=xn_dram, probs=probs)
        for n in ("w1_hi", "w1_lo", "w2_hi", "w2_lo"):
            h[n] = sb(n, [P, E, F], F32R)
        layer(experts_layer, xn_dram, probs, "e1", None, weights=(w["w1e"], w["w2e"]))
        layer(scan_layer, xn_dram, probs)
        layer(experts_layer, xn_dram, probs, "e2", out)


_OUTS = [((16, 512, 128), 'float32')]


def layouts(i):
    import numpy as np

    a = {k: np.ascontiguousarray(v) for k, v in i.items()}
    half = HD // 2
    wq = a["L0_attn_Wq"].reshape(D, NH, HD).transpose(0, 2, 1)
    wk = a["L0_attn_Wk"].reshape(D, NKV, HD).transpose(0, 2, 1)
    swap = np.r_[half:HD, 0:half]
    twice = lambda x: np.concatenate([x, x], 0)
    hm = lambda x: x.reshape(M, HT, 2).transpose(2, 0, 1).reshape(P, HT)
    w = {
        "x": a["L0_attn_x"],
        "win2": np.concatenate([a["L0_ffn_Win"]] * 2, 1), "bin2": twice(a["L0_ffn_bin_"])[:, None],
        "w1p": hm(a["L0_ffn_W1"]), "b1p": hm(a["L0_ffn_b1"]), "w2p": hm(a["L0_ffn_W2"]),
        "b2p": np.concatenate([a["L0_ffn_b2"], np.zeros(M, np.float32)])[:, None],
        "wout2": twice(a["L0_ffn_Wout"]), "bout": a["L0_ffn_bout"][None, :],
        "wq": wq.reshape(D, D), "wqs": wq[:, swap].reshape(D, D), "wk": wk.reshape(D, -1), "wks": wk[:, swap].reshape(D, -1),
        "wv": a["L0_attn_Wv"], "wo": a["L0_attn_Wo"],
        "gw": a["L1_ffn_gate_w"].T, "w1e": a["L1_ffn_w1"].transpose(1, 0, 2),
        "w2e": a["L1_ffn_w2"].reshape(E, FC, P, D).transpose(2, 0, 1, 3).reshape(P, E, FC * D),
        "wu": a["L1_attn_W_U"].reshape(D, M * 4), "wv4": a["L1_attn_W_V"].reshape(1, M * 4),
        "wtop": a["L1_attn_W_toP"], "wf": a["L1_attn_W_F"], "wlam": a["L1_attn_W_lam"], "bmat": a["L1_attn_B_mat"],
        "ct": a["L1_attn_C_mat"].T, "wfromp": a["L1_attn_W_fromP"],
    }
    f32 = np.float32
    freq = (f32(1.0) / np.power(f32(10000.0), np.arange(half, dtype=f32) / f32(half))).astype(f32)
    angle = np.arange(T, dtype=f32)[None, :] * freq[:, None]
    cos = np.cos(np.concatenate([angle, angle])).astype(f32)
    sin = np.sin(np.concatenate([angle, angle])).astype(f32)
    sin[:half] *= f32(-1)
    w["cosq"], w["sinq"] = np.repeat(cos, NH, 0), np.repeat(sin, NH, 0)
    w["cosk"], w["sink"] = (np.tile(np.repeat(x, NKV, 0), (W, 1)) for x in (cos, sin))
    at = np.arange(P)
    w["ident"] = np.eye(P, dtype=f32)
    w["pairsum"] = np.tile(np.eye(M, dtype=f32), (2, 2))
    w["mask"] = np.where(at[None, :] > at[:, None], f32(MASKED), f32(0))
    w["iota"] = np.broadcast_to(np.arange(T, dtype=f32), (P, T))
    w["rowbase"] = (at // E * T).astype(f32)[:, None]
    w["mhalf"] = np.full((P, W * C), -0.5, f32)
    w["maskf"] = w.pop("mask")
    for name, columns in (("pack", PACK), ("pack_late", PACK_LATE)):
        w[name] = np.concatenate([w.pop(n) for n, _ in columns], 1)
    return {k: np.ascontiguousarray(v) for k, v in w.items()}


def kernel(**inputs):
    import numpy as _np
    import concourse.bacc as _bacc
    from concourse import mybir as _mybir
    from concourse.bass_utils import run_bass_kernel_spmd as _run

    nc = _bacc.Bacc("TRN2", target_bir_lowering=False, num_devices=1)
    arrays, w = {}, {}
    for name, a in layouts(inputs).items():
        arrays[f"in_{name}_dram"] = a
        w[name] = nc.dram_tensor(f"in_{name}_dram", a.shape, _mybir.dt.from_np(a.dtype), kind="ExternalInput").ap()
    outs = [nc.dram_tensor(f"out_{i}_dram", s, _mybir.dt.from_np(_np.dtype(d)), kind="ExternalOutput").ap()
            for i, (s, d) in enumerate(_OUTS)]
    program(nc, w, outs[0])
    r = _run(nc, [arrays], core_ids=[0])
    return r.results[0]["out_0_dram"]
```
